# Optimizing a Trainium2 kernel written in Bass

```python
import numpy as np
import jax
import jax.numpy as jnp

def _softmax(x, axis=-1):
    return jax.nn.softmax(x, axis=axis)

def _gelu(x):
    return jax.nn.gelu(x, approximate=True)

def _silu(x):
    return jax.nn.silu(x)

def _sigmoid(x):
    return jax.nn.sigmoid(x)

def _layernorm(x, axis=-1, eps=1e-05):
    m = jnp.mean(x, axis=axis, keepdims=True)
    v = jnp.var(x, axis=axis, keepdims=True)
    return (x - m) / jnp.sqrt(v + eps)

def _scatter_add(tgt, idx, src, axis=0):
    return tgt.at[idx].add(src)

def _segment_sum(src, seg, n):
    return jax.ops.segment_sum(src, seg, n)
kernel_name = 'mk_adaln_d2_jaxref_r4_0698b3'

def setup_inputs(seed: int=0):
    np.random.seed(seed)
    _w = jnp.asarray

    def _L0_attn_setup():
        import jax, jax.numpy as jnp
        import numpy as np
        B_, L, D_MODEL = (2, 512, 256)
        EXPAND, D_INNER, D_STATE, DT_RANK, D_CONV = (2, 512, 16, 64, 4)
        DT_MIN, DT_MAX = (0.001, 0.1)
        key = jax.random.key(seed)
        ks = jax.random.split(key, 8)
        s = lambda fan: 1.0 / np.sqrt(fan)
        A0 = jnp.broadcast_to(jnp.arange(1, D_STATE + 1, dtype=jnp.float32), (D_INNER, D_STATE))
        return {'x': jax.random.normal(ks[0], (B_, L, D_MODEL), jnp.float32), 'W_in': jax.random.normal(ks[1], (D_MODEL, 2 * D_INNER), jnp.float32) * s(D_MODEL), 'conv_k': jax.random.normal(ks[2], (D_CONV, D_INNER // EXPAND, D_INNER), jnp.float32) * s(D_CONV * D_INNER // EXPAND), 'conv_b': jnp.zeros((D_INNER,), jnp.float32), 'W_x': jax.random.normal(ks[3], (D_INNER, DT_RANK + 2 * D_STATE), jnp.float32) * s(D_INNER), 'W_dt': jax.random.normal(ks[4], (DT_RANK, D_INNER), jnp.float32) * s(DT_RANK), 'b_dt': jnp.zeros((D_INNER,), jnp.float32), 'A_log': jnp.log(A0), 'D': jnp.ones((D_INNER,), jnp.float32), 'W_out': jax.random.normal(ks[5], (D_INNER, D_MODEL), jnp.float32) * s(D_INNER)}
    _L0_attn_in = _L0_attn_setup()

    def _L0_ffn_setup():
        import jax, jax.numpy as jnp
        import numpy as np
        E = 8
        K = 2
        CAP_RATIO = 1.05
        key = jax.random.key(seed)
        ks = jax.random.split(key, 4)
        B, S, D, H = (2, 512, 256, 1024)
        x = jax.random.normal(ks[0], (B, S, D), jnp.float32)
        Wg = jax.random.normal(ks[1], (E, D), jnp.float32) * 0.02
        W1 = jax.random.normal(ks[2], (E, D, H), jnp.float32) * 0.02
        b1 = jnp.zeros((E, H), jnp.float32)
        W2 = jax.random.normal(ks[3], (E, H, D), jnp.float32) * 0.02
        b2 = jnp.zeros((E, D), jnp.float32)
        return {'x': x, 'Wg': Wg, 'W1': W1, 'b1': b1, 'W2': W2, 'b2': b2}
    _L0_ffn_in = _L0_ffn_setup()
    _L0_c = _w((lambda *s: np.random.randn(*s).astype(np.float32) * 0.05)(8, 256))
    _L0_wmod = _w((lambda *s: np.random.randn(*s).astype(np.float32) * 0.05)(256, 6 * 256) * 256 ** (-0.5))

    def _L1_attn_setup():
        import jax, jax.numpy as jnp
        import numpy as np
        T, B, D, H = (2048, 4, 256, 16)
        key = jax.random.key(seed)
        k1, k2, k3 = jax.random.split(key, 3)
        s = 1.0 / np.sqrt(D).astype(np.float32)
        return {'query': jax.random.normal(k1, (T, B, D), jnp.float32), 'Wqkv': jax.random.normal(k2, (3 * D, D), jnp.float32) * s, 'bqkv': jnp.zeros((3 * D,), jnp.float32), 'Wout': jax.random.normal(k3, (D, D), jnp.float32) * s, 'bout': jnp.zeros((D,), jnp.float32)}
    _L1_attn_in = _L1_attn_setup()

    def _L1_ffn_setup():
        import jax, jax.numpy as jnp
        import numpy as np
        D = 256
        H = 1024
        E = 8
        TOPK = 2

        def _moe_forward(x, router_w, w1, b1, w2, b2):
            orig_shape = x.shape
            xf = x.reshape(-1, orig_shape[-1])
            logits = xf @ router_w
            probs = jax.nn.softmax(logits, axis=-1)
            top_p, top_i = jax.lax.top_k(probs, TOPK)
            top_p = top_p / jnp.sum(top_p, axis=-1, keepdims=True)
            onehot = jax.nn.one_hot(top_i, E, dtype=xf.dtype)
            combine = jnp.einsum('tk,tke->te', top_p, onehot)
            out = jnp.zeros_like(xf)
            for e in range(E):
                h = jax.nn.gelu(xf @ w1[e] + b1[e], approximate=False)
                y = h @ w2[e] + b2[e]
                out = out + combine[:, e:e + 1] * y
            return out.reshape(orig_shape)
        key = jax.random.key(seed)
        ks = jax.random.split(key, 6)
        x = jax.random.normal(ks[0], (8, 256, D), dtype=jnp.float32)
        router_w = jax.random.normal(ks[1], (D, E), dtype=jnp.float32) * (1.0 / np.sqrt(D))
        w1 = jax.random.normal(ks[2], (E, D, H), dtype=jnp.float32) * (1.0 / np.sqrt(D))
        b1 = jnp.zeros((E, H), dtype=jnp.float32)
        w2 = jax.random.normal(ks[3], (E, H, D), dtype=jnp.float32) * (1.0 / np.sqrt(H))
        b2 = jnp.zeros((E, D), dtype=jnp.float32)
        return {'x': x, 'router_w': router_w, 'w1': w1, 'b1': b1, 'w2': w2, 'b2': b2}
    _L1_ffn_in = _L1_ffn_setup()
    _L1_c = _w((lambda *s: np.random.randn(*s).astype(np.float32) * 0.05)(8, 256))
    _L1_wmod = _w((lambda *s: np.random.randn(*s).astype(np.float32) * 0.05)(256, 6 * 256) * 256 ** (-0.5))
    _d = {'L0_attn_x': _L0_attn_in['x'], 'L0_attn_W_in': _L0_attn_in['W_in'], 'L0_attn_conv_k': _L0_attn_in['conv_k'], 'L0_attn_conv_b': _L0_attn_in['conv_b'], 'L0_attn_W_x': _L0_attn_in['W_x'], 'L0_attn_W_dt': _L0_attn_in['W_dt'], 'L0_attn_b_dt': _L0_attn_in['b_dt'], 'L0_attn_A_log': _L0_attn_in['A_log'], 'L0_attn_D': _L0_attn_in['D'], 'L0_attn_W_out': _L0_attn_in['W_out'], 'L0_ffn_Wg': _L0_ffn_in['Wg'], 'L0_ffn_W1': _L0_ffn_in['W1'], 'L0_ffn_b1': _L0_ffn_in['b1'], 'L0_ffn_W2': _L0_ffn_in['W2'], 'L0_ffn_b2': _L0_ffn_in['b2'], 'L0_c': _L0_c, 'L0_wmod': _L0_wmod, 'L1_attn_Wqkv': _L1_attn_in['Wqkv'], 'L1_attn_bqkv': _L1_attn_in['bqkv'], 'L1_attn_Wout': _L1_attn_in['Wout'], 'L1_attn_bout': _L1_attn_in['bout'], 'L1_ffn_router_w': _L1_ffn_in['router_w'], 'L1_ffn_w1': _L1_ffn_in['w1'], 'L1_ffn_b1': _L1_ffn_in['b1'], 'L1_ffn_w2': _L1_ffn_in['w2'], 'L1_ffn_b2': _L1_ffn_in['b2'], 'L1_c': _L1_c, 'L1_wmod': _L1_wmod}
    _x0 = _d['L0_attn_x']
    _d['L0_attn_x'] = jax.random.normal(jax.random.fold_in(jax.random.key(seed), 1), (8, 512, 256), dtype=_x0.dtype)
    del _x0
    return _d

def reference(L0_attn_x, L0_attn_W_in, L0_attn_conv_k, L0_attn_conv_b, L0_attn_W_x, L0_attn_W_dt, L0_attn_b_dt, L0_attn_A_log, L0_attn_D, L0_attn_W_out, L0_ffn_Wg, L0_ffn_W1, L0_ffn_b1, L0_ffn_W2, L0_ffn_b2, L0_c, L0_wmod, L1_attn_Wqkv, L1_attn_bqkv, L1_attn_Wout, L1_attn_bout, L1_ffn_router_w, L1_ffn_w1, L1_ffn_b1, L1_ffn_w2, L1_ffn_b2, L1_c, L1_wmod):

    def _L0_attn_ref(x, W_in, conv_k, conv_b, W_x, W_dt, b_dt, A_log, D, W_out):
        import jax, jax.numpy as jnp
        import numpy as np
        B_, L, D_MODEL = (2, 512, 256)
        EXPAND, D_INNER, D_STATE, DT_RANK, D_CONV = (2, 512, 16, 64, 4)
        DT_MIN, DT_MAX = (0.001, 0.1)
        xz = x @ W_in
        xs, res = jnp.split(xz, 2, axis=-1)
        xc = jax.lax.conv_general_dilated(xs, conv_k, window_strides=(1,), padding=[(D_CONV - 1, 0)], dimension_numbers=('NWC', 'WIO', 'NWC'), feature_group_count=EXPAND) + conv_b
        u = jax.nn.silu(xc)
        dbc = u @ W_x
        dt_raw = dbc[..., :DT_RANK]
        Bm = dbc[..., DT_RANK:DT_RANK + D_STATE]
        Cm = dbc[..., DT_RANK + D_STATE:]
        delta = jax.nn.softplus(dt_raw @ W_dt + b_dt)
        delta = jnp.clip(delta, DT_MIN, DT_MAX)
        A = -jnp.exp(A_log)
        dA = jnp.exp(delta[..., None] * A)
        dBu = delta[..., None] * u[..., None] * Bm[:, :, None, :]

        def step(h, inp):
            dA_t, dBu_t, C_t = inp
            h = dA_t * h + dBu_t
            y_t = jnp.einsum('bdn,bn->bd', h, C_t)
            return (h, y_t)
        h0 = jnp.zeros((x.shape[0], D_INNER, D_STATE), dA.dtype)
        _, y = jax.lax.scan(step, h0, (dA.transpose(1, 0, 2, 3), dBu.transpose(1, 0, 2, 3), Cm.transpose(1, 0, 2)))
        y = y.transpose(1, 0, 2) + u * D
        out = y * jax.nn.silu(res) @ W_out
        return out

    def _L0_ffn_ref(x, Wg, W1, b1, W2, b2):
        import jax, jax.numpy as jnp
        import numpy as np
        E = 8
        K = 2
        CAP_RATIO = 1.05
        B, S, D = x.shape
        T = B * S
        xf = x.reshape(T, D)
        gates = jax.nn.softmax(xf @ Wg.T, axis=-1)
        topw, topi = jax.lax.top_k(gates, K)
        C = int(round(K * T * CAP_RATIO / E))
        e_ord = topi.T.reshape(-1)
        tok_ord = jnp.tile(jnp.arange(T), K)
        oh = jax.nn.one_hot(e_ord, E, dtype=jnp.int32)
        cnt = jnp.take_along_axis(jnp.cumsum(oh, 0) - oh, e_ord[:, None], 1)[:, 0]
        within = cnt < C
        pos = jnp.where(within, cnt, C)
        x_disp = xf[tok_ord]
        buf = jnp.zeros((E, C + 1, D), xf.dtype).at[e_ord, pos].add(x_disp)[:, :C]
        h = jax.nn.gelu(jnp.einsum('ecd,edh->ech', buf, W1) + b1[:, None, :], approximate=False)
        y = jnp.einsum('ech,ehd->ecd', h, W2) + b2[:, None, :]
        y_ord = y[e_ord, jnp.minimum(pos, C - 1)] * within[:, None].astype(y.dtype)
        y_tk = y_ord.reshape(K, T, D).transpose(1, 0, 2)
        cw = topw * within.reshape(K, T).T.astype(topw.dtype)
        out = jnp.einsum('tk,tkd->td', cw, y_tk)
        return out.reshape(B, S, D)

    def _L1_attn_ref(query, Wqkv, bqkv, Wout, bout):
        import jax, jax.numpy as jnp
        import numpy as np
        T, B, D, H = (2048, 4, 256, 16)
        Tl, Bs, Dm = query.shape
        hd = Dm // H
        qkv = query @ Wqkv.T + bqkv
        q, k, v = jnp.split(qkv, 3, axis=-1)

        def heads(x):
            return x.reshape(Tl, Bs, H, hd).transpose(1, 2, 0, 3)
        qh, kh, vh = (heads(q), heads(k), heads(v))
        X = jnp.swapaxes(qh, -1, -2)
        Y = jnp.swapaxes(kh, -1, -2)
        Xc = X - X.mean(-1, keepdims=True)
        Yc = Y - Y.mean(-1, keepdims=True)
        c = jnp.einsum('bhiT,bhjT->bhij', Xc, Yc)
        sx = (Xc * Xc).sum(-1, keepdims=True)
        sy = (Yc * Yc).sum(-1)[..., None, :]
        corr = jnp.clip(c / jnp.sqrt(sx * sy), 0.0, 1.0)
        corr = jax.nn.softmax(corr, axis=-2)
        attn = jnp.einsum('bhtd,bhde->bhte', vh, corr)
        out = attn.transpose(2, 0, 1, 3).reshape(Tl * Bs, Dm) @ Wout.T + bout
        return out.reshape(Tl, Bs, Dm)

    def _L1_ffn_ref(x, router_w, w1, b1, w2, b2):
        import jax, jax.numpy as jnp
        import numpy as np
        D = 256
        H = 1024
        E = 8
        TOPK = 2

        def _moe_forward(x, router_w, w1, b1, w2, b2):
            orig_shape = x.shape
            xf = x.reshape(-1, orig_shape[-1])
            logits = xf @ router_w
            probs = jax.nn.softmax(logits, axis=-1)
            top_p, top_i = jax.lax.top_k(probs, TOPK)
            top_p = top_p / jnp.sum(top_p, axis=-1, keepdims=True)
            onehot = jax.nn.one_hot(top_i, E, dtype=xf.dtype)
            combine = jnp.einsum('tk,tke->te', top_p, onehot)
            out = jnp.zeros_like(xf)
            for e in range(E):
                h = jax.nn.gelu(xf @ w1[e] + b1[e], approximate=False)
                y = h @ w2[e] + b2[e]
                out = out + combine[:, e:e + 1] * y
            return out.reshape(orig_shape)
        return _moe_forward(x, router_w, w1, b1, w2, b2)
    x = L0_attn_x
    mod = (_silu(L0_c) @ L0_wmod).reshape(L0_c.shape[0], 6, 1, -1)
    sa, ca, ga, sb, cb, gb = (mod[:, 0], mod[:, 1], mod[:, 2], mod[:, 3], mod[:, 4], mod[:, 5])
    ga = (2 * (ga >= 0) - 1) * jnp.maximum(jnp.abs(ga), 0.25)
    gb = (2 * (gb >= 0) - 1) * jnp.maximum(jnp.abs(gb), 0.25)
    h = _layernorm(x, axis=-1) * (1 + ca) + sa
    x = x + ga * _L0_attn_ref(h, L0_attn_W_in, L0_attn_conv_k, L0_attn_conv_b, L0_attn_W_x, L0_attn_W_dt, L0_attn_b_dt, L0_attn_A_log, L0_attn_D, L0_attn_W_out)
    h = _layernorm(x, axis=-1) * (1 + cb) + sb
    x = x + gb * _L0_ffn_ref(h, L0_ffn_Wg, L0_ffn_W1, L0_ffn_b1, L0_ffn_W2, L0_ffn_b2)
    mod = (_silu(L1_c) @ L1_wmod).reshape(L1_c.shape[0], 6, 1, -1)
    sa, ca, ga, sb, cb, gb = (mod[:, 0], mod[:, 1], mod[:, 2], mod[:, 3], mod[:, 4], mod[:, 5])
    ga = (2 * (ga >= 0) - 1) * jnp.maximum(jnp.abs(ga), 0.25)
    gb = (2 * (gb >= 0) - 1) * jnp.maximum(jnp.abs(gb), 0.25)
    h = _layernorm(x, axis=-1) * (1 + ca) + sa
    x = x + ga * _L1_attn_ref(h, L1_attn_Wqkv, L1_attn_bqkv, L1_attn_Wout, L1_attn_bout)
    h = _layernorm(x, axis=-1) * (1 + cb) + sb
    x = x + gb * _L1_ffn_ref(h, L1_ffn_router_w, L1_ffn_w1, L1_ffn_b1, L1_ffn_w2, L1_ffn_b2)
    return x

_drawn_inputs = setup_inputs


def setup_inputs(seed=0):
    import zlib

    import numpy as np

    out = dict(_drawn_inputs(seed))
    spreads = {'L0_attn_conv_b': (0.0, 0.541),
     'L0_attn_b_dt': (0.0, 0.8),
     'L0_attn_D': (1.0, 0.6),
     'L0_ffn_b1': (0.0, 0.8),
     'L0_ffn_b2': (0.0, 0.794),
     'L1_attn_bqkv': (0.0, 0.8),
     'L1_attn_bout': (0.0, 0.269),
     'L1_ffn_b1': (0.0, 0.636),
     'L1_ffn_b2': (0.0, 0.433)}
    factors = {'L0_attn_W_dt': 8.0,
     'L0_attn_A_log': 4.351,
     'L0_ffn_Wg': 4.942,
     'L0_ffn_W1': 5.902,
     'L0_ffn_W2': 5.549}
    for name, (base, spread) in spreads.items():
        noise = np.random.default_rng([zlib.crc32(name.encode()), seed]).standard_normal(out[name].shape)
        drawn = base * np.exp(spread * noise) if base else spread * noise
        out[name] = jnp.asarray(drawn.astype(out[name].dtype))
    for name, factor in factors.items():
        out[name] = (out[name] * factor).astype(out[name].dtype)
    return out
```

```python
from contextlib import ExitStack

import concourse.bass as bass
from concourse import mybir

F32 = mybir.dt.float32
I32 = mybir.dt.int32
ALU = mybir.AluOpType
ACT = mybir.ActivationFunctionType
AX = mybir.AxisListType
P = 128

B, L, D = 8, 512, 256
T = B * L
NT = T // P
JT = L // P
DI, NS, DR, TAPS = 512, 16, 64, 4
MD = DI // P
KD = D // P
DT_MIN, DT_MAX = 0.001, 0.1
EPS = 1e-5
E, K = 8, 2
H = 1024
MH = H // P
CAP = int(round(K * T * 1.05 / E))
TS = 256
NTILES = (K * T + E * (TS - 1)) // TS
SLOTS = NTILES * TS
MAXT = (T + TS - 1) // TS
HEADS, HD = 16, 16
TQ, SQ = 8, 512
UNITS = 2 * NS


class Signal:

    def __init__(self, sem, per):
        self.sem, self.per = sem, per

    def at(self, r, k=None):
        return r * self.per + (self.per if k is None else k)


class Room:

    def __init__(self, nc, ctx, tag, keep):
        self.nc, self.ctx, self.tag, self.taken = nc, ctx, tag, keep["taken"]

    def sb(self, name, shape, dt=F32):
        return self.ctx.enter_context(self.nc.sbuf_tensor(f"{self.tag}_{name}", shape, dt))

    def ps(self, name, shape):
        return self.ctx.enter_context(self.nc.psum_tensor(f"{self.tag}_{name}", shape, F32))

    def sig(self, name, per=1):
        sem = self.nc.alloc_semaphore(name=f"{self.tag}_{name}")
        self.taken.append(sem)
        return Signal(sem, per)


def moments(nc, dve, r, mom, stats, n, sig):
    even, odd = stats[:, 0:n, 1], stats[:, 0:n, 4]
    nc.vector.tensor_tensor(mom[:, 0, 0:n], even, odd, ALU.add).then_inc(sig.sem, 1)
    nc.vector.tensor_tensor(mom[:, 1, 0:n], even, odd, ALU.subtract).then_inc(sig.sem, 1)
    nc.vector.tensor_tensor(mom[:, 2, 0:n], stats[:, 0:n, 2], stats[:, 0:n, 5], ALU.add).then_inc(sig.sem, 1)
    dve.wait_ge(sig.sem, r + 3)
    nc.vector.tensor_scalar(mom[:, 0, 0:n], mom[:, 0, 0:n], 0.5, None, ALU.mult).then_inc(sig.sem, 1)
    nc.vector.tensor_tensor(mom[:, 1, 0:n], mom[:, 1, 0:n], mom[:, 1, 0:n], ALU.mult).then_inc(sig.sem, 1)
    dve.wait_ge(sig.sem, r + 5)
    nc.vector.scalar_tensor_tensor(mom[:, 2, 0:n], mom[:, 1, 0:n], D / 4.0, mom[:, 2, 0:n], ALU.mult, ALU.add).then_inc(sig.sem, 1)


def setup(nc, io, keep):
    with ExitStack() as ctx:
        r = Room(nc, ctx, "set", keep)
        cT = r.sb("cT", [P, 2, KD, B])
        sT = r.sb("sT", [P, 2, KD, B])
        wmod = r.sb("wmod", [P, 2, KD, 6 * D])
        row = r.sb("row", [B, 2, 6 * D])
        sgn = r.sb("sgn", [B, 2, 2, D])
        zero = r.sb("zero", [P, 3 * D])
        rowp = r.ps("rowp", [B, 3, 512])
        colp = r.ps("colp", [P, 2 * KD, B])
        c_in, w_in, consts = r.sig("c_in", 32), r.sig("w_in", 32), r.sig("consts", 48)
        silu_c, row_mm, row_cp, col_mm, col_cp = r.sig("silu_c"), r.sig("row_mm"), r.sig("row_cp"), r.sig("col_mm"), r.sig("col_cp")
        step, row_ok, row_out = r.sig("step"), r.sig("row_ok"), r.sig("row_out")
        zeroed, zero_out = r.sig("zeroed"), r.sig("zero_out")
        block = ctx.enter_context(nc.Block())
        zt = SLOTS // P // 3

        @block.sync
        def _(sp):
            for ly in range(2):
                sp.dma_start(cT[:, ly], io["cT"][ly]).then_inc(c_in.sem, 16)
                sp.dma_start(wmod[:, ly], io["wmod"][ly].rearrange("(k p) n -> p k n", p=P)).then_inc(w_in.sem, 16)
            sp.dma_start(keep["ident"][:, :], io["ident"]).then_inc(consts.sem, 16)
            sp.dma_start(keep["below"][:, :], io["below"]).then_inc(consts.sem, 16)
            sp.dma_start(keep["iota"][:, :], io["iota"]).then_inc(consts.sem, 16)
            sp.wait_ge(row_ok.sem, 2)
            for ly in range(2):
                sp.dma_start(io["modrow"][ly], row[:, ly, 2 * D:]).then_inc(row_out.sem, 16)
            sp.wait_ge(row_out.sem, 32)
            sp.wait_ge(consts.sem, 48)

        @block.gpsimd
        def _(pool):
            pool.memset(zero[:, :], 0.0).then_inc(zeroed.sem, 1)
            pool.memset(keep["ones"][:, :], 1.0).then_inc(zeroed.sem, 1)

        @block.scalar
        def _(act):
            act.wait_ge(c_in.sem, 32)
            nc.scalar.activation(sT[:, :, :, :], cT[:, :, :, :], ACT.Silu).then_inc(silu_c.sem, 1)
            act.wait_ge(zeroed.sem, 2)
            for ly in range(2):
                v = io[f"xbuf{ly}"][0:SLOTS, :].rearrange("(a p c) d -> a p (c d)", p=P, c=3)
                with act.Fori(0, zt) as i:
                    act.dma_start(v[bass.ds(i, 1)].rearrange("a p f -> (a p) f"), zero[:, :]).then_inc(zero_out.sem, 16)
            act.wait_ge(zero_out.sem, 2 * zt * 16)

        @block.tensor
        def _(pe):
            pe.wait_ge(silu_c.sem, 1)
            pe.wait_ge(w_in.sem, 32)
            for ly in range(2):
                if ly:
                    pe.wait_ge(row_cp.sem, ly)
                for n in range(3):
                    for k in range(KD):
                        mm = nc.tensor.matmul(rowp[:, n, :], sT[:, ly, k, :], wmod[:, ly, k, n * 512:(n + 1) * 512],
                                              start=(k == 0), stop=(k == KD - 1))
                mm.then_inc(row_mm.sem, 1)
                if ly:
                    pe.wait_ge(col_cp.sem, ly)
                for c in range(2 * KD):
                    for k in range(KD):
                        mm = nc.tensor.matmul(colp[:, c, :], wmod[:, ly, k, c * P:(c + 1) * P], sT[:, ly, k, :],
                                              start=(k == 0), stop=(k == KD - 1))
                mm.then_inc(col_mm.sem, 1)

        @block.vector
        def _(dve):
            n = 0
            for ly in range(2):
                dve.wait_ge(row_mm.sem, ly + 1)
                nc.vector.tensor_copy(row[:, ly, :].rearrange("b (n c) -> b n c", n=3), rowp[:, :, :]).then_inc(row_cp.sem, 1)
                dve.wait_ge(row_cp.sem, ly + 1)
                m = row[:, ly, :].rearrange("b (m d) -> b m d", m=6)
                gate = m[:, 2:6:3, :]
                nc.vector.tensor_scalar(sgn[:, ly], gate, 0.0, 2.0, ALU.is_ge, ALU.mult).then_inc(step.sem, 1)
                n += 1
                dve.wait_ge(step.sem, n)
                nc.vector.tensor_scalar(sgn[:, ly], sgn[:, ly], 1.0, None, ALU.subtract).then_inc(step.sem, 1)
                n += 1
                dve.wait_ge(step.sem, n)
                nc.vector.tensor_tensor(gate, gate, sgn[:, ly], ALU.mult).then_inc(step.sem, 1)
                n += 1
                dve.wait_ge(step.sem, n)
                nc.vector.scalar_tensor_tensor(gate, gate, 0.25, sgn[:, ly], ALU.max, ALU.mult).then_inc(step.sem, 1)
                n += 1
                dve.wait_ge(step.sem, n)
                nc.vector.tensor_scalar(m[:, 4, :], m[:, 4, :], 1.0, None, ALU.add).then_inc(row_ok.sem, 1)
                dve.wait_ge(col_mm.sem, ly + 1)
                nc.vector.tensor_copy(keep["modT"][:, ly, 0:KD, :], colp[:, 0:KD, :]).then_inc(step.sem, 1)
                n += 1
                nc.vector.tensor_scalar(keep["modT"][:, ly, KD:, :], colp[:, KD:, :], 1.0, None, ALU.add).then_inc(col_cp.sem, 1)


def mamba(nc, io, keep):
    with ExitStack() as ctx:
        r = Room(nc, ctx, "mam", keep)
        ident = keep["ident"]
        w_in = r.sb("w_in", [P, KD, 2 * DI])
        w_conv = r.sb("w_conv", [P, TAPS, 2, DI])
        w_x = r.sb("w_x", [P, MD, DR + 2 * NS])
        w_dt = r.sb("w_dt", [DR, DI])
        w_out = r.sb("w_out", [P, MD, D])
        w_gate = r.sb("w_gate", [P, KD, E])
        vecs = r.sb("vecs", [P, 3, MD])
        a_neg = r.sb("a_neg", [P, MD, NS])
        eps = r.sb("eps", [P, 1])
        x = r.sb("x", [P, JT, D])
        st = r.sb("st", [P, JT, 6])
        mom = r.sb("mom", [P, 3, JT])
        rstd = r.sb("rstd", [P, JT])
        hT = r.sb("hT", [P, KD, L])
        xs = r.sb("xs", [P, MD, TAPS - 1 + L])
        raw = r.sb("raw", [P, 2 * MD, L])
        su = [r.sb(f"su{i}", [P, 2 * MD, L]) for i in range(2)]
        dtT = r.sb("dtT", [DR, L])
        bcT = r.sb("bcT", [2 * NS, L])
        delta = [r.sb(f"delta{i}", [P, MD, L]) for i in range(2)]
        du = [r.sb(f"du{i}", [P, MD, L]) for i in range(2)]
        bc = [r.sb(f"bc{i}", [P, 2, 2, L]) for i in range(2)]
        dA = [r.sb(f"dA{i}", [P, 2, L]) for i in range(4)]
        w = [r.sb(f"w{i}", [P, 2, L]) for i in range(4)]
        xres = r.sb("xres", [P, JT, D])
        rep = r.sb("rep", [P, 4, D])
        x1 = r.sb("x1", [P, JT, D])
        h2 = r.sb("h2", [P, JT, D])
        st2 = r.sb("st2", [P, JT, 6])
        mom2 = r.sb("mom2", [P, 3, JT])
        rstd2 = r.sb("rstd2", [P, JT])
        hT2 = r.sb("hT2", [P, KD, L])
        yacc = r.ps("yacc", [P, MD, L])
        fb = [r.ps(f"fb{i}", [P, L]) for i in range(2)]
        tb = [r.ps(f"tb{i}", [P, L]) for i in range(2)]

        weights, ready = r.sig("weights"), r.sig("ready")
        x_in, ln_st, ln_mv, ln_rs, xn_ok = r.sig("x_in", 16), r.sig("ln_st", 4), r.sig("ln_mv", 6), r.sig("ln_rs", 2), r.sig("xn_ok", 4)
        FJ = 2 + 2 * MD + MD + 2 + MD
        FA = FJ - MD
        f_mm, f_act, f_dve = r.sig("f_mm", FJ), r.sig("f_act", FA), r.sig("f_dve", MD)
        silued, sp_exp, sp_ln, clipped, du_ok = r.sig("silued", 2), r.sig("sp_exp"), r.sig("sp_ln"), r.sig("clipped"), r.sig("du_ok")
        bc_out, bc_in = r.sig("bc_out", 16), [r.sig(f"bc_in{i}", 64) for i in range(2)]
        da_ok, bu_ok, h_ok, hc_ok, acc_ok = (r.sig(n, UNITS) for n in ("da_ok", "bu_ok", "h_ok", "hc_ok", "acc_ok"))
        yd_ok, z_ok = r.sig("yd_ok", MD), r.sig("z_ok")
        res_in, rep_in = r.sig("res_in", 16), r.sig("rep_in", 16)
        t_mm, o_ok, x1_ok = r.sig("t_mm", 5), r.sig("o_ok", 2), r.sig("x1_ok")
        st2_ok, mv2_ok, rs2_ok, xn2_ok, sc2_ok, h2_ok = r.sig("st2_ok", 4), r.sig("mv2_ok", 6), r.sig("rs2_ok", 2), r.sig("xn2_ok", 4), r.sig("sc2_ok"), r.sig("h2_ok")
        hT2_ok, lg_ok = r.sig("hT2_ok", 2), r.sig("lg_ok")
        x1_out, h2_out = r.sig("x1_out", 16), r.sig("h2_out", 16)
        block = ctx.enter_context(nc.Block())
        x_dram = io["x"].rearrange("b (j p) d -> b p j d", p=P)
        x1_dram = io["x1"].rearrange("(b j p) d -> b p j d", b=B, p=P)
        h_dram = io["h0"].rearrange("(b j p) d -> b p j d", b=B, p=P)

        def one(ap, b):
            return ap[b] if isinstance(b, int) else ap[bass.ds(b, 1)].rearrange("o p j d -> (o p) j d")

        def periods(eng, body):
            body(0, None, None, 0)
            body(1, 0, None, 1)
            body(2, 1, 0, 0)
            body(3, 2, 1, 1)
            with eng.Fori(1, (B - 2) // 2) as i:
                body(i * 2 + 2, i * 2 + 1, i * 2, 0)
                body(i * 2 + 3, i * 2 + 2, i * 2 + 1, 1)
            body(None, B - 1, B - 2, 0)
            body(None, None, B - 1, 1)

        def before(b, n=1):
            return not isinstance(b, int) or b >= n

        @block.sync
        def _(sp):
            for dst, src in ((w_in[:, :, :], io["W_in"].rearrange("(k p) n -> p k n", p=P)),
                             (w_conv[:, :, :, :].rearrange("p t k n -> p (t k) n"),
                              io["conv_k"].rearrange("t (k p) n -> p (t k) n", p=P)),
                             (w_x[:, :, :], io["W_x"].rearrange("(k p) n -> p k n", p=P)),
                             (w_dt[:, :], io["W_dt"]),
                             (w_out[:, :, :], io["W_out"].rearrange("(k p) n -> p k n", p=P)),
                             (w_gate[:, :, :], io["gate0"]),
                             (vecs[:, :, :], io["vecs"]),
                             (a_neg[:, :, :], io["A_log"].rearrange("(m p) n -> p m n", p=P))):
                sp.dma_start(dst, src).then_inc(weights.sem, 16)

            def body(fr, sc, tl, par):
                if fr is not None:
                    if before(fr):
                        sp.wait_ge(f_mm.sem, f_mm.at(fr - 1, 2))
                    sp.dma_start(x[:, :, :], one(x_dram, fr)).then_inc(x_in.sem, 16)
                if tl is not None:
                    if before(tl):
                        sp.wait_ge(x1_ok.sem, x1_ok.at(tl - 1))
                        sp.wait_ge(h2_ok.sem, h2_ok.at(tl - 1))
                    sp.dma_start(xres[:, :, :], one(x_dram, tl)).then_inc(res_in.sem, 16)
                    src = io["modrow"][0, bass.ds(tl, 1)] if not isinstance(tl, int) else io["modrow"][0, tl:tl + 1]
                    sp.dma_start(rep[:, :, :], src.rearrange("o (m d) -> o m d", m=4).to_broadcast([P, 4, D])).then_inc(rep_in.sem, 16)
                for c in range(NS // 2):
                    if sc is not None:
                        if c >= 2 or before(sc):
                            sp.wait_ge(hc_ok.sem, hc_ok.at(sc, 4 * (c - 1)) if c >= 2 else hc_ok.at(sc - 1, UNITS - 4 + 4 * c))
                        if c == 0:
                            sp.wait_ge(bc_out.sem, bc_out.at(sc))
                        src = io["bc"][1 - par].rearrange("(g n) t -> n g t", g=2)[2 * c:2 * c + 2]
                        for n in range(2):
                            for g in range(2):
                                sp.dma_start(bc[c % 2][:, n, g], src[n, g:g + 1, :].to_broadcast([P, L])).then_inc(bc_in[c % 2].sem, 16)
                    if tl is not None and c == 3:
                        sp.wait_ge(x1_ok.sem, x1_ok.at(tl))
                        sp.dma_start(one(x1_dram, tl), x1[:, :, :]).then_inc(x1_out.sem, 16)
                    if tl is not None and c == 6:
                        sp.wait_ge(h2_ok.sem, h2_ok.at(tl))
                        sp.dma_start(one(h_dram, tl), h2[:, :, :]).then_inc(h2_out.sem, 16)
                if fr is not None:
                    if before(fr, 2):
                        sp.wait_ge(bc_in[0].sem, bc_in[0].at(fr - 2) * (NS // 4))
                        sp.wait_ge(bc_in[1].sem, bc_in[1].at(fr - 2) * (NS // 4))
                    sp.wait_ge(f_act.sem, f_act.at(fr))
                    sp.dma_start(io["bc"][par], bcT[:, :]).then_inc(bc_out.sem, 16)

            periods(sp, body)
            sp.wait_ge(x1_out.sem, 16 * B)
            sp.wait_ge(h2_out.sem, 16 * B)

        @block.scalar
        def _(act):
            act.wait_ge(weights.sem, 8 * 16)
            nc.scalar.activation(a_neg[:, :, :], a_neg[:, :, :], ACT.Exp).then_inc(ready.sem, 1)
            act.wait_ge(ready.sem, 5)

            def unit(b, q, par):
                n, m0 = q // 2, 2 * (q % 2)
                if q == 0:
                    act.wait_ge(clipped.sem, clipped.at(b))
                if q >= 4 or before(b):
                    act.wait_ge(h_ok.sem, h_ok.at(b, q - 3) if q >= 4 else h_ok.at(b - 1, UNITS + q - 3))
                for m in range(2):
                    ins = nc.scalar.activation(dA[q % 4][:, m, 1:], delta[par][:, m0 + m, 1:], ACT.Exp,
                                               scale=a_neg[:, m0 + m, n:n + 1])
                ins.then_inc(da_ok.sem, 1)

            def evac(b, job, out, func, **kw):
                act.wait_ge(f_mm.sem, f_mm.at(b, job + 1))
                nc.scalar.activation(out, kw.pop("src"), func, **kw).then_inc(f_act.sem, 1)

            def front(b, s, par):
                if s == 1:
                    act.wait_ge(ln_mv.sem, ln_mv.at(b))
                    nc.scalar.activation(rstd[:, :], mom[:, 2, :], ACT.Ln, bias=eps[:, 0:1], scale=1.0 / D).then_inc(ln_rs.sem, 1)
                    act.wait_ge(ln_rs.sem, ln_rs.at(b, 1))
                    nc.scalar.activation(rstd[:, :], rstd[:, :], ACT.Exp, scale=-0.5).then_inc(ln_rs.sem, 1)
                if s == 3:
                    for dh in range(KD):
                        act.wait_ge(f_mm.sem, f_mm.at(b, dh + 1))
                        if isinstance(b, int):
                            sc_, bi_ = keep["modT"][:, 0, KD + dh, b:b + 1], keep["modT"][:, 0, dh, b:b + 1]
                        else:
                            sc_, bi_ = keep["modT"][:, 0, KD + dh, bass.ds(b, 1)], keep["modT"][:, 0, dh, bass.ds(b, 1)]
                        nc.scalar.activation(hT[:, dh, :], fb[dh % 2][:, :], ACT.Identity, scale=sc_, bias=bi_).then_inc(f_act.sem, 1)
                if 4 <= s < 8:
                    for m in (2 * (s - 4), 2 * (s - 4) + 1):
                        out = xs[:, m, TAPS - 1:] if m < MD else raw[:, m - MD, :]
                        evac(b, 2 + m, out, ACT.Copy, src=fb[m % 2][:, :])
                if 8 <= s < 12:
                    m = s - 8
                    evac(b, 10 + m, raw[:, MD + m, :], ACT.Identity, src=fb[m % 2][:, :], bias=vecs[:, 0, m:m + 1])
                if s == 12:
                    if before(b, 2):
                        act.wait_ge(t_mm.sem, t_mm.at(b - 2, 2))
                    act.wait_ge(f_act.sem, f_act.at(b, 14))
                    for g in range(2):
                        nc.scalar.activation(su[par][:, MD * g:MD * g + MD, :], raw[:, MD * g:MD * g + MD, :], ACT.Silu).then_inc(silued.sem, 1)
                if s == 13:
                    evac(b, 14, dtT[:, :], ACT.Copy, src=fb[0][0:DR, :])
                    if before(b):
                        act.wait_ge(bc_out.sem, bc_out.at(b - 1))
                    evac(b, 15, bcT[:, :], ACT.Copy, src=fb[1][0:2 * NS, :])
                if s == 15:
                    act.wait_ge(f_dve.sem, f_dve.at(b))
                    nc.scalar.activation(delta[par][:, :, :], delta[par][:, :, :], ACT.Exp).then_inc(sp_exp.sem, 1)
                    act.wait_ge(sp_exp.sem, sp_exp.at(b))
                    nc.scalar.activation(delta[par][:, :, :], delta[par][:, :, :], ACT.Ln, bias=1.0).then_inc(sp_ln.sem, 1)

            def tail(b, s):
                if s == 3:
                    act.wait_ge(mv2_ok.sem, mv2_ok.at(b))
                    nc.scalar.activation(rstd2[:, :], mom2[:, 2, :], ACT.Ln, bias=eps[:, 0:1], scale=1.0 / D).then_inc(rs2_ok.sem, 1)
                    act.wait_ge(rs2_ok.sem, rs2_ok.at(b, 1))
                    nc.scalar.activation(rstd2[:, :], rstd2[:, :], ACT.Exp, scale=-0.5).then_inc(rs2_ok.sem, 1)
                if s == 6:
                    for dh in range(KD):
                        act.wait_ge(t_mm.sem, t_mm.at(b, 3 + dh))
                        nc.scalar.activation(hT2[:, dh, :], tb[dh % 2][:, :], ACT.Copy).then_inc(hT2_ok.sem, 1)

            def body(fr, sc, tl, par):
                for q in range(UNITS):
                    if sc is not None:
                        unit(sc, q, 1 - par)
                    if fr is not None and q % 2 == 0:
                        front(fr, q // 2, par)
                    if tl is not None and q % 4 == 1:
                        tail(tl, q // 4)

            periods(act, body)

        @block.vector
        def _(dve):
            for i in range(4):
                nc.vector.memset(dA[i][:, :, 0:1], 0.0)
            nc.vector.memset(xs[:, :, 0:TAPS - 1], 0.0).then_inc(ready.sem, 1)
            nc.vector.memset(eps[:, :], EPS).then_inc(ready.sem, 1)
            nc.vector.memset(rstd[:, :], 0.0).then_inc(ready.sem, 1)
            dve.wait_ge(ready.sem, 4)
            nc.vector.tensor_scalar(a_neg[:, :, :], a_neg[:, :, :], -1.0, None, ALU.mult).then_inc(ready.sem, 1)

            def unit(b, q, par):
                n, m0 = q // 2, 2 * (q % 2)
                if q == 0:
                    dve.wait_ge(du_ok.sem, du_ok.at(b))
                if q % 4 == 0:
                    dve.wait_ge(bc_in[(q // 4) % 2].sem, b * (64 * NS // 4) + 64 * (q // 8 + 1))
                if q >= 4 or before(b):
                    dve.wait_ge(acc_ok.sem, acc_ok.at(b, q - 3) if q >= 4 else acc_ok.at(b - 1, UNITS + q - 3))
                bn = bc[(q // 4) % 2][:, n % 2, 0:1, :].to_broadcast([P, 2, L])
                nc.vector.tensor_tensor(w[q % 4][:, :, :], du[par][:, m0:m0 + 2, :], bn, ALU.mult).then_inc(bu_ok.sem, 1)
                dve.wait_ge(bu_ok.sem, bu_ok.at(b, q + 1))
                dve.wait_ge(da_ok.sem, da_ok.at(b, q + 1))
                wf = w[q % 4][:, :, :].rearrange("p m t -> p (m t)")
                nc.vector.tensor_tensor_scan(wf, dA[q % 4][:, :, :].rearrange("p m t -> p (m t)"), wf, 0.0,
                                             ALU.mult, ALU.add).then_inc(h_ok.sem, 1)

            def last(b, par):
                dve.wait_ge(acc_ok.sem, acc_ok.at(b))
                for m in range(MD):
                    nc.vector.scalar_tensor_tensor(su[par][:, MD + m, :], su[par][:, MD + m, :], vecs[:, 2, m:m + 1],
                                                   yacc[:, m, :], ALU.mult, ALU.add).then_inc(yd_ok.sem, 1)
                dve.wait_ge(yd_ok.sem, yd_ok.at(b))
                nc.vector.tensor_tensor(su[par][:, MD:, :], su[par][:, MD:, :], su[par][:, 0:MD, :], ALU.mult).then_inc(z_ok.sem, 1)

            def norm(b, src, stats, mean, s_ok, m_ok):
                for j in range(JT):
                    nc.vector.bn_stats(stats[:, j, :], src[:, j, :]).then_inc(s_ok.sem, 1)
                dve.wait_ge(s_ok.sem, s_ok.at(b))
                moments(nc, dve, m_ok.at(b, 0), mean, stats, JT, m_ok)

            def front(b, s, par):
                if s == 0:
                    dve.wait_ge(x_in.sem, x_in.at(b))
                    norm(b, x, st, mom, ln_st, ln_mv)
                if s == 2:
                    dve.wait_ge(ln_rs.sem, ln_rs.at(b))
                    for j in range(JT):
                        nc.vector.tensor_scalar(x[:, j, :], x[:, j, :], mom[:, 0, j:j + 1], rstd[:, j:j + 1],
                                                ALU.subtract, ALU.mult).then_inc(xn_ok.sem, 1)
                if s == 14:
                    for m in range(MD):
                        dve.wait_ge(f_mm.sem, f_mm.at(b, FA + m + 1))
                        nc.vector.tensor_scalar(delta[par][:, m, :], fb[m % 2][:, :], vecs[:, 1, m:m + 1], 20.0,
                                                ALU.add, ALU.min).then_inc(f_dve.sem, 1)
                if s == 15:
                    dve.wait_ge(sp_ln.sem, sp_ln.at(b))
                    nc.vector.tensor_scalar(delta[par][:, :, :], delta[par][:, :, :], DT_MIN, DT_MAX,
                                            ALU.max, ALU.min).then_inc(clipped.sem, 1)
                    dve.wait_ge(clipped.sem, clipped.at(b))
                    nc.vector.tensor_tensor(du[par][:, :, :], delta[par][:, :, :], su[par][:, MD:, :], ALU.mult).then_inc(du_ok.sem, 1)

            def tail(b, s):
                if s == 1:
                    dve.wait_ge(rep_in.sem, rep_in.at(b))
                    dve.wait_ge(res_in.sem, res_in.at(b))
                    if before(b):
                        dve.wait_ge(x1_out.sem, x1_out.at(b - 1))
                    for g in range(2):
                        dve.wait_ge(t_mm.sem, t_mm.at(b, g + 1))
                        nc.vector.tensor_tensor(x1[:, 2 * g:2 * g + 2, :], tb[g][:, :].rearrange("p (j d) -> p j d", j=2),
                                                rep[:, 0:1, :].to_broadcast([P, 2, D]), ALU.mult).then_inc(o_ok.sem, 1)
                    dve.wait_ge(o_ok.sem, o_ok.at(b))
                    nc.vector.tensor_tensor(x1[:, :, :], x1[:, :, :], xres[:, :, :], ALU.add).then_inc(x1_ok.sem, 1)
                if s == 2:
                    dve.wait_ge(x1_ok.sem, x1_ok.at(b))
                    norm(b, x1, st2, mom2, st2_ok, mv2_ok)
                if s == 4:
                    dve.wait_ge(rs2_ok.sem, rs2_ok.at(b))
                    if before(b):
                        dve.wait_ge(h2_out.sem, h2_out.at(b - 1))
                    for j in range(JT):
                        nc.vector.tensor_scalar(h2[:, j, :], x1[:, j, :], mom2[:, 0, j:j + 1], rstd2[:, j:j + 1],
                                                ALU.subtract, ALU.mult).then_inc(xn2_ok.sem, 1)
                if s == 7:
                    dve.wait_ge(t_mm.sem, t_mm.at(b))
                    dst = keep["logits"][:, b * JT:(b + 1) * JT, :] if isinstance(b, int) else keep["logits"][:, bass.ds(b * JT, JT), :]
                    nc.vector.tensor_scalar(dst, tb[0][:, 0:JT * E].rearrange("p (j e) -> p j e", j=JT), 1.0, None,
                                            ALU.mult).then_inc(lg_ok.sem, 1)

            def body(fr, sc, tl, par):
                for q in range(UNITS):
                    if sc is not None:
                        unit(sc, q, 1 - par)
                    if fr is not None and q % 2 == 0:
                        front(fr, q // 2, par)
                    if tl is not None and q % 4 == 1:
                        tail(tl, q // 4)
                if sc is not None:
                    last(sc, 1 - par)

            periods(dve, body)

        @block.gpsimd
        def _(pool):
            def unit(b, q):
                n = q // 2
                if q % 4 == 0:
                    pool.wait_ge(bc_in[(q // 4) % 2].sem, b * (64 * NS // 4) + 64 * (q // 8 + 1))
                pool.wait_ge(h_ok.sem, h_ok.at(b, q + 1))
                cn = bc[(q // 4) % 2][:, n % 2, 1:2, :].to_broadcast([P, 2, L])
                nc.gpsimd.tensor_tensor(w[q % 4][:, :, :], w[q % 4][:, :, :], cn, ALU.mult).then_inc(hc_ok.sem, 1)

            def tail(b, s):
                if s == 5:
                    pool.wait_ge(xn2_ok.sem, xn2_ok.at(b))
                    nc.gpsimd.tensor_tensor(h2[:, :, :], h2[:, :, :], rep[:, 2:3, :].to_broadcast([P, JT, D]), ALU.mult).then_inc(sc2_ok.sem, 1)
                    pool.wait_ge(sc2_ok.sem, sc2_ok.at(b))
                    nc.gpsimd.tensor_tensor(h2[:, :, :], h2[:, :, :], rep[:, 1:2, :].to_broadcast([P, JT, D]), ALU.add).then_inc(h2_ok.sem, 1)

            def body(fr, sc, tl, par):
                for q in range(UNITS):
                    if sc is not None:
                        unit(sc, q)
                    if tl is not None and q % 4 == 1:
                        tail(tl, q // 4)

            periods(pool, body)

        @block.tensor
        def _(pe):
            pe.wait_ge(weights.sem, 8 * 16)
            pe.wait_ge(ready.sem, 5)

            def unit(b, q):
                m0 = 2 * (q % 2)
                if q == 0 and before(b):
                    pe.wait_ge(yd_ok.sem, yd_ok.at(b - 1))
                pe.wait_ge(hc_ok.sem, hc_ok.at(b, q + 1))
                for m in range(2):
                    mm = nc.tensor.matmul(yacc[:, m0 + m, :], ident[:, :], w[q % 4][:, m, :],
                                          start=(q < 2), stop=(q >= UNITS - 2))
                mm.then_inc(acc_ok.sem, 1)

            def free(b, job):
                if job < 2:
                    if before(b):
                        pe.wait_ge(f_dve.sem, f_dve.at(b - 1, MD - 1 + job))
                elif job < FA + 2:
                    pe.wait_ge(f_act.sem, f_act.at(b, job - 1))
                else:
                    pe.wait_ge(f_dve.sem, f_dve.at(b, job - FA - 1))

            def product(b, job, out, pairs):
                free(b, job)
                for i, (lhsT, rhs) in enumerate(pairs):
                    mm = nc.tensor.matmul(out, lhsT, rhs, start=(i == 0), stop=(i == len(pairs) - 1))
                mm.then_inc(f_mm.sem, 1)

            def front(b, s, par):
                if s == 3:
                    pe.wait_ge(xn_ok.sem, xn_ok.at(b))
                    for dh in range(KD):
                        free(b, dh)
                        for j in range(JT):
                            mm = nc.tensor.transpose(fb[dh][:, j * P:(j + 1) * P], x[:, j, dh * P:(dh + 1) * P], ident[:, :])
                        mm.then_inc(f_mm.sem, 1)
                if 4 <= s < 8:
                    if s == 4:
                        pe.wait_ge(f_act.sem, f_act.at(b, 2))
                    for m in (2 * (s - 4), 2 * (s - 4) + 1):
                        product(b, 2 + m, fb[m % 2][:, :], [(w_in[:, k, m * P:(m + 1) * P], hT[:, k, :]) for k in range(KD)])
                if 8 <= s < 12:
                    m = s - 8
                    g = m // 2
                    if s == 8:
                        pe.wait_ge(f_act.sem, f_act.at(b, 2 + MD))
                    product(b, 10 + m, fb[m % 2][:, :],
                            [(w_conv[:, tap, k, m * P:(m + 1) * P], xs[:, 2 * g + k, tap:tap + L])
                             for tap in range(TAPS) for k in range(2)])
                if s == 13:
                    pe.wait_ge(silued.sem, silued.at(b))
                    product(b, 14, fb[0][0:DR, :], [(w_x[:, k, 0:DR], su[par][:, MD + k, :]) for k in range(MD)])
                    product(b, 15, fb[1][0:2 * NS, :], [(w_x[:, k, DR:], su[par][:, MD + k, :]) for k in range(MD)])
                if s == 14:
                    pe.wait_ge(f_act.sem, f_act.at(b, 15))
                    for m in range(MD):
                        product(b, FA + m, fb[m % 2][:, :], [(w_dt[:, m * P:(m + 1) * P], dtT[:, :])])

            def tail(b, s, par):
                if s == 0:
                    pe.wait_ge(z_ok.sem, z_ok.at(b))
                    for g in range(2):
                        if g == 0 and before(b):
                            pe.wait_ge(lg_ok.sem, lg_ok.at(b - 1))
                        if g == 1 and before(b):
                            pe.wait_ge(hT2_ok.sem, hT2_ok.at(b - 1))
                        for j in (2 * g, 2 * g + 1):
                            for k in range(MD):
                                mm = nc.tensor.matmul(tb[g][:, (j % 2) * D:(j % 2 + 1) * D], su[par][:, MD + k, j * P:(j + 1) * P],
                                                      w_out[:, k, :], start=(k == 0), stop=(k == MD - 1))
                        mm.then_inc(t_mm.sem, 1)
                if s == 6:
                    pe.wait_ge(h2_ok.sem, h2_ok.at(b))
                    for dh in range(KD):
                        pe.wait_ge(o_ok.sem, o_ok.at(b, dh + 1))
                        for j in range(JT):
                            mm = nc.tensor.transpose(tb[dh][:, j * P:(j + 1) * P], h2[:, j, dh * P:(dh + 1) * P], ident[:, :])
                        mm.then_inc(t_mm.sem, 1)
                if s == 7:
                    pe.wait_ge(hT2_ok.sem, hT2_ok.at(b))
                    for j in range(JT):
                        for dh in range(KD):
                            mm = nc.tensor.matmul(tb[0][:, j * E:(j + 1) * E], hT2[:, dh, j * P:(j + 1) * P], w_gate[:, dh, :],
                                                  start=(dh == 0), stop=(dh == KD - 1))
                    mm.then_inc(t_mm.sem, 1)

            def body(fr, sc, tl, par):
                for q in range(UNITS):
                    if sc is not None:
                        unit(sc, q)
                    if fr is not None and q % 2 == 0:
                        front(fr, q // 2, par)
                    if tl is not None and q % 4 == 1:
                        tail(tl, q // 4, par)

            periods(pe, body)


def route(nc, io, keep, ly):
    with ExitStack() as ctx:
        r = Room(nc, ctx, f"rt{ly}", keep)
        lg, iota = keep["logits"], keep["iota"]
        rows = r.sb("rows", [P, NT, D])
        lg2 = r.sb("lg2", [P, NT, E])
        top = [r.sb(f"top{k}", [P, NT]) for k in range(K)]
        sc = r.sb("sc", [P, NT, E])
        best = r.sb("best", [P, NT])
        hot = r.sb("hot", [P, E, K, NT])
        ex = r.sb("ex", [P, NT, E])
        d2 = r.sb("d2", [P, NT])
        ssum = r.sb("ssum", [P, NT])
        seg = r.sb("seg", [P, E, K * NT])
        tot = r.sb("tot", [P, E, K * NT])
        inc = r.sb("inc", [P, E, K * NT])
        rank = r.sb("rank", [P, E, K * NT])
        cnt = r.sb("cnt", [P, E])
        cmp = r.sb("cmp", [P, E, MAXT])
        nt = r.sb("nt", [P, E])
        end = r.sb("end", [P, E])
        base = r.sb("base", [P, E])
        own = r.sb("own", [P, NTILES, E])
        ownf = r.sb("ownf", [P, NTILES])
        rk = r.sb("rk", [P, K * NT])
        slot = r.sb("slot", [P, K * NT])
        inside = r.sb("inside", [P, K * NT])
        put = r.sb("put", [P, K * NT])
        pre_p, tot_p = r.ps("pre_p", [P, E * K * NT]), r.ps("tot_p", [P, E * K * NT])
        step, hot_ok, counted, diff_ok, exp_ok, put_ok = (r.sig(n) for n in ("step", "hot_ok", "counted", "diff_ok", "exp_ok", "put_ok"))
        rows_in = [r.sig(f"rows_in{g}", 16) for g in range(4)]
        placed = r.sig("placed", 16)
        block = ctx.enter_context(nc.Block())
        grp = NT // 4

        @block.sync
        def _(sp):
            src = io[f"h{ly}"].rearrange("(j p) d -> p j d", p=P)
            for g in range(4):
                sp.dma_start(rows[:, g * grp:(g + 1) * grp, :], src[:, g * grp:(g + 1) * grp, :]).then_inc(rows_in[g].sem, 16)

        @block.gpsimd
        def _(pool):
            pool.wait_ge(put_ok.sem, 1)
            for j in range(NT):
                if j % grp == 0:
                    pool.wait_ge(rows_in[j // grp].sem, 16)
                for k in range(K):
                    c = k * NT + j
                    pool.indirect_dma_start(io[f"xbuf{ly}"], bass.IndirectOffsetOnAxis(ap=keep["put"][:, c:c + 1], axis=0),
                                            rows[:, j, :], None).then_inc(placed.sem, 16)
            pool.wait_ge(placed.sem, 16 * K * NT)

        @block.tensor
        def _(pe):
            pe.wait_ge(hot_ok.sem, K)
            hf = hot[:, :, :, :].rearrange("p e k j -> p (e k j)")
            nc.tensor.matmul(pre_p[:, :], keep["below"][:, :], hf, start=True, stop=True)
            nc.tensor.matmul(tot_p[:, :], keep["ones"][:, :], hf, start=True, stop=True).then_inc(counted.sem, 1)

        @block.scalar
        def _(act):
            act.wait_ge(diff_ok.sem, 2)
            nc.scalar.activation(ex[:, :, :], ex[:, :, :], ACT.Exp).then_inc(exp_ok.sem, 1)
            nc.scalar.activation(d2[:, :], d2[:, :], ACT.Exp).then_inc(exp_ok.sem, 1)

        @block.vector
        def _(dve):
            done = [0]

            def link(ins):
                done[0] += 1
                ins.then_inc(step.sem, 1)
                dve.wait_ge(step.sem, done[0])

            V = nc.vector

            def wide(ap, n=E):
                return ap.unsqueeze(2).to_broadcast([P, ap.shape[1], n])

            falling = iota[:, 0:E].unsqueeze(1).to_broadcast([P, NT, E])
            for k in range(K):
                cur = lg if k == 0 else lg2
                link(V.tensor_reduce(top[k][:, :], cur[:, :, :], AX.X, ALU.max))
                link(V.tensor_tensor(sc[:, :, :], cur[:, :, :], wide(top[k][:, :]), ALU.is_equal))
                link(V.tensor_tensor(sc[:, :, :], sc[:, :, :], falling, ALU.mult))
                link(V.tensor_reduce(best[:, :], sc[:, :, :], AX.X, ALU.max))
                link(V.tensor_tensor(sc[:, :, :], sc[:, :, :], wide(best[:, :]), ALU.is_equal))
                V.tensor_copy(hot[:, :, k, :], sc[:, :, :].rearrange("p j e -> p e j")).then_inc(hot_ok.sem, 1)
                if k == 0:
                    link(V.scalar_tensor_tensor(lg2[:, :, :], sc[:, :, :], -3e38, lg[:, :, :], ALU.mult, ALU.add))
            V.tensor_tensor(ex[:, :, :], lg[:, :, :], wide(top[0][:, :]), ALU.subtract).then_inc(diff_ok.sem, 1)
            V.tensor_tensor(d2[:, :], top[1][:, :], top[0][:, :], ALU.subtract).then_inc(diff_ok.sem, 1)
            link(V.memset(seg[:, :, :], 1.0))
            link(V.memset(seg[:, :, 0:1], 0.0))
            dve.wait_ge(exp_ok.sem, 2)
            link(V.tensor_reduce(ssum[:, :], ex[:, :, :], AX.X, ALU.add))
            w0, w1 = keep["wts"][:, 0:NT], keep["wts"][:, NT:]
            link(V.reciprocal(w0, ssum[:, :]))
            link(V.tensor_tensor(w1, d2[:, :], w0, ALU.mult))
            if ly == 1:
                link(V.tensor_tensor(ssum[:, :], w0, w1, ALU.add))
                link(V.reciprocal(ssum[:, :], ssum[:, :]))
                link(V.tensor_tensor(w0, w0, ssum[:, :], ALU.mult))
                link(V.tensor_tensor(w1, w1, ssum[:, :], ALU.mult))
            dve.wait_ge(counted.sem, 1)
            flat = "p e c -> p (e c)"
            link(V.tensor_copy(tot[:, :, :].rearrange(flat), tot_p[:, :]))
            link(V.tensor_tensor_scan(inc[:, :, :].rearrange(flat), seg[:, :, :].rearrange(flat),
                                      tot[:, :, :].rearrange(flat), 0.0, ALU.mult, ALU.add))
            link(V.tensor_tensor(tot[:, :, :], inc[:, :, :], tot[:, :, :], ALU.subtract))
            link(V.tensor_tensor(rank[:, :, :].rearrange(flat), pre_p[:, :], tot[:, :, :].rearrange(flat), ALU.add))
            cap = float(CAP if ly == 0 else T)
            link(V.tensor_scalar(cnt[:, :], inc[:, :, K * NT - 1], cap, None, ALU.min))
            link(V.tensor_tensor(cmp[:, :, :], wide(cnt[:, :], MAXT), iota[:, E:E + MAXT].unsqueeze(1).to_broadcast([P, E, MAXT]), ALU.is_gt))
            link(V.tensor_reduce(nt[:, :], cmp[:, :, :], AX.X, ALU.add))
            link(V.memset(base[:, :], 1.0))
            link(V.tensor_tensor_scan(end[:, :], base[:, :], nt[:, :], 0.0, ALU.mult, ALU.add))
            link(V.tensor_tensor(base[:, :], end[:, :], nt[:, :], ALU.subtract))
            link(V.tensor_scalar(base[:, :], base[:, :], float(TS), None, ALU.mult))
            tiles = iota[:, 24:24 + NTILES].unsqueeze(2).to_broadcast([P, NTILES, E])
            link(V.tensor_tensor(own[:, :, :], end[:, :].unsqueeze(1).to_broadcast([P, NTILES, E]), tiles, ALU.is_le))
            link(V.tensor_reduce(ownf[:, :], own[:, :, :], AX.X, ALU.add))
            link(V.tensor_scalar(keep["owner"][:, :], ownf[:, :], float(E - 1), None, ALU.min))
            hotc = hot[:, :, :, :].rearrange("p e k j -> p e (k j)")
            link(V.tensor_tensor(tot[:, :, :], rank[:, :, :], hotc, ALU.mult))
            link(V.tensor_reduce(rk[:, :], tot[:, :, :].rearrange("p e c -> p c e"), AX.X, ALU.add))
            link(V.tensor_tensor(tot[:, :, :], hotc, wide(base[:, :], K * NT), ALU.mult))
            link(V.tensor_reduce(slot[:, :], tot[:, :, :].rearrange("p e c -> p c e"), AX.X, ALU.add))
            link(V.tensor_tensor(slot[:, :], slot[:, :], rk[:, :], ALU.add))
            link(V.tensor_scalar(inside[:, :], rk[:, :], cap, None, ALU.is_lt))
            link(V.tensor_tensor(slot[:, :], slot[:, :], inside[:, :], ALU.mult))
            link(V.tensor_tensor(keep["wts"][:, :], keep["wts"][:, :], inside[:, :], ALU.mult))
            link(V.tensor_copy(keep["get"][:, :], slot[:, :]))
            link(V.tensor_scalar(inside[:, :], inside[:, :], -1.0, 1.0, ALU.mult, ALU.add))
            link(V.tensor_tensor(put[:, :], inside[:, :], iota[:, 64:64 + K * NT], ALU.mult))
            V.tensor_tensor(keep["put"][:, :], put[:, :], slot[:, :], ALU.add).then_inc(put_ok.sem, 1)


def experts(nc, io, keep, ly):
    with ExitStack() as ctx:
        r = Room(nc, ctx, f"ex{ly}", keep)
        ident = keep["ident"]
        SB = TS // P
        w1 = [r.sb(f"w1_{i}", [P, KD, H]) for i in range(2)]
        w2 = [r.sb(f"w2_{i}", [P, MH, D]) for i in range(2)]
        b1 = [r.sb(f"b1_{i}", [P, MH]) for i in range(2)]
        b2 = [r.sb(f"b2_{i}", [P, D]) for i in range(2)]
        xin = [r.sb(f"xin{i}", [P, SB, D]) for i in range(2)]
        xT = [r.sb(f"xT{i}", [P, KD, TS]) for i in range(2)]
        hid = [r.sb(f"hid{i}", [P, MH, TS]) for i in range(2)]
        y = [r.sb(f"y{i}", [P, SB, D]) for i in range(2)]
        tp = [r.ps(f"tp{i}", [P, KD, TS]) for i in range(2)]
        hp = [r.ps(f"hp{i}", [P, 2, TS]) for i in range(4)]
        yp = [r.ps(f"yp{i}", [P, SB, D]) for i in range(2)]
        w1_in, w2_in = [r.sig(f"w1_in{i}", 32) for i in range(2)], [r.sig(f"w2_in{i}", 32) for i in range(2)]
        x_in = [r.sig(f"x_in{i}", 16) for i in range(2)]
        turned, xT_ok = r.sig("turned"), r.sig("xT_ok")
        h_mm, h_ok = r.sig("h_mm", MH // 2), r.sig("h_ok", MH // 2)
        y_mm, y_ok = r.sig("y_mm"), [r.sig(f"y_ok{i}") for i in range(2)]
        y_out = [r.sig(f"y_out{i}", 16) for i in range(2)]
        block = ctx.enter_context(nc.Block())
        W1, W2, B1, B2 = (io[f"{n}_{ly}"] for n in ("w1", "w2", "b1", "b2"))
        xbuf = io[f"xbuf{ly}"][0:SLOTS, :].rearrange("(t s p) d -> t p s d", s=SB, p=P)
        ybuf = io[f"ybuf{ly}"].rearrange("(t s p) d -> t p s d", s=SB, p=P)

        def one(ap, t):
            return ap[t] if isinstance(t, int) else ap[bass.ds(t, 1)].rearrange("o p s d -> (o p) s d")

        def tiles(eng, body):
            for t in range(3):
                body(t, t % 2, t // 2)
            with eng.Fori(1, (NTILES - 2) // 2) as i:
                body(i * 2 + 1, 1, i)
                body(i * 2 + 2, 0, i + 1)
            for t in range(1 + 2 * ((NTILES - 2) // 2), NTILES):
                body(t, t % 2, t // 2)

        def first(t):
            return isinstance(t, int) and t == 0

        def old(t):
            return not isinstance(t, int) or t >= 2

        def final(t):
            return isinstance(t, int) and t == NTILES - 1

        @block.sync
        def _(sp):
            def body(t, par, rd):
                idx = keep["owner"][0:1, t:t + 1] if isinstance(t, int) else keep["owner"][0:1, bass.ds(t, 1)]
                e = sp.value_load(idx, min_val=0, max_val=E - 1)
                if old(t):
                    sp.wait_ge(turned.sem, turned.at(t - 2))
                sp.dma_start(xin[par][:, :, :], one(xbuf, t)).then_inc(x_in[par].sem, 16)
                if old(t):
                    sp.wait_ge(h_mm.sem, h_mm.at(t - 2))
                sp.dma_start(w1[par][:, :, :], W1[bass.ds(e, 1)].rearrange("o (k p) h -> (o p) k h", p=P)).then_inc(w1_in[par].sem, 16)
                if old(t):
                    sp.wait_ge(h_ok.sem, h_ok.at(t - 2))
                sp.dma_start(b1[par][:, :], B1[bass.ds(e, 1)].rearrange("o p m -> (o p) m")).then_inc(w1_in[par].sem, 16)
                if old(t):
                    sp.wait_ge(y_mm.sem, y_mm.at(t - 2))
                sp.dma_start(w2[par][:, :, :], W2[bass.ds(e, 1)].rearrange("o (m p) d -> (o p) m d", p=P)).then_inc(w2_in[par].sem, 16)
                if old(t):
                    sp.wait_ge(y_ok[par].sem, rd)
                sp.dma_start(b2[par][:, :], B2[bass.ds(e, 1), :].to_broadcast([P, D])).then_inc(w2_in[par].sem, 16)

            tiles(sp, body)

        @block.gpsimd
        def _(pool):
            def body(t, par, rd):
                pool.wait_ge(y_ok[par].sem, y_ok[par].at(rd))
                pool.dma_start(one(ybuf, t), y[par][:, :, :]).then_inc(y_out[par].sem, 16)

            tiles(pool, body)
            pool.wait_ge(y_out[0].sem, 16 * ((NTILES + 1) // 2))
            pool.wait_ge(y_out[1].sem, 16 * (NTILES // 2))

        @block.scalar
        def _(act):
            def body(t, par, rd):
                if old(t):
                    act.wait_ge(y_mm.sem, y_mm.at(t - 2))
                act.wait_ge(w1_in[par].sem, w1_in[par].at(rd))
                for i in range(MH // 2):
                    act.wait_ge(h_mm.sem, h_mm.at(t, i + 1))
                    for m in range(2):
                        ins = nc.scalar.activation(hid[par][:, 2 * i + m, :], hp[i][:, m, :], ACT.Gelu,
                                                   bias=b1[par][:, 2 * i + m:2 * i + m + 1])
                    ins.then_inc(h_ok.sem, 1)

            tiles(act, body)

        @block.vector
        def _(dve):
            def rows(t, par):
                if old(t):
                    dve.wait_ge(h_mm.sem, h_mm.at(t - 2))
                dve.wait_ge(turned.sem, turned.at(t))
                nc.vector.tensor_copy(xT[par][:, :, :], tp[par][:, :, :]).then_inc(xT_ok.sem, 1)

            def out(t, par, rd):
                dve.wait_ge(w2_in[par].sem, w2_in[par].at(rd))
                if old(t):
                    dve.wait_ge(y_out[par].sem, y_out[par].per * rd)
                dve.wait_ge(y_mm.sem, y_mm.at(t))
                nc.vector.tensor_tensor(y[par][:, :, :], yp[par][:, :, :], b2[par][:, :].unsqueeze(1).to_broadcast([P, SB, D]),
                                        ALU.add).then_inc(y_ok[par].sem, 1)

            def body(t, par, rd):
                if first(t):
                    rows(0, 0)
                if not final(t):
                    rows(t + 1, 1 - par)
                if not first(t):
                    out(t - 1, 1 - par, rd - 1 + par)

            tiles(dve, body)
            out(NTILES - 1, (NTILES - 1) % 2, (NTILES - 1) // 2)

        @block.tensor
        def _(pe):
            def turn(t, par, rd):
                pe.wait_ge(x_in[par].sem, x_in[par].at(rd))
                if old(t):
                    pe.wait_ge(xT_ok.sem, xT_ok.at(t - 2))
                for s in range(SB):
                    for k in range(KD):
                        mm = nc.tensor.transpose(tp[par][:, k, s * P:(s + 1) * P], xin[par][:, s, k * P:(k + 1) * P], ident[:, :])
                mm.then_inc(turned.sem, 1)

            def up(t, par, rd):
                pe.wait_ge(w1_in[par].sem, w1_in[par].at(rd))
                pe.wait_ge(xT_ok.sem, xT_ok.at(t))
                for i in range(MH // 2):
                    if not first(t):
                        pe.wait_ge(h_ok.sem, h_ok.at(t - 1, i + 1))
                    for m in (2 * i, 2 * i + 1):
                        for k in range(KD):
                            mm = nc.tensor.matmul(hp[i][:, m % 2, :], w1[par][:, k, m * P:(m + 1) * P], xT[par][:, k, :],
                                                  start=(k == 0), stop=(k == KD - 1))
                    mm.then_inc(h_mm.sem, 1)

            def down(t, par, rd):
                pe.wait_ge(w2_in[par].sem, w2_in[par].at(rd))
                if old(t):
                    pe.wait_ge(y_ok[par].sem, rd)
                pe.wait_ge(h_ok.sem, h_ok.at(t))
                for s in range(SB):
                    for m in range(MH):
                        mm = nc.tensor.matmul(yp[par][:, s, :], hid[par][:, m, s * P:(s + 1) * P], w2[par][:, m, :],
                                              start=(m == 0), stop=(m == MH - 1))
                mm.then_inc(y_mm.sem, 1)

            def body(t, par, rd):
                if first(t):
                    turn(0, 0, 0)
                up(t, par, rd)
                if not final(t):
                    turn(t + 1, 1 - par, rd + par)
                if not first(t):
                    down(t - 1, 1 - par, rd - 1 + par)

            tiles(pe, body)
            down(NTILES - 1, (NTILES - 1) % 2, (NTILES - 1) // 2)


def gather(nc, io, keep, ly, pool, dst, got, free, order):
    for n, j in enumerate(order):
        for k in range(K):
            buf = n % len(dst[k])
            if n >= len(dst[k]):
                pool.wait_ge(free.sem, n - len(dst[k]) + 1)
            c = k * NT + j
            pool.indirect_dma_start(dst[k][buf][:, :], None, io[f"ybuf{ly}"],
                                    bass.IndirectOffsetOnAxis(ap=keep["get"][:, c:c + 1], axis=0)).then_inc(got[buf].sem, 16)


def mixer(nc, io, keep):
    with ExitStack() as ctx:
        r = Room(nc, ctx, "mix", keep)
        ident = keep["ident"]
        NST = SQ // P
        W3 = 3 * D
        w_qkv = r.sb("w_qkv", [P, KD, W3])
        w_o = r.sb("w_o", [P, KD, D])
        w_gate = r.sb("w_gate", [P, KD, E])
        b_qkv = r.sb("b_qkv", [P, W3])
        b_o = r.sb("b_o", [P, D])
        gb0 = r.sb("gb0", [P, TQ, D])
        rep = r.sb("rep", [P, TQ, 3, D])
        eps = r.sb("eps", [P, 1])
        yk = [[r.sb(f"y{k}_{i}", [P, D]) for i in range(4)] for k in range(K)]
        x = r.sb("x", [P, TQ, D])
        st, mom, rstd = r.sb("st", [P, TQ, 6]), r.sb("mom", [P, 3, TQ]), r.sb("rstd", [P, TQ])
        xn = r.sb("xn", [P, TQ, D])
        hT = r.sb("hT", [P, KD, TQ, P])
        qkv = r.sb("qkv", [P, TQ, W3])
        mean = r.sb("mean", [P, 2, D])
        rs = r.sb("rs", [P, 2, D])
        corr = r.sb("corr", [P, HEADS, HD, HD])
        rz = r.sb("rz", [P, HEADS, HD])
        prod = [r.sb(f"prod{i}", [P, TQ * D]) for i in range(4)]
        att = r.sb("att", [P, TQ, D])
        bank = r.ps("bank", [P, 8, 512])
        NPC, NPA = 2 * TQ, HD
        NPR = NPC + NPA
        weights, ready = r.sig("weights"), r.sig("ready")
        x_in, got, used = r.sig("x_in", 16), [r.sig(f"got{i}", 16 * K) for i in range(4)], r.sig("used", TQ)
        yw, ysum, x2_ok = r.sig("yw", TQ), r.sig("ysum"), r.sig("x2_ok")
        stats, means, rstds, norms = r.sig("stats", 2 * TQ), r.sig("means", 12), r.sig("rstds", 4), r.sig("norms", 2 * TQ)
        turned, hT_ok = r.sig("turned", 12), r.sig("hT_ok", 3)
        qkv_mm, qkv_ok = r.sig("qkv_mm", TQ), r.sig("qkv_ok", TQ)
        msum, centred, sq, sqs, unit, unit_ok = r.sig("msum"), r.sig("centred"), r.sig("sq"), r.sig("sqs"), r.sig("unit", 2), r.sig("unit_ok")
        prod_ok, acc_ok = r.sig("prod_ok", NPR), r.sig("acc_ok", NPR)
        clip_ok, exp_ok, zs_ok, rz_ok, att_ok = r.sig("clip_ok", 2), r.sig("exp_ok", 2), r.sig("zs_ok"), r.sig("rz_ok"), r.sig("att_ok")
        o_mm, o_b, o_g, x3_ok, sc_ok, h_ok, lg_mm, lg_ok = (r.sig(n) for n in ("o_mm", "o_b", "o_g", "x3_ok", "sc_ok", "h_ok", "lg_mm", "lg_ok"))
        x_out, h_out = r.sig("x_out", 16), r.sig("h_out", 16)
        block = ctx.enter_context(nc.Block())

        def seqs(name):
            return io[name].rearrange("(t s p) d -> s p t d", t=TQ, p=P)

        def one(ap, s):
            return ap[s] if isinstance(s, int) else ap[bass.ds(s, 1)].rearrange("o p t d -> (o p) t d")

        def rounds(eng, body):
            body(0, False)
            with eng.Fori(1, NST) as s:
                body(s, True)

        @block.sync
        def _(sp):
            mod = io["modrow"][1]
            for dst, src in ((w_qkv[:, :, :], io["WqkvT"]), (w_o[:, :, :], io["WoutT"]), (w_gate[:, :, :], io["gate1"]),
                             (b_qkv[:, :], io["bqkv"].to_broadcast([P, W3])), (b_o[:, :], io["bout"].to_broadcast([P, D]))):
                sp.dma_start(dst, src).then_inc(weights.sem, 16)
            for b in range(B):
                sp.dma_start(gb0[:, b, :], io["modrow"][0][b:b + 1, 3 * D:].to_broadcast([P, D])).then_inc(weights.sem, 16)
                sp.dma_start(rep[:, b, :, :].rearrange("p m d -> p (m d)"), mod[b:b + 1, 0:3 * D].to_broadcast([P, 3 * D])).then_inc(weights.sem, 16)
            def body(s, later):
                if later:
                    sp.wait_ge(x_out.sem, s * 16)
                sp.dma_start(x[:, :, :], one(seqs("x1"), s)).then_inc(x_in.sem, 16)
                sp.wait_ge(x3_ok.sem, x3_ok.at(s))
                sp.dma_start(one(seqs("x3"), s), x[:, :, :]).then_inc(x_out.sem, 16)
                sp.wait_ge(h_ok.sem, h_ok.at(s))
                sp.dma_start(one(seqs("h1"), s), xn[:, :, :]).then_inc(h_out.sem, 16)

            rounds(sp, body)
            sp.wait_ge(x_out.sem, 16 * NST)
            sp.wait_ge(h_out.sem, 16 * NST)

        @block.gpsimd
        def _(pool):
            gather(nc, io, keep, 0, pool, yk, got, used, [t * NST + s for s in range(NST) for t in range(TQ)])

        @block.scalar
        def _(act):
            act.wait_ge(ready.sem, 1)

            def norm(s, half):
                act.wait_ge(means.sem, means.at(s, 6 * (half + 1)))
                nc.scalar.activation(rstd[:, :], mom[:, 2, :], ACT.Ln, bias=eps[:, 0:1], scale=1.0 / D).then_inc(rstds.sem, 1)
                act.wait_ge(rstds.sem, rstds.at(s, 2 * half + 1))
                nc.scalar.activation(rstd[:, :], rstd[:, :], ACT.Exp, scale=-0.5).then_inc(rstds.sem, 1)

            def body(s, later):
                norm(s, 0)
                for g in range(4):
                    act.wait_ge(turned.sem, turned.at(s, g + 1))
                    for dh in range(KD):
                        for t in (2 * g, 2 * g + 1):
                            ins = nc.scalar.activation(hT[:, dh, t, :], bank[:, g, (2 * dh + t % 2) * P:(2 * dh + t % 2 + 1) * P],
                                                       ACT.Identity, scale=keep["modT"][:, 1, KD + dh, t:t + 1],
                                                       bias=keep["modT"][:, 1, dh, t:t + 1])
                ins.then_inc(hT_ok.sem, 1)
                act.wait_ge(sqs.sem, sqs.at(s))
                nc.scalar.activation(rs[:, :, :], rs[:, :, :], ACT.Ln).then_inc(unit.sem, 1)
                act.wait_ge(unit.sem, unit.at(s, 1))
                nc.scalar.activation(rs[:, :, :], rs[:, :, :], ACT.Exp, scale=-0.5).then_inc(unit.sem, 1)
                for hf in range(2):
                    act.wait_ge(clip_ok.sem, clip_ok.at(s, hf + 1))
                    c = corr[:, 8 * hf:8 * hf + 8, :, :].rearrange("p h i j -> p (h i j)")
                    nc.scalar.activation(c, c, ACT.Exp).then_inc(exp_ok.sem, 1)
                for g in range(4):
                    act.wait_ge(turned.sem, turned.at(s, 5 + g))
                    ins = nc.scalar.activation(hT[:, :, 2 * g:2 * g + 2, :], bank[:, g, :].rearrange("p (d t c) -> p d t c", d=KD, t=2), ACT.Copy)
                ins.then_inc(hT_ok.sem, 1)
                norm(s, 1)
                for g in range(4):
                    act.wait_ge(turned.sem, turned.at(s, 9 + g))
                    ins = nc.scalar.activation(hT[:, :, 2 * g:2 * g + 2, :], bank[:, g, :].rearrange("p (d t c) -> p d t c", d=KD, t=2), ACT.Copy)
                ins.then_inc(hT_ok.sem, 1)

            rounds(act, body)

        @block.vector
        def _(dve):
            V = nc.vector
            V.memset(eps[:, :], EPS).then_inc(ready.sem, 1)
            dve.wait_ge(weights.sem, 16 * (5 + 2 * B))

            def column(c):
                return keep["wts"][:, c:c + 1] if isinstance(c, int) else keep["wts"][:, bass.ds(c, 1)]

            def norm(s, half):
                for t in range(TQ):
                    V.bn_stats(st[:, t, :], x[:, t, :]).then_inc(stats.sem, 1)
                dve.wait_ge(stats.sem, stats.at(s, TQ * (half + 1)))
                moments(nc, dve, means.at(s, 6 * half), mom, st, TQ, means)
                dve.wait_ge(rstds.sem, rstds.at(s, 2 * half + 2))
                for t in range(TQ):
                    V.tensor_scalar(xn[:, t, :], x[:, t, :], mom[:, 0, t:t + 1], rstd[:, t:t + 1], ALU.subtract, ALU.mult).then_inc(norms.sem, 1)

            def body(s, later):
                if later:
                    dve.wait_ge(h_out.sem, s * 16)
                for t in range(TQ):
                    dve.wait_ge(got[t % 4].sem, got[t % 4].per * (s * 2 + t // 4 + 1))
                    wt = [column(s + (k * NT + t * NST)) for k in range(K)]
                    V.tensor_scalar(xn[:, t, :], yk[0][t % 4][:, :], wt[0], None, ALU.mult).then_inc(yw.sem, 1)
                    dve.wait_ge(yw.sem, yw.at(s, t + 1))
                    V.scalar_tensor_tensor(xn[:, t, :], yk[1][t % 4][:, :], wt[1], xn[:, t, :], ALU.mult, ALU.add).then_inc(used.sem, 1)
                dve.wait_ge(used.sem, used.at(s))
                V.tensor_tensor(xn[:, :, :], xn[:, :, :], gb0[:, :, :], ALU.mult).then_inc(ysum.sem, 1)
                dve.wait_ge(ysum.sem, ysum.at(s))
                dve.wait_ge(x_in.sem, x_in.at(s))
                V.tensor_tensor(x[:, :, :], x[:, :, :], xn[:, :, :], ALU.add).then_inc(x2_ok.sem, 1)
                dve.wait_ge(x2_ok.sem, x2_ok.at(s))
                norm(s, 0)
                for t in range(TQ):
                    dve.wait_ge(qkv_mm.sem, qkv_mm.at(s, t + 1))
                    b0 = 4 + 2 * (t % 2)
                    V.tensor_tensor(qkv[:, t, :], bank[:, b0:b0 + 2, :].rearrange("p b c -> p (b c)")[:, 0:W3], b_qkv[:, :],
                                    ALU.add).then_inc(qkv_ok.sem, 1)
                dve.wait_ge(qkv_ok.sem, qkv_ok.at(s))
                qk = qkv[:, :, 0:2 * D]
                V.tensor_reduce(mean[:, :, :].rearrange("p a d -> p (a d)"), qk.rearrange("p t c -> p c t"), AX.X, ALU.add).then_inc(msum.sem, 1)
                dve.wait_ge(msum.sem, msum.at(s))
                mb = mean[:, :, :].rearrange("p a d -> p (a d)").unsqueeze(1).to_broadcast([P, TQ, 2 * D])
                V.scalar_tensor_tensor(qk, mb, -1.0 / TQ, qk, ALU.mult, ALU.add).then_inc(centred.sem, 1)
                dve.wait_ge(centred.sem, centred.at(s))
                for g in range(2):
                    half = prod[g][:, :].rearrange("p (t c) -> p t c", t=TQ)
                    ins = V.tensor_tensor(half, qkv[:, :, g * D:(g + 1) * D], qkv[:, :, g * D:(g + 1) * D], ALU.mult)
                ins.then_inc(sq.sem, 1)
                dve.wait_ge(sq.sem, sq.at(s))
                for g in range(2):
                    ins = V.tensor_reduce(rs[:, g, :], prod[g][:, :].rearrange("p (t c) -> p c t", t=TQ), AX.X, ALU.add)
                ins.then_inc(sqs.sem, 1)
                dve.wait_ge(unit.sem, unit.at(s))
                V.tensor_tensor(qk, qk, rs[:, :, :].rearrange("p a d -> p (a d)").unsqueeze(1).to_broadcast([P, TQ, 2 * D]),
                                ALU.mult).then_inc(unit_ok.sem, 1)
                dve.wait_ge(unit_ok.sem, unit_ok.at(s))
                for hf in range(2):
                    for t in range(TQ):
                        n = TQ * hf + t
                        if n >= 4:
                            dve.wait_ge(acc_ok.sem, acc_ok.at(s, n - 3))
                        q_ = qkv[:, t, 128 * hf:128 * hf + 128].rearrange("p (h i) -> p h i", i=HD).unsqueeze(3).to_broadcast([P, 8, HD, HD])
                        k_ = qkv[:, t, D + 128 * hf:D + 128 * hf + 128].rearrange("p (h j) -> p h j", j=HD).unsqueeze(2).to_broadcast([P, 8, HD, HD])
                        V.tensor_tensor(prod[n % 4][:, :].rearrange("p (h i j) -> p h i j", h=8, i=HD), q_, k_, ALU.mult).then_inc(prod_ok.sem, 1)
                for hf in range(2):
                    dve.wait_ge(acc_ok.sem, acc_ok.at(s, TQ * (hf + 1)))
                    V.tensor_scalar(corr[:, 8 * hf:8 * hf + 8, :, :].rearrange("p h i j -> p (h i j)"),
                                    bank[:, 4 * hf:4 * hf + 4, :].rearrange("p b c -> p (b c)"), 0.0, 1.0, ALU.max, ALU.min).then_inc(clip_ok.sem, 1)
                dve.wait_ge(exp_ok.sem, exp_ok.at(s))
                V.tensor_reduce(rz[:, :, :], corr[:, :, :, :].rearrange("p h i j -> p h j i"), AX.X, ALU.add).then_inc(zs_ok.sem, 1)
                dve.wait_ge(zs_ok.sem, zs_ok.at(s))
                V.reciprocal(rz[:, :, :], rz[:, :, :]).then_inc(rz_ok.sem, 1)
                for d in range(HD):
                    n = NPC + d
                    dve.wait_ge(acc_ok.sem, acc_ok.at(s, n - 3))
                    v_ = qkv[:, :, 2 * D:].rearrange("p t (h d) -> p t h d", d=HD)[:, :, :, d:d + 1].to_broadcast([P, TQ, HEADS, HD])
                    c_ = corr[:, :, d, :].unsqueeze(1).to_broadcast([P, TQ, HEADS, HD])
                    V.tensor_tensor(prod[n % 4][:, :].rearrange("p (t h e) -> p t h e", t=TQ, h=HEADS), v_, c_, ALU.mult).then_inc(prod_ok.sem, 1)
                dve.wait_ge(acc_ok.sem, acc_ok.at(s))
                dve.wait_ge(rz_ok.sem, rz_ok.at(s))
                V.tensor_tensor(att[:, :, :], bank[:, 0:4, :].rearrange("p b (t c) -> p (b t) c", t=2),
                                rz[:, :, :].rearrange("p h e -> p (h e)").unsqueeze(1).to_broadcast([P, TQ, D]), ALU.mult).then_inc(att_ok.sem, 1)
                dve.wait_ge(o_mm.sem, o_mm.at(s))
                V.tensor_tensor(xn[:, :, :], bank[:, 4:8, :].rearrange("p b (t c) -> p (b t) c", t=2),
                                b_o[:, :].unsqueeze(1).to_broadcast([P, TQ, D]), ALU.add).then_inc(o_b.sem, 1)
                dve.wait_ge(o_b.sem, o_b.at(s))
                V.tensor_tensor(xn[:, :, :], xn[:, :, :], rep[:, :, 0, :], ALU.mult).then_inc(o_g.sem, 1)
                dve.wait_ge(o_g.sem, o_g.at(s))
                V.tensor_tensor(x[:, :, :], x[:, :, :], xn[:, :, :], ALU.add).then_inc(x3_ok.sem, 1)
                dve.wait_ge(x3_ok.sem, x3_ok.at(s))
                norm(s, 1)
                dve.wait_ge(norms.sem, norms.at(s))
                V.tensor_tensor(xn[:, :, :], xn[:, :, :], rep[:, :, 2, :], ALU.mult).then_inc(sc_ok.sem, 1)
                dve.wait_ge(sc_ok.sem, sc_ok.at(s))
                V.tensor_tensor(xn[:, :, :], xn[:, :, :], rep[:, :, 1, :], ALU.add).then_inc(h_ok.sem, 1)
                dve.wait_ge(lg_mm.sem, lg_mm.at(s))
                dst = keep["logits"][:, :, :].rearrange("p (t s) e -> p s t e", s=NST)
                dst = dst[:, s] if isinstance(s, int) else dst[:, bass.ds(s, 1)].rearrange("p o t e -> p (o t) e")
                V.tensor_scalar(dst, bank[:, 4, 0:TQ * E].rearrange("p (t e) -> p t e", t=TQ), 1.0, None, ALU.mult).then_inc(lg_ok.sem, 1)

            rounds(dve, body)

        @block.tensor
        def _(pe):
            pe.wait_ge(weights.sem, 16 * (5 + 2 * B))

            def turn(src):
                for g in range(4):
                    for dh in range(KD):
                        for t in (2 * g, 2 * g + 1):
                            mm = nc.tensor.transpose(bank[:, g, (2 * dh + t % 2) * P:(2 * dh + t % 2 + 1) * P], src[:, t, dh * P:(dh + 1) * P], ident[:, :])
                    mm.then_inc(turned.sem, 1)

            def body(s, later):
                if later:
                    pe.wait_ge(hT_ok.sem, s * 3)
                pe.wait_ge(norms.sem, norms.at(s, TQ))
                turn(xn)
                if later:
                    pe.wait_ge(lg_ok.sem, s)
                pe.wait_ge(hT_ok.sem, hT_ok.at(s, 1))
                for t in range(TQ):
                    if t >= 2:
                        pe.wait_ge(qkv_ok.sem, qkv_ok.at(s, t - 1))
                    b0 = 4 + 2 * (t % 2)
                    for c0, c1, bk in ((0, 512, b0), (512, W3, b0 + 1)):
                        for k in range(KD):
                            mm = nc.tensor.matmul(bank[:, bk, 0:c1 - c0], hT[:, k, t, :], w_qkv[:, k, c0:c1], start=(k == 0), stop=(k == KD - 1))
                    mm.then_inc(qkv_mm.sem, 1)
                for n in range(NPR):
                    pe.wait_ge(prod_ok.sem, prod_ok.at(s, n + 1))
                    if n == NPC:
                        pe.wait_ge(clip_ok.sem, clip_ok.at(s, 1))
                    b0 = 4 if TQ <= n < NPC else 0
                    a, z = (n % TQ == 0, n % TQ == TQ - 1) if n < NPC else (n == NPC, n == NPR - 1)
                    for i in range(4):
                        mm = nc.tensor.matmul(bank[:, b0 + i, :], ident[:, :], prod[n % 4][:, 512 * i:512 * (i + 1)], start=a, stop=z)
                    mm.then_inc(acc_ok.sem, 1)
                pe.wait_ge(att_ok.sem, att_ok.at(s))
                turn(att)
                pe.wait_ge(hT_ok.sem, hT_ok.at(s, 2))
                pe.wait_ge(clip_ok.sem, clip_ok.at(s, 2))
                for t in range(TQ):
                    for k in range(KD):
                        mm = nc.tensor.matmul(bank[:, 4 + t // 2, (t % 2) * D:(t % 2 + 1) * D], hT[:, k, t, :], w_o[:, k, :], start=(k == 0), stop=(k == KD - 1))
                mm.then_inc(o_mm.sem, 1)
                pe.wait_ge(h_ok.sem, h_ok.at(s))
                turn(xn)
                pe.wait_ge(hT_ok.sem, hT_ok.at(s))
                pe.wait_ge(o_b.sem, o_b.at(s))
                for t in range(TQ):
                    for k in range(KD):
                        mm = nc.tensor.matmul(bank[:, 4, t * E:(t + 1) * E], hT[:, k, t, :], w_gate[:, k, :], start=(k == 0), stop=(k == KD - 1))
                mm.then_inc(lg_mm.sem, 1)

            rounds(pe, body)


def last(nc, io, keep):
    with ExitStack() as ctx:
        r = Room(nc, ctx, "last", keep)
        gb = [r.sb(f"gb{i}", [P, D]) for i in range(2)]
        yk = [[r.sb(f"y{k}_{i}", [P, D]) for i in range(8)] for k in range(K)]
        x = [r.sb(f"x{i}", [P, JT, D]) for i in range(2)]
        acc = [r.sb(f"acc{i}", [P, JT, D]) for i in range(2)]
        x_in, out = [r.sig(f"x_in{i}", 32) for i in range(2)], [r.sig(f"out{i}", 16) for i in range(2)]
        got, used = [r.sig(f"got{i}", 16 * K) for i in range(8)], r.sig("used", JT)
        yw, gated, sum_ok = r.sig("yw", JT), r.sig("gated"), r.sig("sum_ok")
        block = ctx.enter_context(nc.Block())

        def one(ap, b):
            return ap[b] if isinstance(b, int) else ap[bass.ds(b, 1)].rearrange("o p j d -> (o p) j d")

        def pairs(eng, body):
            body(0, False)
            with eng.Fori(1, B // 2) as i:
                body(i, True)

        @block.sync
        def _(sp):
            src = io["x3"].rearrange("(b j p) d -> b p j d", b=B, p=P)
            dst = io["out"].rearrange("b (j p) d -> b p j d", p=P)
            def body(i, later):
                for h in range(2):
                    if later:
                        sp.wait_ge(out[h].sem, i * 16)
                    sp.dma_start(x[h][:, :, :], one(src, i * 2 + h)).then_inc(x_in[h].sem, 16)
                    b = i * 2 + h
                    src_gb = io["modrow"][1][b:b + 1, 3 * D:] if isinstance(b, int) else io["modrow"][1][bass.ds(b, 1), 3 * D:]
                    sp.dma_start(gb[h][:, :], src_gb.to_broadcast([P, D])).then_inc(x_in[h].sem, 16)
                for h in range(2):
                    sp.wait_ge(sum_ok.sem, sum_ok.at(i * 2 + h))
                    sp.dma_start(one(dst, i * 2 + h), x[h][:, :, :]).then_inc(out[h].sem, 16)

            pairs(sp, body)
            for h in range(2):
                sp.wait_ge(out[h].sem, 16 * (B // 2))

        @block.gpsimd
        def _(pool):
            gather(nc, io, keep, 1, pool, yk, got, used, range(NT))

        @block.vector
        def _(dve):
            V = nc.vector
            def body(i, later):
                for h in range(2):
                    b = i * 2 + h
                    for j in range(JT):
                        n = h * JT + j
                        dve.wait_ge(got[n].sem, got[n].at(i))
                        cs = [b * JT + (k * NT + j) for k in range(K)]
                        wt = [keep["wts"][:, c:c + 1] if isinstance(c, int) else keep["wts"][:, bass.ds(c, 1)] for c in cs]
                        V.tensor_scalar(acc[h][:, j, :], yk[0][n][:, :], wt[0], None, ALU.mult).then_inc(yw.sem, 1)
                        dve.wait_ge(yw.sem, yw.at(b, j + 1))
                        V.scalar_tensor_tensor(acc[h][:, j, :], yk[1][n][:, :], wt[1], acc[h][:, j, :], ALU.mult, ALU.add).then_inc(used.sem, 1)
                    dve.wait_ge(used.sem, used.at(b))
                    dve.wait_ge(x_in[h].sem, x_in[h].at(i))
                    V.tensor_tensor(acc[h][:, :, :], acc[h][:, :, :], gb[h][:, :].unsqueeze(1).to_broadcast([P, JT, D]), ALU.mult).then_inc(gated.sem, 1)
                    dve.wait_ge(gated.sem, gated.at(b))
                    V.tensor_tensor(x[h][:, :, :], x[h][:, :, :], acc[h][:, :, :], ALU.add).then_inc(sum_ok.sem, 1)

            pairs(dve, body)


def program(nc, io, until=99):
    scratch = {"modrow": [2, B, 4 * D], "bc": [2, 2 * NS, L], "x1": [T, D], "h0": [T, D], "x3": [T, D], "h1": [T, D],
               "xbuf0": [SLOTS + K * T, D], "xbuf1": [SLOTS + K * T, D], "ybuf0": [SLOTS, D], "ybuf1": [SLOTS, D]}
    for name, shape in scratch.items():
        io[name] = nc.dram_tensor(f"s_{name}", shape, F32, kind="Internal").ap()
    with ExitStack() as ctx:
        def sb(name, shape, dt=F32):
            return ctx.enter_context(nc.sbuf_tensor(f"keep_{name}", shape, dt))

        keep = {"ident": sb("ident", [P, P]), "below": sb("below", [P, P]), "ones": sb("ones", [P, P]), "iota": sb("iota", [P, P]),
                "modT": sb("modT", [P, 2, 2 * KD, B]), "logits": sb("logits", [P, NT, E]), "wts": sb("wts", [P, K * NT]),
                "put": sb("put", [P, K * NT], I32), "get": sb("get", [P, K * NT], I32), "owner": sb("owner", [P, NTILES], I32), "taken": []}
        stages = [lambda: setup(nc, io, keep), lambda: mamba(nc, io, keep), lambda: route(nc, io, keep, 0),
                  lambda: experts(nc, io, keep, 0), lambda: mixer(nc, io, keep), lambda: route(nc, io, keep, 1),
                  lambda: experts(nc, io, keep, 1), lambda: last(nc, io, keep)]
        for stage in stages[:until]:
            stage()
            nc.clear_and_free_semaphores(keep["taken"])
            keep["taken"].clear()
            nc.all_engine_barrier()


def kernel(**a):
    import numpy as np
    from concourse import bacc
    from concourse.bass_utils import run_bass_kernel_spmd

    def cols(v):
        return np.ascontiguousarray(v.reshape(-1, P).T)

    def rows(w):
        return np.ascontiguousarray(w.reshape(-1, P, w.shape[1]).transpose(1, 0, 2))

    a = {n: np.asarray(v) for n, v in a.items()}
    iota = np.zeros((P, P), np.float32)
    iota[:, 0:E] = E - np.arange(E)
    iota[:, E:E + MAXT] = TS * np.arange(MAXT)
    iota[:, 24:24 + NTILES] = np.arange(NTILES)
    iota[:, 64:64 + K * NT] = SLOTS + P * np.arange(K * NT)[None, :] + np.arange(P)[:, None]
    arrays = {
        "x": a["L0_attn_x"], "W_in": a["L0_attn_W_in"], "conv_k": a["L0_attn_conv_k"], "W_x": a["L0_attn_W_x"],
        "W_dt": a["L0_attn_W_dt"], "A_log": a["L0_attn_A_log"], "W_out": a["L0_attn_W_out"],
        "vecs": np.stack([cols(a["L0_attn_conv_b"]), cols(a["L0_attn_b_dt"]), cols(a["L0_attn_D"])], axis=1),
        "gate0": rows(a["L0_ffn_Wg"].T), "gate1": rows(a["L1_ffn_router_w"]),
        "WqkvT": rows(a["L1_attn_Wqkv"].T), "WoutT": rows(a["L1_attn_Wout"].T),
        "bqkv": a["L1_attn_bqkv"].reshape(1, -1), "bout": a["L1_attn_bout"].reshape(1, -1),
        "cT": np.stack([rows(a["L0_c"].T), rows(a["L1_c"].T)]), "wmod": np.stack([a["L0_wmod"], a["L1_wmod"]]),
        "w1_0": a["L0_ffn_W1"], "w2_0": a["L0_ffn_W2"], "b2_0": a["L0_ffn_b2"],
        "w1_1": a["L1_ffn_w1"], "w2_1": a["L1_ffn_w2"], "b2_1": a["L1_ffn_b2"],
        "b1_0": a["L0_ffn_b1"].reshape(E, MH, P).transpose(0, 2, 1), "b1_1": a["L1_ffn_b1"].reshape(E, MH, P).transpose(0, 2, 1),
        "ident": np.eye(P, dtype=np.float32), "below": np.triu(np.ones((P, P), np.float32), 1), "iota": iota,
    }
    arrays = {n: np.ascontiguousarray(v) for n, v in arrays.items()}
    nc = bacc.Bacc("TRN2", target_bir_lowering=False, num_devices=1)
    io = {n: nc.dram_tensor(f"in_{n}", v.shape, mybir.dt.from_np(v.dtype), kind="ExternalInput").ap() for n, v in arrays.items()}
    io["out"] = nc.dram_tensor("out", (B, L, D), F32, kind="ExternalOutput").ap()
    program(nc, io, kernel.until)
    r = run_bass_kernel_spmd(nc, [{f"in_{n}": v for n, v in arrays.items()}], core_ids=[0])
    return r.results[0]["out"]


kernel.until = 99
```

```python
from contextlib import ExitStack

import concourse.bass as bass
from concourse import mybir

F32 = mybir.dt.float32
F32R = mybir.dt.float32r
I32 = mybir.dt.int32
ALU = mybir.AluOpType
ACT = mybir.ActivationFunctionType
AX = mybir.AxisListType
P = 128

B, L, D = 8, 512, 256
T = B * L
NT = T // P
JT = L // P
DI, NS, DR, TAPS = 512, 16, 64, 4
MD = DI // P
KD = D // P
DT_MIN, DT_MAX = 0.001, 0.1
EPS = 1e-5
E, K = 8, 2
H = 1024
MH = H // P
CAP = int(round(K * T * 1.05 / E))
TS = 256
NTILES = (K * T + E * (TS - 1)) // TS
SLOTS = NTILES * TS
MAXT = (T + TS - 1) // TS
HEADS, HD = 16, 16
TQ, SQ = 8, 512
UNITS = 2 * NS


class Signal:

    def __init__(self, sem, per):
        self.sem, self.per = sem, per

    def at(self, r, k=None):
        return r * self.per + (self.per if k is None else k)


class Room:

    def __init__(self, nc, ctx, tag, keep):
        self.nc, self.ctx, self.tag, self.taken = nc, ctx, tag, keep["taken"]

    def sb(self, name, shape, dt=F32):
        return self.ctx.enter_context(self.nc.sbuf_tensor(f"{self.tag}_{name}", shape, dt))

    def ps(self, name, shape):
        return self.ctx.enter_context(self.nc.psum_tensor(f"{self.tag}_{name}", shape, F32))

    def sig(self, name, per=1):
        sem = self.nc.alloc_semaphore(name=f"{self.tag}_{name}")
        self.taken.append(sem)
        return Signal(sem, per)


def moments(nc, dve, r, mom, stats, n, sig):
    even, odd = stats[:, 0:n, 1], stats[:, 0:n, 4]
    nc.vector.tensor_tensor(mom[:, 0, 0:n], even, odd, ALU.add).then_inc(sig.sem, 1)
    nc.vector.tensor_tensor(mom[:, 1, 0:n], even, odd, ALU.subtract).then_inc(sig.sem, 1)
    nc.vector.tensor_tensor(mom[:, 2, 0:n], stats[:, 0:n, 2], stats[:, 0:n, 5], ALU.add).then_inc(sig.sem, 1)
    dve.wait_ge(sig.sem, r + 3)
    nc.vector.tensor_scalar(mom[:, 0, 0:n], mom[:, 0, 0:n], 0.5, None, ALU.mult).then_inc(sig.sem, 1)
    nc.vector.tensor_tensor(mom[:, 1, 0:n], mom[:, 1, 0:n], mom[:, 1, 0:n], ALU.mult).then_inc(sig.sem, 1)
    dve.wait_ge(sig.sem, r + 5)
    nc.vector.scalar_tensor_tensor(mom[:, 2, 0:n], mom[:, 1, 0:n], D / 4.0, mom[:, 2, 0:n], ALU.mult, ALU.add).then_inc(sig.sem, 1)


def setup(nc, io, keep):
    with ExitStack() as ctx:
        r = Room(nc, ctx, "set", keep)
        cT = r.sb("cT", [P, 2, KD, B])
        sT = r.sb("sT", [P, 2, KD, B])
        wmod = r.sb("wmod", [P, 2, KD, 6 * D])
        row = r.sb("row", [B, 2, 6 * D])
        sgn = r.sb("sgn", [B, 2, 2, D])
        zero = r.sb("zero", [P, 3 * D])
        rowp = r.ps("rowp", [B, 3, 512])
        colp = r.ps("colp", [P, 2 * KD, B])
        c_in, w_in, consts = r.sig("c_in", 32), r.sig("w_in", 32), r.sig("consts", 48)
        silu_c, row_mm, row_cp, col_mm, col_cp = r.sig("silu_c"), r.sig("row_mm"), r.sig("row_cp"), r.sig("col_mm"), r.sig("col_cp")
        step, row_ok, row_out = r.sig("step"), r.sig("row_ok"), r.sig("row_out")
        zeroed, zero_out = r.sig("zeroed"), r.sig("zero_out")
        block = ctx.enter_context(nc.Block())
        zt = SLOTS // P // 3

        @block.sync
        def _(sp):
            for ly in range(2):
                sp.dma_start(cT[:, ly], io["cT"][ly]).then_inc(c_in.sem, 16)
                sp.dma_start(wmod[:, ly], io["wmod"][ly].rearrange("(k p) n -> p k n", p=P)).then_inc(w_in.sem, 16)
            sp.dma_start(keep["ident"][:, :], io["ident"]).then_inc(consts.sem, 16)
            sp.dma_start(keep["below"][:, :], io["below"]).then_inc(consts.sem, 16)
            sp.dma_start(keep["iota"][:, :], io["iota"]).then_inc(consts.sem, 16)
            sp.wait_ge(row_ok.sem, 2)
            for ly in range(2):
                sp.dma_start(io["modrow"][ly], row[:, ly, 2 * D:]).then_inc(row_out.sem, 16)
            sp.wait_ge(row_out.sem, 32)
            sp.wait_ge(consts.sem, 48)

        @block.gpsimd
        def _(pool):
            pool.memset(zero[:, :], 0.0).then_inc(zeroed.sem, 1)
            pool.memset(keep["ones"][:, :], 1.0).then_inc(zeroed.sem, 1)

        @block.scalar
        def _(act):
            act.wait_ge(c_in.sem, 32)
            nc.scalar.activation(sT[:, :, :, :], cT[:, :, :, :], ACT.Silu).then_inc(silu_c.sem, 1)
            act.wait_ge(zeroed.sem, 2)
            for ly in range(2):
                v = io[f"xbuf{ly}"][0:SLOTS, :].rearrange("(a p c) d -> a p (c d)", p=P, c=3)
                with act.Fori(0, zt) as i:
                    act.dma_start(v[bass.ds(i, 1)].rearrange("a p f -> (a p) f"), zero[:, :]).then_inc(zero_out.sem, 16)
            act.wait_ge(zero_out.sem, 2 * zt * 16)

        @block.tensor
        def _(pe):
            pe.wait_ge(silu_c.sem, 1)
            pe.wait_ge(w_in.sem, 32)
            for ly in range(2):
                if ly:
                    pe.wait_ge(row_cp.sem, ly)
                for n in range(3):
                    for k in range(KD):
                        mm = nc.tensor.matmul(rowp[:, n, :], sT[:, ly, k, :], wmod[:, ly, k, n * 512:(n + 1) * 512],
                                              start=(k == 0), stop=(k == KD - 1))
                mm.then_inc(row_mm.sem, 1)
                if ly:
                    pe.wait_ge(col_cp.sem, ly)
                for c in range(2 * KD):
                    for k in range(KD):
                        mm = nc.tensor.matmul(colp[:, c, :], wmod[:, ly, k, c * P:(c + 1) * P], sT[:, ly, k, :],
                                              start=(k == 0), stop=(k == KD - 1))
                mm.then_inc(col_mm.sem, 1)

        @block.vector
        def _(dve):
            n = 0
            for ly in range(2):
                dve.wait_ge(row_mm.sem, ly + 1)
                nc.vector.tensor_copy(row[:, ly, :].rearrange("b (n c) -> b n c", n=3), rowp[:, :, :]).then_inc(row_cp.sem, 1)
                dve.wait_ge(row_cp.sem, ly + 1)
                m = row[:, ly, :].rearrange("b (m d) -> b m d", m=6)
                gate = m[:, 2:6:3, :]
                nc.vector.tensor_scalar(sgn[:, ly], gate, 0.0, 2.0, ALU.is_ge, ALU.mult).then_inc(step.sem, 1)
                n += 1
                dve.wait_ge(step.sem, n)
                nc.vector.tensor_scalar(sgn[:, ly], sgn[:, ly], 1.0, None, ALU.subtract).then_inc(step.sem, 1)
                n += 1
                dve.wait_ge(step.sem, n)
                nc.vector.tensor_tensor(gate, gate, sgn[:, ly], ALU.mult).then_inc(step.sem, 1)
                n += 1
                dve.wait_ge(step.sem, n)
                nc.vector.scalar_tensor_tensor(gate, gate, 0.25, sgn[:, ly], ALU.max, ALU.mult).then_inc(step.sem, 1)
                n += 1
                dve.wait_ge(step.sem, n)
                nc.vector.tensor_scalar(m[:, 4, :], m[:, 4, :], 1.0, None, ALU.add).then_inc(row_ok.sem, 1)
                dve.wait_ge(col_mm.sem, ly + 1)
                nc.vector.tensor_copy(keep["modT"][:, ly, 0:KD, :], colp[:, 0:KD, :]).then_inc(step.sem, 1)
                n += 1
                nc.vector.tensor_scalar(keep["modT"][:, ly, KD:, :], colp[:, KD:, :], 1.0, None, ALU.add).then_inc(col_cp.sem, 1)


def mamba(nc, io, keep):
    with ExitStack() as ctx:
        r = Room(nc, ctx, "mam", keep)
        ident = keep["ident"]
        w_in = r.sb("w_in", [P, KD, 2 * DI])
        w_conv = r.sb("w_conv", [P, TAPS, 2, DI])
        w_x = r.sb("w_x", [P, MD, DR + 2 * NS])
        w_dt = r.sb("w_dt", [DR, DI])
        w_out = r.sb("w_out", [P, MD, D])
        w_gate = r.sb("w_gate", [P, KD, E])
        vecs = r.sb("vecs", [P, 3, MD])
        a_neg = r.sb("a_neg", [P, MD, NS])
        eps = r.sb("eps", [P, 1])
        x = r.sb("x", [P, JT, D])
        st = r.sb("st", [P, JT, 6])
        mom = r.sb("mom", [P, 3, JT])
        rstd = r.sb("rstd", [P, JT])
        hT = r.sb("hT", [P, KD, L])
        xs = r.sb("xs", [P, MD, TAPS - 1 + L])
        raw = r.sb("raw", [P, 2 * MD, L])
        su = [r.sb(f"su{i}", [P, 2 * MD, L]) for i in range(2)]
        dtT = r.sb("dtT", [DR, L])
        bcT = r.sb("bcT", [2 * NS, L])
        delta = [r.sb(f"delta{i}", [P, MD, L]) for i in range(2)]
        du = [r.sb(f"du{i}", [P, MD, L]) for i in range(2)]
        bc = [r.sb(f"bc{i}", [P, 2, 2, L]) for i in range(2)]
        dA = [r.sb(f"dA{i}", [P, 2, L]) for i in range(4)]
        w = [r.sb(f"w{i}", [P, 2, L]) for i in range(4)]
        xres = r.sb("xres", [P, JT, D])
        rep = r.sb("rep", [P, 4, D])
        x1 = r.sb("x1", [P, JT, D])
        h2 = r.sb("h2", [P, JT, D])
        st2 = r.sb("st2", [P, JT, 6])
        mom2 = r.sb("mom2", [P, 3, JT])
        rstd2 = r.sb("rstd2", [P, JT])
        hT2 = r.sb("hT2", [P, KD, L])
        yacc = r.ps("yacc", [P, MD, L])
        fb = [r.ps(f"fb{i}", [P, L]) for i in range(2)]
        tb = [r.ps(f"tb{i}", [P, L]) for i in range(2)]

        weights, ready = r.sig("weights"), r.sig("ready")
        x_in, ln_st, ln_mv, ln_rs, xn_ok = r.sig("x_in", 16), r.sig("ln_st", 4), r.sig("ln_mv", 6), r.sig("ln_rs", 2), r.sig("xn_ok", 4)
        mm = {"turn": r.sig("turn_mm", KD), "in": r.sig("in_mm", 2 * MD), "conv": r.sig("conv_mm", MD),
              "xb": r.sig("xb_mm", 2), "dt": r.sig("dt_mm", MD)}
        ev = {"turn": r.sig("turn_ev", KD), "in": r.sig("in_ev", 2 * MD), "conv": r.sig("conv_ev", MD),
              "xb": r.sig("xb_ev", 2), "dt": r.sig("dt_ev", MD)}
        silued, sp_exp, sp_ln, clipped, du_ok = r.sig("silued", 2), r.sig("sp_exp"), r.sig("sp_ln"), r.sig("clipped"), r.sig("du_ok")
        bc_out, bc_in = r.sig("bc_out", 16), [r.sig(f"bc_in{i}", 64) for i in range(2)]
        da_ok, bu_ok, h_ok, hc_ok, acc_ok = (r.sig(n, UNITS) for n in ("da_ok", "bu_ok", "h_ok", "hc_ok", "acc_ok"))
        yd_ok, z_ok = r.sig("yd_ok", MD), r.sig("z_ok")
        res_in, rep_in = r.sig("res_in", 16), r.sig("rep_in", 16)
        t_mm, o_ok, x1_ok = r.sig("t_mm", 5), r.sig("o_ok", 2), r.sig("x1_ok")
        st2_ok, mv2_ok, rs2_ok, xn2_ok, sc2_ok, h2_ok = r.sig("st2_ok", 4), r.sig("mv2_ok", 6), r.sig("rs2_ok", 2), r.sig("xn2_ok", 4), r.sig("sc2_ok"), r.sig("h2_ok")
        hT2_ok, lg_ok = r.sig("hT2_ok", 2), r.sig("lg_ok")
        x1_out, h2_out = r.sig("x1_out", 16), r.sig("h2_out", 16)
        block = ctx.enter_context(nc.Block())
        x_dram = io["x"].rearrange("b (j p) d -> b p j d", p=P)
        x1_dram = io["x1"].rearrange("(b j p) d -> b p j d", b=B, p=P)
        h_dram = io["h0"].rearrange("(b j p) d -> b p j d", b=B, p=P)

        PHASES, SCAN = 4, 2
        front_mm = [(10, "turn", 0), (10, "turn", 1), (12, "in", 0), (14, "in", 1), (17, "in", 2), (19, "in", 3),
                    (20, "conv", 0), (22, "in", 4), (25, "conv", 1), (26, "in", 5), (30, "conv", 2), (31, "in", 6),
                    (34, "conv", 3), (35, "in", 7), (44, "xb", 0), (45, "xb", 1),
                    (48, "dt", 0), (48, "dt", 1), (50, "dt", 2), (50, "dt", 3)]
        ring = sorted(front_mm, key=lambda job: job[0] % UNITS)
        bank = {(kind, i): fb[n % 2] for n, (_, kind, i) in enumerate(ring)}

        def one(ap, b):
            return ap[b] if isinstance(b, int) else ap[bass.ds(b, 1)].rearrange("o p j d -> (o p) j d")

        def periods(eng, events, unit=None):
            def period(batch, par):
                for q in range(UNITS):
                    for place, step in events:
                        k = place // UNITS
                        if place % UNITS == q and batch(k) is not None:
                            step(batch(k), (par + k) % 2)
                    if unit is not None and batch(SCAN) is not None:
                        unit(batch(SCAN), q, par)

            def fixed(p):
                return lambda k: p - k if 0 <= p - k < B else None

            for p in range(PHASES):
                period(fixed(p), p % 2)
            with eng.Fori(PHASES // 2, B // 2) as i:
                for half in range(2):
                    period(lambda k, half=half: i * 2 + (half - k), half)
            for p in range(B, B + PHASES - 1):
                period(fixed(p), p % 2)

        def before(b, n=1):
            return not isinstance(b, int) or b >= n

        @block.sync
        def _(sp):
            for dst, src in ((w_in[:, :, :], io["W_in"].rearrange("(k p) n -> p k n", p=P)),
                             (w_conv[:, :, :, :].rearrange("p t k n -> p (t k) n"),
                              io["conv_k"].rearrange("t (k p) n -> p (t k) n", p=P)),
                             (w_x[:, :, :], io["W_x"].rearrange("(k p) n -> p k n", p=P)),
                             (w_dt[:, :], io["W_dt"]),
                             (w_out[:, :, :], io["W_out"].rearrange("(k p) n -> p k n", p=P)),
                             (w_gate[:, :, :], io["gate0"]),
                             (vecs[:, :, :], io["vecs"]),
                             (a_neg[:, :, :], io["A_log"].rearrange("(m p) n -> p m n", p=P))):
                sp.dma_start(dst, src).then_inc(weights.sem, 16)

            def load_x(b, par):
                if before(b):
                    sp.wait_ge(mm["turn"].sem, mm["turn"].at(b - 1))
                sp.dma_start(x[:, :, :], one(x_dram, b)).then_inc(x_in.sem, 16)

            def store_bc(b, par):
                if before(b, 2):
                    sp.wait_ge(bc_in[0].sem, bc_in[0].at(b - 2) * (NS // 4))
                    sp.wait_ge(bc_in[1].sem, bc_in[1].at(b - 2) * (NS // 4))
                sp.wait_ge(ev["xb"].sem, ev["xb"].at(b))
                sp.dma_start(io["bc"][par], bcT[:, :]).then_inc(bc_out.sem, 16)

            def load_tail(b, par):
                if before(b):
                    sp.wait_ge(x1_ok.sem, x1_ok.at(b - 1))
                    sp.wait_ge(h2_ok.sem, h2_ok.at(b - 1))
                sp.dma_start(xres[:, :, :], one(x_dram, b)).then_inc(res_in.sem, 16)
                src = io["modrow"][0, bass.ds(b, 1)] if not isinstance(b, int) else io["modrow"][0, b:b + 1]
                sp.dma_start(rep[:, :, :], src.rearrange("o (m d) -> o m d", m=4).to_broadcast([P, 4, D])).then_inc(rep_in.sem, 16)

            def store_x1(b, par):
                sp.wait_ge(x1_ok.sem, x1_ok.at(b))
                sp.dma_start(one(x1_dram, b), x1[:, :, :]).then_inc(x1_out.sem, 16)

            def store_h2(b, par):
                sp.wait_ge(h2_ok.sem, h2_ok.at(b))
                sp.dma_start(one(h_dram, b), h2[:, :, :]).then_inc(h2_out.sem, 16)

            def unit(b, q, par):
                if q % 4:
                    return
                c = q // 4
                if c >= 2 or before(b):
                    sp.wait_ge(hc_ok.sem, hc_ok.at(b, 4 * (c - 1)) if c >= 2 else hc_ok.at(b - 1, UNITS - 4 + 4 * c))
                if c == 0:
                    sp.wait_ge(bc_out.sem, bc_out.at(b))
                src = io["bc"][par].rearrange("(g n) t -> n g t", g=2)[2 * c:2 * c + 2]
                for n in range(2):
                    for g in range(2):
                        sp.dma_start(bc[c % 2][:, n, g], src[n, g:g + 1, :].to_broadcast([P, L])).then_inc(bc_in[c % 2].sem, 16)

            periods(sp, [(0, load_x), (54, store_bc), (98, load_tail), (113, store_x1), (125, store_h2)], unit)
            sp.wait_ge(x1_out.sem, 16 * B)
            sp.wait_ge(h2_out.sem, 16 * B)

        @block.scalar
        def _(act):
            act.wait_ge(weights.sem, 8 * 16)
            nc.scalar.activation(a_neg[:, :, :], a_neg[:, :, :], ACT.Exp).then_inc(ready.sem, 1)
            act.wait_ge(ready.sem, 5)

            def unit(b, q, par):
                n, m0 = q // 2, 2 * (q % 2)
                if q == 0:
                    act.wait_ge(clipped.sem, clipped.at(b))
                if q >= 4 or before(b):
                    act.wait_ge(h_ok.sem, h_ok.at(b, q - 3) if q >= 4 else h_ok.at(b - 1, UNITS + q - 3))
                for m in range(2):
                    ins = nc.scalar.activation(dA[q % 4][:, m, 1:], delta[par][:, m0 + m, 1:], ACT.Exp,
                                               scale=a_neg[:, m0 + m, n:n + 1])
                ins.then_inc(da_ok.sem, 1)

            def evac(kind, i, out, func, b, rows=P, **kw):
                act.wait_ge(mm[kind].sem, mm[kind].at(b, i + 1))
                nc.scalar.activation(out, bank[kind, i][0:rows, :], func, **kw).then_inc(ev[kind].sem, 1)

            def rstd_x(b, par):
                act.wait_ge(ln_mv.sem, ln_mv.at(b))
                nc.scalar.activation(rstd[:, :], mom[:, 2, :], ACT.Ln, bias=eps[:, 0:1], scale=1.0 / D).then_inc(ln_rs.sem, 1)
                act.wait_ge(ln_rs.sem, ln_rs.at(b, 1))
                nc.scalar.activation(rstd[:, :], rstd[:, :], ACT.Exp, scale=-0.5).then_inc(ln_rs.sem, 1)

            def turned(b, par):
                if before(b):
                    act.wait_ge(mm["in"].sem, mm["in"].at(b - 1))
                for dh in range(KD):
                    at = slice(b, b + 1) if isinstance(b, int) else bass.ds(b, 1)
                    evac("turn", dh, hT[:, dh, :], ACT.Identity, b,
                         scale=keep["modT"][:, 0, KD + dh, at], bias=keep["modT"][:, 0, dh, at])

            def in_out(m):
                def step(b, par):
                    if m == 0 and before(b):
                        act.wait_ge(mm["conv"].sem, mm["conv"].at(b - 1))
                    evac("in", m, xs[:, m, TAPS - 1:] if m < MD else raw[:, m - MD, :], ACT.Copy, b)
                return step

            def conv_out(m):
                def step(b, par):
                    evac("conv", m, raw[:, MD + m, :], ACT.Identity, b, bias=vecs[:, 0, m:m + 1])
                return step

            def silu(b, par):
                if before(b, 2):
                    act.wait_ge(t_mm.sem, t_mm.at(b - 2, 2))
                act.wait_ge(ev["conv"].sem, ev["conv"].at(b))
                act.wait_ge(ev["in"].sem, ev["in"].at(b))
                for g in (1, 0):
                    nc.scalar.activation(su[par][:, MD * g:MD * g + MD, :], raw[:, MD * g:MD * g + MD, :], ACT.Silu).then_inc(silued.sem, 1)

            def dt_row(b, par):
                if before(b):
                    act.wait_ge(mm["dt"].sem, mm["dt"].at(b - 1))
                evac("xb", 0, dtT[:, :], ACT.Copy, b, rows=DR)

            def bc_row(b, par):
                if before(b):
                    act.wait_ge(bc_out.sem, bc_out.at(b - 1))
                evac("xb", 1, bcT[:, :], ACT.Copy, b, rows=2 * NS)

            def softplus(b, par):
                act.wait_ge(ev["dt"].sem, ev["dt"].at(b))
                nc.scalar.activation(delta[par][:, :, :], delta[par][:, :, :], ACT.Exp).then_inc(sp_exp.sem, 1)
                act.wait_ge(sp_exp.sem, sp_exp.at(b))
                nc.scalar.activation(delta[par][:, :, :], delta[par][:, :, :], ACT.Ln, bias=1.0).then_inc(sp_ln.sem, 1)

            def rstd_x1(b, par):
                act.wait_ge(mv2_ok.sem, mv2_ok.at(b))
                nc.scalar.activation(rstd2[:, :], mom2[:, 2, :], ACT.Ln, bias=eps[:, 0:1], scale=1.0 / D).then_inc(rs2_ok.sem, 1)
                act.wait_ge(rs2_ok.sem, rs2_ok.at(b, 1))
                nc.scalar.activation(rstd2[:, :], rstd2[:, :], ACT.Exp, scale=-0.5).then_inc(rs2_ok.sem, 1)

            def turned2(b, par):
                for dh in range(KD):
                    act.wait_ge(t_mm.sem, t_mm.at(b, 3 + dh))
                    nc.scalar.activation(hT2[:, dh, :], tb[dh % 2][:, :], ACT.Copy).then_inc(hT2_ok.sem, 1)

            periods(act, [(7, rstd_x), (15, turned)]
                    + [(place + 5, in_out(i)) for place, kind, i in front_mm if kind == "in"]
                    + [(place + 8, conv_out(i)) for place, kind, i in front_mm if kind == "conv"]
                    + [(45, silu), (50, dt_row), (51, bc_row), (56, softplus), (114, rstd_x1), (125, turned2)], unit)

        @block.vector
        def _(dve):
            for i in range(4):
                nc.vector.memset(dA[i][:, :, 0:1], 0.0)
            nc.vector.memset(xs[:, :, 0:TAPS - 1], 0.0).then_inc(ready.sem, 1)
            nc.vector.memset(eps[:, :], EPS).then_inc(ready.sem, 1)
            nc.vector.memset(rstd[:, :], 0.0).then_inc(ready.sem, 1)
            dve.wait_ge(ready.sem, 4)
            nc.vector.tensor_scalar(a_neg[:, :, :], a_neg[:, :, :], -1.0, None, ALU.mult).then_inc(ready.sem, 1)

            def unit(b, q, par):
                n, m0 = q // 2, 2 * (q % 2)
                if q == 0:
                    dve.wait_ge(du_ok.sem, du_ok.at(b))
                if q % 4 == 0:
                    dve.wait_ge(bc_in[(q // 4) % 2].sem, b * (64 * NS // 4) + 64 * (q // 8 + 1))
                if q >= 4 or before(b):
                    dve.wait_ge(acc_ok.sem, acc_ok.at(b, q - 3) if q >= 4 else acc_ok.at(b - 1, UNITS + q - 3))
                bn = bc[(q // 4) % 2][:, n % 2, 0:1, :].to_broadcast([P, 2, L])
                nc.vector.tensor_tensor(w[q % 4][:, :, :], du[par][:, m0:m0 + 2, :], bn, ALU.mult).then_inc(bu_ok.sem, 1)
                dve.wait_ge(bu_ok.sem, bu_ok.at(b, q + 1))
                dve.wait_ge(da_ok.sem, da_ok.at(b, q + 1))
                wf = w[q % 4][:, :, :].rearrange("p m t -> p (m t)")
                nc.vector.tensor_tensor_scan(wf, dA[q % 4][:, :, :].rearrange("p m t -> p (m t)"), wf, 0.0,
                                             ALU.mult, ALU.add).then_inc(h_ok.sem, 1)

            def add_du(half):
                def step(b, par):
                    dve.wait_ge(acc_ok.sem, acc_ok.at(b, UNITS - 1 + half))
                    for m in (2 * half, 2 * half + 1):
                        nc.vector.scalar_tensor_tensor(su[par][:, MD + m, :], su[par][:, MD + m, :], vecs[:, 2, m:m + 1],
                                                       yacc[:, m, :], ALU.mult, ALU.add).then_inc(yd_ok.sem, 1)
                return step

            def gated(b, par):
                dve.wait_ge(yd_ok.sem, yd_ok.at(b))
                nc.vector.tensor_tensor(su[par][:, MD:, :], su[par][:, MD:, :], su[par][:, 0:MD, :], ALU.mult).then_inc(z_ok.sem, 1)

            def norm(b, src, stats, mean, s_ok, m_ok):
                for j in range(JT):
                    nc.vector.bn_stats(stats[:, j, :], src[:, j, :]).then_inc(s_ok.sem, 1)
                dve.wait_ge(s_ok.sem, s_ok.at(b))
                moments(nc, dve, m_ok.at(b, 0), mean, stats, JT, m_ok)

            def norm_x(b, par):
                dve.wait_ge(x_in.sem, x_in.at(b))
                norm(b, x, st, mom, ln_st, ln_mv)

            def scaled_x(b, par):
                dve.wait_ge(ln_rs.sem, ln_rs.at(b))
                for j in range(JT):
                    nc.vector.tensor_scalar(x[:, j, :], x[:, j, :], mom[:, 0, j:j + 1], rstd[:, j:j + 1],
                                            ALU.subtract, ALU.mult).then_inc(xn_ok.sem, 1)

            def dt_out(half):
                def step(b, par):
                    for m in (2 * half, 2 * half + 1):
                        dve.wait_ge(mm["dt"].sem, mm["dt"].at(b, m + 1))
                        nc.vector.tensor_scalar(delta[par][:, m, :], bank["dt", m][:, :], vecs[:, 1, m:m + 1], 20.0,
                                                ALU.add, ALU.min).then_inc(ev["dt"].sem, 1)
                return step

            def clip(b, par):
                dve.wait_ge(sp_ln.sem, sp_ln.at(b))
                nc.vector.tensor_scalar(delta[par][:, :, :], delta[par][:, :, :], DT_MIN, DT_MAX,
                                        ALU.max, ALU.min).then_inc(clipped.sem, 1)

            def times_u(b, par):
                dve.wait_ge(clipped.sem, clipped.at(b))
                nc.vector.tensor_tensor(du[par][:, :, :], delta[par][:, :, :], su[par][:, MD:, :], ALU.mult).then_inc(du_ok.sem, 1)

            def residual(g):
                def step(b, par):
                    if g == 0:
                        dve.wait_ge(rep_in.sem, rep_in.at(b))
                        dve.wait_ge(res_in.sem, res_in.at(b))
                        if before(b):
                            dve.wait_ge(x1_out.sem, x1_out.at(b - 1))
                    dve.wait_ge(t_mm.sem, t_mm.at(b, g + 1))
                    nc.vector.tensor_tensor(x1[:, 2 * g:2 * g + 2, :], tb[g][:, :].rearrange("p (j d) -> p j d", j=2),
                                            rep[:, 0:1, :].to_broadcast([P, 2, D]), ALU.mult).then_inc(o_ok.sem, 1)
                    if g == 1:
                        dve.wait_ge(o_ok.sem, o_ok.at(b))
                        nc.vector.tensor_tensor(x1[:, :, :], x1[:, :, :], xres[:, :, :], ALU.add).then_inc(x1_ok.sem, 1)
                return step

            def norm_x1(b, par):
                dve.wait_ge(x1_ok.sem, x1_ok.at(b))
                norm(b, x1, st2, mom2, st2_ok, mv2_ok)

            def scaled_x1(b, par):
                dve.wait_ge(rs2_ok.sem, rs2_ok.at(b))
                if before(b):
                    dve.wait_ge(h2_out.sem, h2_out.at(b - 1))
                for j in range(JT):
                    nc.vector.tensor_scalar(h2[:, j, :], x1[:, j, :], mom2[:, 0, j:j + 1], rstd2[:, j:j + 1],
                                            ALU.subtract, ALU.mult).then_inc(xn2_ok.sem, 1)

            def logits(b, par):
                dve.wait_ge(t_mm.sem, t_mm.at(b))
                dst = keep["logits"][:, b * JT:(b + 1) * JT, :] if isinstance(b, int) else keep["logits"][:, bass.ds(b * JT, JT), :]
                nc.vector.tensor_scalar(dst, tb[0][:, 0:JT * E].rearrange("p (j e) -> p j e", j=JT), 1.0, None,
                                        ALU.mult).then_inc(lg_ok.sem, 1)

            periods(dve, [(4, norm_x), (9, scaled_x), (52, dt_out(0)), (54, dt_out(1)), (58, clip), (59, times_u),
                          (98, add_du(0)), (99, add_du(1)), (99, gated), (107, residual(0)), (109, residual(1)),
                          (111, norm_x1), (116, scaled_x1), (127, logits)], unit)

        @block.gpsimd
        def _(pool):
            def unit(b, q, par):
                n = q // 2
                if q % 4 == 0:
                    pool.wait_ge(bc_in[(q // 4) % 2].sem, b * (64 * NS // 4) + 64 * (q // 8 + 1))
                pool.wait_ge(h_ok.sem, h_ok.at(b, q + 1))
                cn = bc[(q // 4) % 2][:, n % 2, 1:2, :].to_broadcast([P, 2, L])
                nc.gpsimd.tensor_tensor(w[q % 4][:, :, :], w[q % 4][:, :, :], cn, ALU.mult).then_inc(hc_ok.sem, 1)

            def scale_h2(b, par):
                pool.wait_ge(xn2_ok.sem, xn2_ok.at(b))
                nc.gpsimd.tensor_tensor(h2[:, :, :], h2[:, :, :], rep[:, 2:3, :].to_broadcast([P, JT, D]), ALU.mult).then_inc(sc2_ok.sem, 1)

            def shift_h2(b, par):
                pool.wait_ge(sc2_ok.sem, sc2_ok.at(b))
                nc.gpsimd.tensor_tensor(h2[:, :, :], h2[:, :, :], rep[:, 1:2, :].to_broadcast([P, JT, D]), ALU.add).then_inc(h2_ok.sem, 1)

            periods(pool, [(115, scale_h2), (117, shift_h2)], unit)

        @block.tensor
        def _(pe):
            pe.wait_ge(weights.sem, 8 * 16)
            pe.wait_ge(ready.sem, 5)

            def unit(b, q, par):
                m0 = 2 * (q % 2)
                if q < 2 and before(b):
                    pe.wait_ge(yd_ok.sem, yd_ok.at(b - 1, 2 * (q + 1)))
                pe.wait_ge(hc_ok.sem, hc_ok.at(b, q + 1))
                for m in range(2):
                    ins = nc.tensor.matmul(yacc[:, m0 + m, :], ident[:, :], w[q % 4][:, m, :],
                                           start=(q < 2), stop=(q >= UNITS - 2))
                ins.then_inc(acc_ok.sem, 1)

            def free(b, kind, i):
                n = [job[1:] for job in ring].index((kind, i))
                p = b + ring[n][0] // UNITS
                while not isinstance(p, int) or p >= 0:
                    n -= 2
                    if n < 0:
                        n, p = n + len(ring), p - 1
                    place, kind, i = ring[n]
                    older = p - place // UNITS
                    if not isinstance(p, int) or 0 <= older < B:
                        pe.wait_ge(ev[kind].sem, ev[kind].at(older, i + 1))
                        return

            def turn(b, par):
                pe.wait_ge(xn_ok.sem, xn_ok.at(b))
                for dh in range(KD):
                    free(b, "turn", dh)
                    for j in range(JT):
                        ins = nc.tensor.transpose(bank["turn", dh][:, j * P:(j + 1) * P], x[:, j, dh * P:(dh + 1) * P], ident[:, :])
                    ins.then_inc(mm["turn"].sem, 1)

            def product(kind, i, pairs, part=0, parts=1, rows=P, need=None):
                def step(b, par):
                    if part == 0:
                        if need is not None:
                            need(b)
                        free(b, kind, i)
                    todo = pairs(par)
                    size = len(todo) // parts
                    for n in range(part * size, (part + 1) * size):
                        ins = nc.tensor.matmul(bank[kind, i][0:rows, :], todo[n][0], todo[n][1], start=(n == 0), stop=(n == len(todo) - 1))
                    if part == parts - 1:
                        ins.then_inc(mm[kind].sem, 1)
                return step

            events = [(10, turn)]
            for place, kind, i in front_mm:
                if kind == "in":
                    events.append((place, product("in", i, lambda par, m=i: [(w_in[:, k, m * P:(m + 1) * P], hT[:, k, :]) for k in range(KD)],
                                                  need=lambda b: pe.wait_ge(ev["turn"].sem, ev["turn"].at(b)))))
                if kind == "conv":
                    at = [place + s for s in ((0, 1, 2, 3) if i < MD - 1 else (0, 1, 3, 5))]
                    for tap in range(TAPS):
                        events.append((at[tap], product("conv", i, lambda par, m=i: [(w_conv[:, t, k, m * P:(m + 1) * P], xs[:, 2 * (m // 2) + k, t:t + L])
                                                                                    for t in range(TAPS) for k in range(2)], tap, TAPS,
                                                        need=lambda b, m=i: pe.wait_ge(ev["in"].sem, ev["in"].at(b, 2 * (m // 2) + 2)))))
                if kind == "xb":
                    rows, cut = ((DR, slice(0, DR)), (2 * NS, slice(DR, DR + 2 * NS)))[i]
                    events.append((place, product("xb", i, lambda par, cut=cut: [(w_x[:, k, cut], su[par][:, MD + k, :]) for k in range(MD)], rows=rows,
                                                  need=lambda b: pe.wait_ge(silued.sem, silued.at(b, 1)))))
                if kind == "dt":
                    events.append((place, product("dt", i, lambda par, m=i: [(w_dt[:, m * P:(m + 1) * P], dtT[:, :])],
                                                  need=lambda b: pe.wait_ge(ev["xb"].sem, ev["xb"].at(b, 1)))))

            def out(j):
                def step(b, par):
                    g = j // 2
                    if j == 0:
                        pe.wait_ge(z_ok.sem, z_ok.at(b))
                    if j == 0 and before(b):
                        pe.wait_ge(lg_ok.sem, lg_ok.at(b - 1))
                    if j == 2 and before(b):
                        pe.wait_ge(hT2_ok.sem, hT2_ok.at(b - 1))
                    for k in range(MD):
                        ins = nc.tensor.matmul(tb[g][:, (j % 2) * D:(j % 2 + 1) * D], su[par][:, MD + k, j * P:(j + 1) * P],
                                               w_out[:, k, :], start=(k == 0), stop=(k == MD - 1))
                    if j % 2:
                        ins.then_inc(t_mm.sem, 1)
                return step

            def turn2(b, par):
                pe.wait_ge(h2_ok.sem, h2_ok.at(b))
                for dh in range(KD):
                    pe.wait_ge(o_ok.sem, o_ok.at(b, dh + 1))
                    for j in range(JT):
                        ins = nc.tensor.transpose(tb[dh][:, j * P:(j + 1) * P], h2[:, j, dh * P:(dh + 1) * P], ident[:, :])
                    ins.then_inc(t_mm.sem, 1)

            def logits(b, par):
                pe.wait_ge(hT2_ok.sem, hT2_ok.at(b))
                for j in range(JT):
                    for dh in range(KD):
                        ins = nc.tensor.matmul(tb[0][:, j * E:(j + 1) * E], hT2[:, dh, j * P:(j + 1) * P], w_gate[:, dh, :],
                                               start=(dh == 0), stop=(dh == KD - 1))
                ins.then_inc(t_mm.sem, 1)

            periods(pe, events + [(100, out(0)), (102, out(1)), (104, out(2)), (105, out(3)), (120, turn2), (123, logits)], unit)


def route(nc, io, keep, ly):
    with ExitStack() as ctx:
        r = Room(nc, ctx, f"rt{ly}", keep)
        lg, iota = keep["logits"], keep["iota"]
        rows = r.sb("rows", [P, NT, D])
        lg2 = r.sb("lg2", [P, NT, E])
        top = [r.sb(f"top{k}", [P, NT]) for k in range(K)]
        sc = r.sb("sc", [P, NT, E])
        best = r.sb("best", [P, NT])
        hot = r.sb("hot", [P, E, K, NT])
        ex = r.sb("ex", [P, NT, E])
        d2 = r.sb("d2", [P, NT])
        ssum = r.sb("ssum", [P, NT])
        seg = r.sb("seg", [P, E, K * NT])
        tot = r.sb("tot", [P, E, K * NT])
        inc = r.sb("inc", [P, E, K * NT])
        rank = r.sb("rank", [P, E, K * NT])
        cnt = r.sb("cnt", [P, E])
        cmp = r.sb("cmp", [P, E, MAXT])
        nt = r.sb("nt", [P, E])
        end = r.sb("end", [P, E])
        base = r.sb("base", [P, E])
        own = r.sb("own", [P, NTILES, E])
        ownf = r.sb("ownf", [P, NTILES])
        rk = r.sb("rk", [P, K * NT])
        slot = r.sb("slot", [P, K * NT])
        inside = r.sb("inside", [P, K * NT])
        put = r.sb("put", [P, K * NT])
        pre_p, tot_p = r.ps("pre_p", [P, E * K * NT]), r.ps("tot_p", [P, E * K * NT])
        step, hot_ok, counted, diff_ok, exp_ok, put_ok = (r.sig(n) for n in ("step", "hot_ok", "counted", "diff_ok", "exp_ok", "put_ok"))
        rows_in = [r.sig(f"rows_in{g}", 16) for g in range(4)]
        placed = r.sig("placed", 16)
        block = ctx.enter_context(nc.Block())
        grp = NT // 4

        @block.sync
        def _(sp):
            src = io[f"h{ly}"].rearrange("(j p) d -> p j d", p=P)
            for g in range(4):
                sp.dma_start(rows[:, g * grp:(g + 1) * grp, :], src[:, g * grp:(g + 1) * grp, :]).then_inc(rows_in[g].sem, 16)

        @block.gpsimd
        def _(pool):
            pool.wait_ge(put_ok.sem, 1)
            for j in range(NT):
                if j % grp == 0:
                    pool.wait_ge(rows_in[j // grp].sem, 16)
                for k in range(K):
                    c = k * NT + j
                    pool.indirect_dma_start(io[f"xbuf{ly}"], bass.IndirectOffsetOnAxis(ap=keep["put"][:, c:c + 1], axis=0),
                                            rows[:, j, :], None).then_inc(placed.sem, 16)
            pool.wait_ge(placed.sem, 16 * K * NT)

        @block.tensor
        def _(pe):
            pe.wait_ge(hot_ok.sem, K)
            hf = hot[:, :, :, :].rearrange("p e k j -> p (e k j)")
            nc.tensor.matmul(pre_p[:, :], keep["below"][:, :], hf, start=True, stop=True)
            nc.tensor.matmul(tot_p[:, :], keep["ones"][:, :], hf, start=True, stop=True).then_inc(counted.sem, 1)

        @block.scalar
        def _(act):
            act.wait_ge(diff_ok.sem, 2)
            nc.scalar.activation(ex[:, :, :], ex[:, :, :], ACT.Exp).then_inc(exp_ok.sem, 1)
            nc.scalar.activation(d2[:, :], d2[:, :], ACT.Exp).then_inc(exp_ok.sem, 1)

        @block.vector
        def _(dve):
            done = [0]

            def link(ins):
                done[0] += 1
                ins.then_inc(step.sem, 1)
                dve.wait_ge(step.sem, done[0])

            V = nc.vector

            def wide(ap, n=E):
                return ap.unsqueeze(2).to_broadcast([P, ap.shape[1], n])

            falling = iota[:, 0:E].unsqueeze(1).to_broadcast([P, NT, E])
            for k in range(K):
                cur = lg if k == 0 else lg2
                link(V.tensor_reduce(top[k][:, :], cur[:, :, :], AX.X, ALU.max))
                link(V.tensor_tensor(sc[:, :, :], cur[:, :, :], wide(top[k][:, :]), ALU.is_equal))
                link(V.tensor_tensor(sc[:, :, :], sc[:, :, :], falling, ALU.mult))
                link(V.tensor_reduce(best[:, :], sc[:, :, :], AX.X, ALU.max))
                link(V.tensor_tensor(sc[:, :, :], sc[:, :, :], wide(best[:, :]), ALU.is_equal))
                V.tensor_copy(hot[:, :, k, :], sc[:, :, :].rearrange("p j e -> p e j")).then_inc(hot_ok.sem, 1)
                if k == 0:
                    link(V.scalar_tensor_tensor(lg2[:, :, :], sc[:, :, :], -3e38, lg[:, :, :], ALU.mult, ALU.add))
            V.tensor_tensor(ex[:, :, :], lg[:, :, :], wide(top[0][:, :]), ALU.subtract).then_inc(diff_ok.sem, 1)
            V.tensor_tensor(d2[:, :], top[1][:, :], top[0][:, :], ALU.subtract).then_inc(diff_ok.sem, 1)
            link(V.memset(seg[:, :, :], 1.0))
            link(V.memset(seg[:, :, 0:1], 0.0))
            dve.wait_ge(exp_ok.sem, 2)
            link(V.tensor_reduce(ssum[:, :], ex[:, :, :], AX.X, ALU.add))
            w0, w1 = keep["wts"][:, 0:NT], keep["wts"][:, NT:]
            link(V.reciprocal(w0, ssum[:, :]))
            link(V.tensor_tensor(w1, d2[:, :], w0, ALU.mult))
            if ly == 1:
                link(V.tensor_tensor(ssum[:, :], w0, w1, ALU.add))
                link(V.reciprocal(ssum[:, :], ssum[:, :]))
                link(V.tensor_tensor(w0, w0, ssum[:, :], ALU.mult))
                link(V.tensor_tensor(w1, w1, ssum[:, :], ALU.mult))
            dve.wait_ge(counted.sem, 1)
            flat = "p e c -> p (e c)"
            link(V.tensor_copy(tot[:, :, :].rearrange(flat), tot_p[:, :]))
            link(V.tensor_tensor_scan(inc[:, :, :].rearrange(flat), seg[:, :, :].rearrange(flat),
                                      tot[:, :, :].rearrange(flat), 0.0, ALU.mult, ALU.add))
            link(V.tensor_tensor(tot[:, :, :], inc[:, :, :], tot[:, :, :], ALU.subtract))
            link(V.tensor_tensor(rank[:, :, :].rearrange(flat), pre_p[:, :], tot[:, :, :].rearrange(flat), ALU.add))
            cap = float(CAP if ly == 0 else T)
            link(V.tensor_scalar(cnt[:, :], inc[:, :, K * NT - 1], cap, None, ALU.min))
            link(V.tensor_tensor(cmp[:, :, :], wide(cnt[:, :], MAXT), iota[:, E:E + MAXT].unsqueeze(1).to_broadcast([P, E, MAXT]), ALU.is_gt))
            link(V.tensor_reduce(nt[:, :], cmp[:, :, :], AX.X, ALU.add))
            link(V.memset(base[:, :], 1.0))
            link(V.tensor_tensor_scan(end[:, :], base[:, :], nt[:, :], 0.0, ALU.mult, ALU.add))
            link(V.tensor_tensor(base[:, :], end[:, :], nt[:, :], ALU.subtract))
            link(V.tensor_scalar(base[:, :], base[:, :], float(TS), None, ALU.mult))
            tiles = iota[:, 24:24 + NTILES].unsqueeze(2).to_broadcast([P, NTILES, E])
            link(V.tensor_tensor(own[:, :, :], end[:, :].unsqueeze(1).to_broadcast([P, NTILES, E]), tiles, ALU.is_le))
            link(V.tensor_reduce(ownf[:, :], own[:, :, :], AX.X, ALU.add))
            link(V.tensor_scalar(keep["owner"][:, :], ownf[:, :], float(E - 1), None, ALU.min))
            hotc = hot[:, :, :, :].rearrange("p e k j -> p e (k j)")
            link(V.tensor_tensor(tot[:, :, :], rank[:, :, :], hotc, ALU.mult))
            link(V.tensor_reduce(rk[:, :], tot[:, :, :].rearrange("p e c -> p c e"), AX.X, ALU.add))
            link(V.tensor_tensor(tot[:, :, :], hotc, wide(base[:, :], K * NT), ALU.mult))
            link(V.tensor_reduce(slot[:, :], tot[:, :, :].rearrange("p e c -> p c e"), AX.X, ALU.add))
            link(V.tensor_tensor(slot[:, :], slot[:, :], rk[:, :], ALU.add))
            link(V.tensor_scalar(inside[:, :], rk[:, :], cap, None, ALU.is_lt))
            link(V.tensor_tensor(slot[:, :], slot[:, :], inside[:, :], ALU.mult))
            link(V.tensor_tensor(keep["wts"][:, :], keep["wts"][:, :], inside[:, :], ALU.mult))
            link(V.tensor_copy(keep["get"][:, :], slot[:, :]))
            link(V.tensor_scalar(inside[:, :], inside[:, :], -1.0, 1.0, ALU.mult, ALU.add))
            link(V.tensor_tensor(put[:, :], inside[:, :], iota[:, 64:64 + K * NT], ALU.mult))
            V.tensor_tensor(keep["put"][:, :], put[:, :], slot[:, :], ALU.add).then_inc(put_ok.sem, 1)


def experts(nc, io, keep, ly):
    with ExitStack() as ctx:
        r = Room(nc, ctx, f"ex{ly}", keep)
        ident = keep["ident"]
        SB = TS // P
        HI, LO = 0, 1
        w1 = [r.sb(f"w1_{i}", [P, KD, H]) for i in range(2)]
        w2 = [r.sb(f"w2_{i}", [P, MH, D]) for i in range(2)]
        w1s = [r.sb(f"w1s_{i}", [P, 2, KD, H], F32R) for i in range(2)]
        w2s = [r.sb(f"w2s_{i}", [P, 2, MH, D], F32R) for i in range(2)]
        b1 = [r.sb(f"b1_{i}", [P, MH]) for i in range(2)]
        b2 = [r.sb(f"b2_{i}", [P, D]) for i in range(2)]
        xin = [r.sb(f"xin{i}", [P, SB, D]) for i in range(2)]
        xTs = [r.sb(f"xTs{i}", [P, 2, KD, TS], F32R) for i in range(2)]
        hid = [r.sb(f"hid{i}", [P, MH, TS]) for i in range(2)]
        hids = [r.sb(f"hids{i}", [P, 2, MH, TS], F32R) for i in range(2)]
        y = [r.sb(f"y{i}", [P, SB, D]) for i in range(2)]
        tp = [r.ps(f"tp{i}", [P, KD, TS]) for i in range(2)]
        hp = [r.ps(f"hp{i}", [P, 2, TS]) for i in range(4)]
        yp = [r.ps(f"yp{i}", [P, SB, D]) for i in range(2)]
        w1_in, w2_in = [r.sig(f"w1_in{i}", 32) for i in range(2)], [r.sig(f"w2_in{i}", 16) for i in range(2)]
        b2_in = [r.sig(f"b2_in{i}", 16) for i in range(2)]
        x_in = [r.sig(f"x_in{i}", 16) for i in range(2)]
        w1_hi, w1_lo, w2_hi, w2_lo = r.sig("w1_hi"), r.sig("w1_lo"), r.sig("w2_hi"), r.sig("w2_lo")
        turned, x_hi, x_lo = r.sig("turned"), r.sig("x_hi"), r.sig("x_lo")
        h_mm, h_ok, h_hi, h_lo = (r.sig(n, MH // 2) for n in ("h_mm", "h_ok", "h_hi", "h_lo"))
        y_mm, y_ok = r.sig("y_mm"), [r.sig(f"y_ok{i}") for i in range(2)]
        y_out = [r.sig(f"y_out{i}", 16) for i in range(2)]
        block = ctx.enter_context(nc.Block())
        W1, W2, B1, B2 = (io[f"{n}_{ly}"] for n in ("w1", "w2", "b1", "b2"))
        xbuf = io[f"xbuf{ly}"][0:SLOTS, :].rearrange("(t s p) d -> t p s d", s=SB, p=P)
        ybuf = io[f"ybuf{ly}"].rearrange("(t s p) d -> t p s d", s=SB, p=P)

        def one(ap, t):
            return ap[t] if isinstance(t, int) else ap[bass.ds(t, 1)].rearrange("o p s d -> (o p) s d")

        def tiles(eng, body):
            for t in range(3):
                body(t, t % 2, t // 2)
            with eng.Fori(1, (NTILES - 2) // 2) as i:
                body(i * 2 + 1, 1, i)
                body(i * 2 + 2, 0, i + 1)
            for t in range(1 + 2 * ((NTILES - 2) // 2), NTILES):
                body(t, t % 2, t // 2)

        def first(t):
            return isinstance(t, int) and t == 0

        def old(t):
            return not isinstance(t, int) or t >= 2

        def final(t):
            return isinstance(t, int) and t == NTILES - 1

        @block.sync
        def _(sp):
            def body(t, par, rd):
                idx = keep["owner"][0:1, t:t + 1] if isinstance(t, int) else keep["owner"][0:1, bass.ds(t, 1)]
                e = sp.value_load(idx, min_val=0, max_val=E - 1)
                if old(t):
                    sp.wait_ge(turned.sem, turned.at(t - 2))
                sp.dma_start(xin[par][:, :, :], one(xbuf, t)).then_inc(x_in[par].sem, 16)
                if old(t):
                    sp.wait_ge(w1_lo.sem, w1_lo.at(t - 2))
                sp.dma_start(w1[par][:, :, :], W1[bass.ds(e, 1)].rearrange("o (k p) h -> (o p) k h", p=P)).then_inc(w1_in[par].sem, 16)
                if old(t):
                    sp.wait_ge(h_ok.sem, h_ok.at(t - 2))
                sp.dma_start(b1[par][:, :], B1[bass.ds(e, 1)].rearrange("o p m -> (o p) m")).then_inc(w1_in[par].sem, 16)
                if old(t):
                    sp.wait_ge(w2_lo.sem, w2_lo.at(t - 2))
                sp.dma_start(w2[par][:, :, :], W2[bass.ds(e, 1)].rearrange("o (m p) d -> (o p) m d", p=P)).then_inc(w2_in[par].sem, 16)
                if not first(t):
                    load_b2(t - 1, 1 - par, rd - 1 + par)

            def load_b2(t, par, rd):
                idx = keep["owner"][0:1, t:t + 1] if isinstance(t, int) else keep["owner"][0:1, bass.ds(t, 1)]
                e = sp.value_load(idx, min_val=0, max_val=E - 1)
                if old(t):
                    sp.wait_ge(y_ok[par].sem, rd)
                sp.dma_start(b2[par][:, :], B2[bass.ds(e, 1), :].to_broadcast([P, D])).then_inc(b2_in[par].sem, 16)

            tiles(sp, body)
            load_b2(NTILES - 1, (NTILES - 1) % 2, (NTILES - 1) // 2)

        @block.gpsimd
        def _(pool):
            def body(t, par, rd):
                pool.wait_ge(y_ok[par].sem, y_ok[par].at(rd))
                pool.dma_start(one(ybuf, t), y[par][:, :, :]).then_inc(y_out[par].sem, 16)

            tiles(pool, body)
            pool.wait_ge(y_out[0].sem, 16 * ((NTILES + 1) // 2))
            pool.wait_ge(y_out[1].sem, 16 * (NTILES // 2))

        @block.scalar
        def _(act):
            def hi_w1(t, par, rd):
                if old(t):
                    act.wait_ge(h_mm.sem, h_mm.at(t - 2))
                act.wait_ge(w1_in[par].sem, w1_in[par].at(rd))
                nc.scalar.activation(w1s[par][:, HI], w1[par][:, :, :], ACT.Copy).then_inc(w1_hi.sem, 1)

            def hi_w2(t, par, rd):
                act.wait_ge(w2_in[par].sem, w2_in[par].at(rd))
                nc.scalar.activation(w2s[par][:, HI], w2[par][:, :, :], ACT.Copy).then_inc(w2_hi.sem, 1)

            def hi_x(t, par):
                if old(t):
                    act.wait_ge(h_mm.sem, h_mm.at(t - 2))
                act.wait_ge(turned.sem, turned.at(t))
                nc.scalar.activation(xTs[par][:, HI], tp[par][:, :, :], ACT.Copy).then_inc(x_hi.sem, 1)

            def body(t, par, rd):
                if first(t):
                    hi_w1(0, 0, 0)
                    hi_x(0, 0)
                if old(t):
                    act.wait_ge(h_lo.sem, h_lo.at(t - 2))
                for i in range(MH // 2):
                    act.wait_ge(h_mm.sem, h_mm.at(t, i + 1))
                    for m in range(2):
                        ins = nc.scalar.activation(hid[par][:, 2 * i + m, :], hp[i][:, m, :], ACT.Gelu,
                                                   bias=b1[par][:, 2 * i + m:2 * i + m + 1])
                    ins.then_inc(h_ok.sem, 1)
                    if i == 0 and old(t):
                        act.wait_ge(y_mm.sem, y_mm.at(t - 2))
                    act.wait_ge(h_ok.sem, h_ok.at(t, i + 1))
                    nc.scalar.activation(hids[par][:, HI, 2 * i:2 * i + 2, :], hid[par][:, 2 * i:2 * i + 2, :], ACT.Copy).then_inc(h_hi.sem, 1)
                    if i == 0 and not final(t):
                        hi_w1(t + 1, 1 - par, rd + par)
                if not final(t):
                    hi_x(t + 1, 1 - par)
                hi_w2(t, par, rd)

            tiles(act, body)

        @block.vector
        def _(dve):
            V = nc.vector

            def lo_w1(t, par):
                dve.wait_ge(w1_hi.sem, w1_hi.at(t))
                V.tensor_tensor(w1s[par][:, LO], w1[par][:, :, :], w1s[par][:, HI].bitcast(F32), ALU.subtract).then_inc(w1_lo.sem, 1)

            def lo_w2(t, par):
                dve.wait_ge(w2_hi.sem, w2_hi.at(t))
                V.tensor_tensor(w2s[par][:, LO], w2[par][:, :, :], w2s[par][:, HI].bitcast(F32), ALU.subtract).then_inc(w2_lo.sem, 1)

            def lo_x(t, par):
                dve.wait_ge(x_hi.sem, x_hi.at(t))
                V.tensor_tensor(xTs[par][:, LO], tp[par][:, :, :], xTs[par][:, HI].bitcast(F32), ALU.subtract).then_inc(x_lo.sem, 1)

            def out(t, par, rd):
                dve.wait_ge(b2_in[par].sem, b2_in[par].at(rd))
                if old(t):
                    dve.wait_ge(y_out[par].sem, y_out[par].per * rd)
                dve.wait_ge(y_mm.sem, y_mm.at(t))
                V.tensor_tensor(y[par][:, :, :], yp[par][:, :, :], b2[par][:, :].unsqueeze(1).to_broadcast([P, SB, D]),
                                ALU.add).then_inc(y_ok[par].sem, 1)

            def body(t, par, rd):
                if first(t):
                    lo_w1(0, 0)
                    lo_x(0, 0)
                for i in range(MH // 2):
                    dve.wait_ge(h_hi.sem, h_hi.at(t, i + 1))
                    V.tensor_tensor(hids[par][:, LO, 2 * i:2 * i + 2, :], hid[par][:, 2 * i:2 * i + 2, :],
                                    hids[par][:, HI, 2 * i:2 * i + 2, :].bitcast(F32), ALU.subtract).then_inc(h_lo.sem, 1)
                    if i == 0 and not final(t):
                        lo_w1(t + 1, 1 - par)
                if not final(t):
                    lo_x(t + 1, 1 - par)
                lo_w2(t, par)
                if not first(t):
                    out(t - 1, 1 - par, rd - 1 + par)

            tiles(dve, body)
            out(NTILES - 1, (NTILES - 1) % 2, (NTILES - 1) // 2)

        @block.tensor
        def _(pe):
            def product(out, terms):
                n = 0
                for a, b in terms:
                    for i, j in ((HI, HI), (HI, LO), (LO, HI)):
                        mm = nc.tensor.matmul(out, a(i), b(j), start=(n == 0), stop=(n == 3 * len(terms) - 1))
                        n += 1
                return mm

            def turn(t, par, rd):
                pe.wait_ge(x_in[par].sem, x_in[par].at(rd))
                if old(t):
                    pe.wait_ge(x_lo.sem, x_lo.at(t - 2))
                for s in range(SB):
                    for k in range(KD):
                        mm = nc.tensor.transpose(tp[par][:, k, s * P:(s + 1) * P], xin[par][:, s, k * P:(k + 1) * P], ident[:, :])
                mm.then_inc(turned.sem, 1)

            def up(t, par, rd):
                pe.wait_ge(w1_lo.sem, w1_lo.at(t))
                pe.wait_ge(x_lo.sem, x_lo.at(t))
                for i in range(MH // 2):
                    if not first(t):
                        pe.wait_ge(h_ok.sem, h_ok.at(t - 1, i + 1))
                    for m in (2 * i, 2 * i + 1):
                        mm = product(hp[i][:, m % 2, :], [(lambda s, k=k: w1s[par][:, s, k, m * P:(m + 1) * P],
                                                           lambda s, k=k: xTs[par][:, s, k, :]) for k in range(KD)])
                    mm.then_inc(h_mm.sem, 1)

            def down(t, par, rd):
                pe.wait_ge(w2_lo.sem, w2_lo.at(t))
                if old(t):
                    pe.wait_ge(y_ok[par].sem, rd)
                pe.wait_ge(h_lo.sem, h_lo.at(t))
                for s in range(SB):
                    mm = product(yp[par][:, s, :], [(lambda i, m=m: hids[par][:, i, m, s * P:(s + 1) * P],
                                                     lambda i, m=m: w2s[par][:, i, m, :]) for m in range(MH)])
                mm.then_inc(y_mm.sem, 1)

            def body(t, par, rd):
                if first(t):
                    turn(0, 0, 0)
                up(t, par, rd)
                if not final(t):
                    turn(t + 1, 1 - par, rd + par)
                if not first(t):
                    down(t - 1, 1 - par, rd - 1 + par)

            tiles(pe, body)
            down(NTILES - 1, (NTILES - 1) % 2, (NTILES - 1) // 2)


def gather(nc, io, keep, ly, pool, dst, got, free, order):
    for n, j in enumerate(order):
        for k in range(K):
            buf = n % len(dst[k])
            if n >= len(dst[k]):
                pool.wait_ge(free.sem, n - len(dst[k]) + 1)
            c = k * NT + j
            pool.indirect_dma_start(dst[k][buf][:, :], None, io[f"ybuf{ly}"],
                                    bass.IndirectOffsetOnAxis(ap=keep["get"][:, c:c + 1], axis=0)).then_inc(got[buf].sem, 16)


def mixer(nc, io, keep):
    with ExitStack() as ctx:
        r = Room(nc, ctx, "mix", keep)
        ident = keep["ident"]
        NST = SQ // P
        W3 = 3 * D
        w_qkv = r.sb("w_qkv", [P, KD, W3])
        w_o = r.sb("w_o", [P, KD, D])
        w_gate = r.sb("w_gate", [P, KD, E])
        b_qkv = r.sb("b_qkv", [P, W3])
        b_o = r.sb("b_o", [P, D])
        gb0 = r.sb("gb0", [P, TQ, D])
        rep = r.sb("rep", [P, TQ, 3, D])
        eps = r.sb("eps", [P, 1])
        yk = [[r.sb(f"y{k}_{i}", [P, D]) for i in range(4)] for k in range(K)]
        x = r.sb("x", [P, TQ, D])
        st, mom, rstd = r.sb("st", [P, TQ, 6]), r.sb("mom", [P, 3, TQ]), r.sb("rstd", [P, TQ])
        xn = r.sb("xn", [P, TQ, D])
        hT = r.sb("hT", [P, KD, TQ, P])
        qkv = r.sb("qkv", [P, TQ, W3])
        mean = r.sb("mean", [P, 2, D])
        rs = r.sb("rs", [P, 2, D])
        corr = r.sb("corr", [P, HEADS, HD, HD])
        rz = r.sb("rz", [P, HEADS, HD])
        prod = [r.sb(f"prod{i}", [P, TQ * D]) for i in range(4)]
        att = r.sb("att", [P, TQ, D])
        bank = r.ps("bank", [P, 8, 512])
        NPC, NPA = 2 * TQ, HD
        NPR = NPC + NPA
        weights, ready = r.sig("weights"), r.sig("ready")
        x_in, got, used = r.sig("x_in", 16), [r.sig(f"got{i}", 16 * K) for i in range(4)], r.sig("used", TQ)
        yw, ysum, x2_ok = r.sig("yw", TQ), r.sig("ysum"), r.sig("x2_ok")
        stats, means, rstds, norms = r.sig("stats", 2 * TQ), r.sig("means", 12), r.sig("rstds", 4), r.sig("norms", 2 * TQ)
        turned, hT_ok = r.sig("turned", 12), r.sig("hT_ok", 3)
        qkv_mm, qkv_ok = r.sig("qkv_mm", TQ), r.sig("qkv_ok", TQ)
        msum, centred, sq, sqs, unit, unit_ok = r.sig("msum"), r.sig("centred"), r.sig("sq"), r.sig("sqs"), r.sig("unit", 2), r.sig("unit_ok")
        prod_ok, acc_ok = r.sig("prod_ok", NPR), r.sig("acc_ok", NPR)
        clip_ok, exp_ok, zs_ok, rz_ok, att_ok = r.sig("clip_ok", 2), r.sig("exp_ok", 2), r.sig("zs_ok"), r.sig("rz_ok"), r.sig("att_ok")
        o_mm, o_b, o_g, x3_ok, sc_ok, h_ok, lg_mm, lg_ok = (r.sig(n) for n in ("o_mm", "o_b", "o_g", "x3_ok", "sc_ok", "h_ok", "lg_mm", "lg_ok"))
        x_out, h_out = r.sig("x_out", 16), r.sig("h_out", 16)
        block = ctx.enter_context(nc.Block())

        def seqs(name):
            return io[name].rearrange("(t s p) d -> s p t d", t=TQ, p=P)

        def one(ap, s):
            return ap[s] if isinstance(s, int) else ap[bass.ds(s, 1)].rearrange("o p t d -> (o p) t d")

        def rounds(eng, body):
            body(0, False)
            with eng.Fori(1, NST) as s:
                body(s, True)

        @block.sync
        def _(sp):
            mod = io["modrow"][1]
            for dst, src in ((w_qkv[:, :, :], io["WqkvT"]), (w_o[:, :, :], io["WoutT"]), (w_gate[:, :, :], io["gate1"]),
                             (b_qkv[:, :], io["bqkv"].to_broadcast([P, W3])), (b_o[:, :], io["bout"].to_broadcast([P, D]))):
                sp.dma_start(dst, src).then_inc(weights.sem, 16)
            for b in range(B):
                sp.dma_start(gb0[:, b, :], io["modrow"][0][b:b + 1, 3 * D:].to_broadcast([P, D])).then_inc(weights.sem, 16)
                sp.dma_start(rep[:, b, :, :].rearrange("p m d -> p (m d)"), mod[b:b + 1, 0:3 * D].to_broadcast([P, 3 * D])).then_inc(weights.sem, 16)
            def body(s, later):
                if later:
                    sp.wait_ge(x_out.sem, s * 16)
                sp.dma_start(x[:, :, :], one(seqs("x1"), s)).then_inc(x_in.sem, 16)
                sp.wait_ge(x3_ok.sem, x3_ok.at(s))
                sp.dma_start(one(seqs("x3"), s), x[:, :, :]).then_inc(x_out.sem, 16)
                sp.wait_ge(h_ok.sem, h_ok.at(s))
                sp.dma_start(one(seqs("h1"), s), xn[:, :, :]).then_inc(h_out.sem, 16)

            rounds(sp, body)
            sp.wait_ge(x_out.sem, 16 * NST)
            sp.wait_ge(h_out.sem, 16 * NST)

        @block.gpsimd
        def _(pool):
            gather(nc, io, keep, 0, pool, yk, got, used, [t * NST + s for s in range(NST) for t in range(TQ)])

        @block.scalar
        def _(act):
            act.wait_ge(ready.sem, 1)

            def norm(s, half):
                act.wait_ge(means.sem, means.at(s, 6 * (half + 1)))
                nc.scalar.activation(rstd[:, :], mom[:, 2, :], ACT.Ln, bias=eps[:, 0:1], scale=1.0 / D).then_inc(rstds.sem, 1)
                act.wait_ge(rstds.sem, rstds.at(s, 2 * half + 1))
                nc.scalar.activation(rstd[:, :], rstd[:, :], ACT.Exp, scale=-0.5).then_inc(rstds.sem, 1)

            def body(s, later):
                norm(s, 0)
                for g in range(4):
                    act.wait_ge(turned.sem, turned.at(s, g + 1))
                    for dh in range(KD):
                        for t in (2 * g, 2 * g + 1):
                            ins = nc.scalar.activation(hT[:, dh, t, :], bank[:, g, (2 * dh + t % 2) * P:(2 * dh + t % 2 + 1) * P],
                                                       ACT.Identity, scale=keep["modT"][:, 1, KD + dh, t:t + 1],
                                                       bias=keep["modT"][:, 1, dh, t:t + 1])
                ins.then_inc(hT_ok.sem, 1)
                act.wait_ge(sqs.sem, sqs.at(s))
                nc.scalar.activation(rs[:, :, :], rs[:, :, :], ACT.Ln).then_inc(unit.sem, 1)
                act.wait_ge(unit.sem, unit.at(s, 1))
                nc.scalar.activation(rs[:, :, :], rs[:, :, :], ACT.Exp, scale=-0.5).then_inc(unit.sem, 1)
                for hf in range(2):
                    act.wait_ge(clip_ok.sem, clip_ok.at(s, hf + 1))
                    c = corr[:, 8 * hf:8 * hf + 8, :, :].rearrange("p h i j -> p (h i j)")
                    nc.scalar.activation(c, c, ACT.Exp).then_inc(exp_ok.sem, 1)
                for g in range(4):
                    act.wait_ge(turned.sem, turned.at(s, 5 + g))
                    ins = nc.scalar.activation(hT[:, :, 2 * g:2 * g + 2, :], bank[:, g, :].rearrange("p (d t c) -> p d t c", d=KD, t=2), ACT.Copy)
                ins.then_inc(hT_ok.sem, 1)
                norm(s, 1)
                for g in range(4):
                    act.wait_ge(turned.sem, turned.at(s, 9 + g))
                    ins = nc.scalar.activation(hT[:, :, 2 * g:2 * g + 2, :], bank[:, g, :].rearrange("p (d t c) -> p d t c", d=KD, t=2), ACT.Copy)
                ins.then_inc(hT_ok.sem, 1)

            rounds(act, body)

        @block.vector
        def _(dve):
            V = nc.vector
            V.memset(eps[:, :], EPS).then_inc(ready.sem, 1)
            dve.wait_ge(weights.sem, 16 * (5 + 2 * B))

            def column(c):
                return keep["wts"][:, c:c + 1] if isinstance(c, int) else keep["wts"][:, bass.ds(c, 1)]

            def norm(s, half):
                for t in range(TQ):
                    V.bn_stats(st[:, t, :], x[:, t, :]).then_inc(stats.sem, 1)
                dve.wait_ge(stats.sem, stats.at(s, TQ * (half + 1)))
                moments(nc, dve, means.at(s, 6 * half), mom, st, TQ, means)
                dve.wait_ge(rstds.sem, rstds.at(s, 2 * half + 2))
                for t in range(TQ):
                    V.tensor_scalar(xn[:, t, :], x[:, t, :], mom[:, 0, t:t + 1], rstd[:, t:t + 1], ALU.subtract, ALU.mult).then_inc(norms.sem, 1)

            def body(s, later):
                if later:
                    dve.wait_ge(h_out.sem, s * 16)
                for t in range(TQ):
                    dve.wait_ge(got[t % 4].sem, got[t % 4].per * (s * 2 + t // 4 + 1))
                    wt = [column(s + (k * NT + t * NST)) for k in range(K)]
                    V.tensor_scalar(xn[:, t, :], yk[0][t % 4][:, :], wt[0], None, ALU.mult).then_inc(yw.sem, 1)
                    dve.wait_ge(yw.sem, yw.at(s, t + 1))
                    V.scalar_tensor_tensor(xn[:, t, :], yk[1][t % 4][:, :], wt[1], xn[:, t, :], ALU.mult, ALU.add).then_inc(used.sem, 1)
                dve.wait_ge(used.sem, used.at(s))
                V.tensor_tensor(xn[:, :, :], xn[:, :, :], gb0[:, :, :], ALU.mult).then_inc(ysum.sem, 1)
                dve.wait_ge(ysum.sem, ysum.at(s))
                dve.wait_ge(x_in.sem, x_in.at(s))
                V.tensor_tensor(x[:, :, :], x[:, :, :], xn[:, :, :], ALU.add).then_inc(x2_ok.sem, 1)
                dve.wait_ge(x2_ok.sem, x2_ok.at(s))
                norm(s, 0)
                for t in range(TQ):
                    dve.wait_ge(qkv_mm.sem, qkv_mm.at(s, t + 1))
                    b0 = 4 + 2 * (t % 2)
                    V.tensor_tensor(qkv[:, t, :], bank[:, b0:b0 + 2, :].rearrange("p b c -> p (b c)")[:, 0:W3], b_qkv[:, :],
                                    ALU.add).then_inc(qkv_ok.sem, 1)
                dve.wait_ge(qkv_ok.sem, qkv_ok.at(s))
                qk = qkv[:, :, 0:2 * D]
                V.tensor_reduce(mean[:, :, :].rearrange("p a d -> p (a d)"), qk.rearrange("p t c -> p c t"), AX.X, ALU.add).then_inc(msum.sem, 1)
                dve.wait_ge(msum.sem, msum.at(s))
                mb = mean[:, :, :].rearrange("p a d -> p (a d)").unsqueeze(1).to_broadcast([P, TQ, 2 * D])
                V.scalar_tensor_tensor(qk, mb, -1.0 / TQ, qk, ALU.mult, ALU.add).then_inc(centred.sem, 1)
                dve.wait_ge(centred.sem, centred.at(s))
                for g in range(2):
                    half = prod[g][:, :].rearrange("p (t c) -> p t c", t=TQ)
                    ins = V.tensor_tensor(half, qkv[:, :, g * D:(g + 1) * D], qkv[:, :, g * D:(g + 1) * D], ALU.mult)
                ins.then_inc(sq.sem, 1)
                dve.wait_ge(sq.sem, sq.at(s))
                for g in range(2):
                    ins = V.tensor_reduce(rs[:, g, :], prod[g][:, :].rearrange("p (t c) -> p c t", t=TQ), AX.X, ALU.add)
                ins.then_inc(sqs.sem, 1)
                dve.wait_ge(unit.sem, unit.at(s))
                V.tensor_tensor(qk, qk, rs[:, :, :].rearrange("p a d -> p (a d)").unsqueeze(1).to_broadcast([P, TQ, 2 * D]),
                                ALU.mult).then_inc(unit_ok.sem, 1)
                dve.wait_ge(unit_ok.sem, unit_ok.at(s))
                for hf in range(2):
                    for t in range(TQ):
                        n = TQ * hf + t
                        if n >= 4:
                            dve.wait_ge(acc_ok.sem, acc_ok.at(s, n - 3))
                        q_ = qkv[:, t, 128 * hf:128 * hf + 128].rearrange("p (h i) -> p h i", i=HD).unsqueeze(3).to_broadcast([P, 8, HD, HD])
                        k_ = qkv[:, t, D + 128 * hf:D + 128 * hf + 128].rearrange("p (h j) -> p h j", j=HD).unsqueeze(2).to_broadcast([P, 8, HD, HD])
                        V.tensor_tensor(prod[n % 4][:, :].rearrange("p (h i j) -> p h i j", h=8, i=HD), q_, k_, ALU.mult).then_inc(prod_ok.sem, 1)
                for hf in range(2):
                    dve.wait_ge(acc_ok.sem, acc_ok.at(s, TQ * (hf + 1)))
                    V.tensor_scalar(corr[:, 8 * hf:8 * hf + 8, :, :].rearrange("p h i j -> p (h i j)"),
                                    bank[:, 4 * hf:4 * hf + 4, :].rearrange("p b c -> p (b c)"), 0.0, 1.0, ALU.max, ALU.min).then_inc(clip_ok.sem, 1)
                dve.wait_ge(exp_ok.sem, exp_ok.at(s))
                V.tensor_reduce(rz[:, :, :], corr[:, :, :, :].rearrange("p h i j -> p h j i"), AX.X, ALU.add).then_inc(zs_ok.sem, 1)
                dve.wait_ge(zs_ok.sem, zs_ok.at(s))
                V.reciprocal(rz[:, :, :], rz[:, :, :]).then_inc(rz_ok.sem, 1)
                for d in range(HD):
                    n = NPC + d
                    dve.wait_ge(acc_ok.sem, acc_ok.at(s, n - 3))
                    v_ = qkv[:, :, 2 * D:].rearrange("p t (h d) -> p t h d", d=HD)[:, :, :, d:d + 1].to_broadcast([P, TQ, HEADS, HD])
                    c_ = corr[:, :, d, :].unsqueeze(1).to_broadcast([P, TQ, HEADS, HD])
                    V.tensor_tensor(prod[n % 4][:, :].rearrange("p (t h e) -> p t h e", t=TQ, h=HEADS), v_, c_, ALU.mult).then_inc(prod_ok.sem, 1)
                dve.wait_ge(acc_ok.sem, acc_ok.at(s))
                dve.wait_ge(rz_ok.sem, rz_ok.at(s))
                V.tensor_tensor(att[:, :, :], bank[:, 0:4, :].rearrange("p b (t c) -> p (b t) c", t=2),
                                rz[:, :, :].rearrange("p h e -> p (h e)").unsqueeze(1).to_broadcast([P, TQ, D]), ALU.mult).then_inc(att_ok.sem, 1)
                dve.wait_ge(o_mm.sem, o_mm.at(s))
                V.tensor_tensor(xn[:, :, :], bank[:, 4:8, :].rearrange("p b (t c) -> p (b t) c", t=2),
                                b_o[:, :].unsqueeze(1).to_broadcast([P, TQ, D]), ALU.add).then_inc(o_b.sem, 1)
                dve.wait_ge(o_b.sem, o_b.at(s))
                V.tensor_tensor(xn[:, :, :], xn[:, :, :], rep[:, :, 0, :], ALU.mult).then_inc(o_g.sem, 1)
                dve.wait_ge(o_g.sem, o_g.at(s))
                V.tensor_tensor(x[:, :, :], x[:, :, :], xn[:, :, :], ALU.add).then_inc(x3_ok.sem, 1)
                dve.wait_ge(x3_ok.sem, x3_ok.at(s))
                norm(s, 1)
                dve.wait_ge(norms.sem, norms.at(s))
                V.tensor_tensor(xn[:, :, :], xn[:, :, :], rep[:, :, 2, :], ALU.mult).then_inc(sc_ok.sem, 1)
                dve.wait_ge(sc_ok.sem, sc_ok.at(s))
                V.tensor_tensor(xn[:, :, :], xn[:, :, :], rep[:, :, 1, :], ALU.add).then_inc(h_ok.sem, 1)
                dve.wait_ge(lg_mm.sem, lg_mm.at(s))
                dst = keep["logits"][:, :, :].rearrange("p (t s) e -> p s t e", s=NST)
                dst = dst[:, s] if isinstance(s, int) else dst[:, bass.ds(s, 1)].rearrange("p o t e -> p (o t) e")
                V.tensor_scalar(dst, bank[:, 4, 0:TQ * E].rearrange("p (t e) -> p t e", t=TQ), 1.0, None, ALU.mult).then_inc(lg_ok.sem, 1)

            rounds(dve, body)

        @block.tensor
        def _(pe):
            pe.wait_ge(weights.sem, 16 * (5 + 2 * B))

            def turn(src):
                for g in range(4):
                    for dh in range(KD):
                        for t in (2 * g, 2 * g + 1):
                            mm = nc.tensor.transpose(bank[:, g, (2 * dh + t % 2) * P:(2 * dh + t % 2 + 1) * P], src[:, t, dh * P:(dh + 1) * P], ident[:, :])
                    mm.then_inc(turned.sem, 1)

            def body(s, later):
                if later:
                    pe.wait_ge(hT_ok.sem, s * 3)
                pe.wait_ge(norms.sem, norms.at(s, TQ))
                turn(xn)
                if later:
                    pe.wait_ge(lg_ok.sem, s)
                pe.wait_ge(hT_ok.sem, hT_ok.at(s, 1))
                for t in range(TQ):
                    if t >= 2:
                        pe.wait_ge(qkv_ok.sem, qkv_ok.at(s, t - 1))
                    b0 = 4 + 2 * (t % 2)
                    for c0, c1, bk in ((0, 512, b0), (512, W3, b0 + 1)):
                        for k in range(KD):
                            mm = nc.tensor.matmul(bank[:, bk, 0:c1 - c0], hT[:, k, t, :], w_qkv[:, k, c0:c1], start=(k == 0), stop=(k == KD - 1))
                    mm.then_inc(qkv_mm.sem, 1)
                for n in range(NPR):
                    pe.wait_ge(prod_ok.sem, prod_ok.at(s, n + 1))
                    if n == NPC:
                        pe.wait_ge(clip_ok.sem, clip_ok.at(s, 1))
                    b0 = 4 if TQ <= n < NPC else 0
                    a, z = (n % TQ == 0, n % TQ == TQ - 1) if n < NPC else (n == NPC, n == NPR - 1)
                    for i in range(4):
                        mm = nc.tensor.matmul(bank[:, b0 + i, :], ident[:, :], prod[n % 4][:, 512 * i:512 * (i + 1)], start=a, stop=z)
                    mm.then_inc(acc_ok.sem, 1)
                pe.wait_ge(att_ok.sem, att_ok.at(s))
                turn(att)
                pe.wait_ge(hT_ok.sem, hT_ok.at(s, 2))
                pe.wait_ge(clip_ok.sem, clip_ok.at(s, 2))
                for t in range(TQ):
                    for k in range(KD):
                        mm = nc.tensor.matmul(bank[:, 4 + t // 2, (t % 2) * D:(t % 2 + 1) * D], hT[:, k, t, :], w_o[:, k, :], start=(k == 0), stop=(k == KD - 1))
                mm.then_inc(o_mm.sem, 1)
                pe.wait_ge(h_ok.sem, h_ok.at(s))
                turn(xn)
                pe.wait_ge(hT_ok.sem, hT_ok.at(s))
                pe.wait_ge(o_b.sem, o_b.at(s))
                for t in range(TQ):
                    for k in range(KD):
                        mm = nc.tensor.matmul(bank[:, 4, t * E:(t + 1) * E], hT[:, k, t, :], w_gate[:, k, :], start=(k == 0), stop=(k == KD - 1))
                mm.then_inc(lg_mm.sem, 1)

            rounds(pe, body)


def last(nc, io, keep):
    with ExitStack() as ctx:
        r = Room(nc, ctx, "last", keep)
        gb = [r.sb(f"gb{i}", [P, D]) for i in range(2)]
        yk = [[r.sb(f"y{k}_{i}", [P, D]) for i in range(8)] for k in range(K)]
        x = [r.sb(f"x{i}", [P, JT, D]) for i in range(2)]
        acc = [r.sb(f"acc{i}", [P, JT, D]) for i in range(2)]
        x_in, out = [r.sig(f"x_in{i}", 32) for i in range(2)], [r.sig(f"out{i}", 16) for i in range(2)]
        got, used = [r.sig(f"got{i}", 16 * K) for i in range(8)], r.sig("used", JT)
        yw, gated, sum_ok = r.sig("yw", JT), r.sig("gated"), r.sig("sum_ok")
        block = ctx.enter_context(nc.Block())

        def one(ap, b):
            return ap[b] if isinstance(b, int) else ap[bass.ds(b, 1)].rearrange("o p j d -> (o p) j d")

        def pairs(eng, body):
            body(0, False)
            with eng.Fori(1, B // 2) as i:
                body(i, True)

        @block.sync
        def _(sp):
            src = io["x3"].rearrange("(b j p) d -> b p j d", b=B, p=P)
            dst = io["out"].rearrange("b (j p) d -> b p j d", p=P)
            def body(i, later):
                for h in range(2):
                    if later:
                        sp.wait_ge(out[h].sem, i * 16)
                    sp.dma_start(x[h][:, :, :], one(src, i * 2 + h)).then_inc(x_in[h].sem, 16)
                    b = i * 2 + h
                    src_gb = io["modrow"][1][b:b + 1, 3 * D:] if isinstance(b, int) else io["modrow"][1][bass.ds(b, 1), 3 * D:]
                    sp.dma_start(gb[h][:, :], src_gb.to_broadcast([P, D])).then_inc(x_in[h].sem, 16)
                for h in range(2):
                    sp.wait_ge(sum_ok.sem, sum_ok.at(i * 2 + h))
                    sp.dma_start(one(dst, i * 2 + h), x[h][:, :, :]).then_inc(out[h].sem, 16)

            pairs(sp, body)
            for h in range(2):
                sp.wait_ge(out[h].sem, 16 * (B // 2))

        @block.gpsimd
        def _(pool):
            gather(nc, io, keep, 1, pool, yk, got, used, range(NT))

        @block.vector
        def _(dve):
            V = nc.vector
            def body(i, later):
                for h in range(2):
                    b = i * 2 + h
                    for j in range(JT):
                        n = h * JT + j
                        dve.wait_ge(got[n].sem, got[n].at(i))
                        cs = [b * JT + (k * NT + j) for k in range(K)]
                        wt = [keep["wts"][:, c:c + 1] if isinstance(c, int) else keep["wts"][:, bass.ds(c, 1)] for c in cs]
                        V.tensor_scalar(acc[h][:, j, :], yk[0][n][:, :], wt[0], None, ALU.mult).then_inc(yw.sem, 1)
                        dve.wait_ge(yw.sem, yw.at(b, j + 1))
                        V.scalar_tensor_tensor(acc[h][:, j, :], yk[1][n][:, :], wt[1], acc[h][:, j, :], ALU.mult, ALU.add).then_inc(used.sem, 1)
                    dve.wait_ge(used.sem, used.at(b))
                    dve.wait_ge(x_in[h].sem, x_in[h].at(i))
                    V.tensor_tensor(acc[h][:, :, :], acc[h][:, :, :], gb[h][:, :].unsqueeze(1).to_broadcast([P, JT, D]), ALU.mult).then_inc(gated.sem, 1)
                    dve.wait_ge(gated.sem, gated.at(b))
                    V.tensor_tensor(x[h][:, :, :], x[h][:, :, :], acc[h][:, :, :], ALU.add).then_inc(sum_ok.sem, 1)

            pairs(dve, body)


def program(nc, io, until=99):
    scratch = {"modrow": [2, B, 4 * D], "bc": [2, 2 * NS, L], "x1": [T, D], "h0": [T, D], "x3": [T, D], "h1": [T, D],
               "xbuf0": [SLOTS + K * T, D], "xbuf1": [SLOTS + K * T, D], "ybuf0": [SLOTS, D], "ybuf1": [SLOTS, D]}
    for name, shape in scratch.items():
        io[name] = nc.dram_tensor(f"s_{name}", shape, F32, kind="Internal").ap()
    with ExitStack() as ctx:
        def sb(name, shape, dt=F32):
            return ctx.enter_context(nc.sbuf_tensor(f"keep_{name}", shape, dt))

        keep = {"ident": sb("ident", [P, P]), "below": sb("below", [P, P]), "ones": sb("ones", [P, P]), "iota": sb("iota", [P, P]),
                "modT": sb("modT", [P, 2, 2 * KD, B]), "logits": sb("logits", [P, NT, E]), "wts": sb("wts", [P, K * NT]),
                "put": sb("put", [P, K * NT], I32), "get": sb("get", [P, K * NT], I32), "owner": sb("owner", [P, NTILES], I32), "taken": []}
        stages = [lambda: setup(nc, io, keep), lambda: mamba(nc, io, keep), lambda: route(nc, io, keep, 0),
                  lambda: experts(nc, io, keep, 0), lambda: mixer(nc, io, keep), lambda: route(nc, io, keep, 1),
                  lambda: experts(nc, io, keep, 1), lambda: last(nc, io, keep)]
        for stage in stages[:until]:
            stage()
            nc.clear_and_free_semaphores(keep["taken"])
            keep["taken"].clear()
            nc.all_engine_barrier()


def kernel(**a):
    import numpy as np
    from concourse import bacc
    from concourse.bass_utils import run_bass_kernel_spmd

    def cols(v):
        return np.ascontiguousarray(v.reshape(-1, P).T)

    def rows(w):
        return np.ascontiguousarray(w.reshape(-1, P, w.shape[1]).transpose(1, 0, 2))

    a = {n: np.asarray(v) for n, v in a.items()}
    iota = np.zeros((P, P), np.float32)
    iota[:, 0:E] = E - np.arange(E)
    iota[:, E:E + MAXT] = TS * np.arange(MAXT)
    iota[:, 24:24 + NTILES] = np.arange(NTILES)
    iota[:, 64:64 + K * NT] = SLOTS + P * np.arange(K * NT)[None, :] + np.arange(P)[:, None]
    arrays = {
        "x": a["L0_attn_x"], "W_in": a["L0_attn_W_in"], "conv_k": a["L0_attn_conv_k"], "W_x": a["L0_attn_W_x"],
        "W_dt": a["L0_attn_W_dt"], "A_log": a["L0_attn_A_log"], "W_out": a["L0_attn_W_out"],
        "vecs": np.stack([cols(a["L0_attn_conv_b"]), cols(a["L0_attn_b_dt"]), cols(a["L0_attn_D"])], axis=1),
        "gate0": rows(a["L0_ffn_Wg"].T), "gate1": rows(a["L1_ffn_router_w"]),
        "WqkvT": rows(a["L1_attn_Wqkv"].T), "WoutT": rows(a["L1_attn_Wout"].T),
        "bqkv": a["L1_attn_bqkv"].reshape(1, -1), "bout": a["L1_attn_bout"].reshape(1, -1),
        "cT": np.stack([rows(a["L0_c"].T), rows(a["L1_c"].T)]), "wmod": np.stack([a["L0_wmod"], a["L1_wmod"]]),
        "w1_0": a["L0_ffn_W1"], "w2_0": a["L0_ffn_W2"], "b2_0": a["L0_ffn_b2"],
        "w1_1": a["L1_ffn_w1"], "w2_1": a["L1_ffn_w2"], "b2_1": a["L1_ffn_b2"],
        "b1_0": a["L0_ffn_b1"].reshape(E, MH, P).transpose(0, 2, 1), "b1_1": a["L1_ffn_b1"].reshape(E, MH, P).transpose(0, 2, 1),
        "ident": np.eye(P, dtype=np.float32), "below": np.triu(np.ones((P, P), np.float32), 1), "iota": iota,
    }
    arrays = {n: np.ascontiguousarray(v) for n, v in arrays.items()}
    nc = bacc.Bacc("TRN2", target_bir_lowering=False, num_devices=1)
    io = {n: nc.dram_tensor(f"in_{n}", v.shape, mybir.dt.from_np(v.dtype), kind="ExternalInput").ap() for n, v in arrays.items()}
    io["out"] = nc.dram_tensor("out", (B, L, D), F32, kind="ExternalOutput").ap()
    program(nc, io, kernel.until)
    r = run_bass_kernel_spmd(nc, [{f"in_{n}": v for n, v in arrays.items()}], core_ids=[0])
    return r.results[0]["out"]


kernel.until = 99
```

```python
from contextlib import ExitStack

import concourse.bass as bass
from concourse import mybir

F32 = mybir.dt.float32
F32R = mybir.dt.float32r
I32 = mybir.dt.int32
ALU = mybir.AluOpType
ACT = mybir.ActivationFunctionType
AX = mybir.AxisListType
P = 128

B, L, D = 8, 512, 256
T = B * L
NT = T // P
JT = L // P
DI, NS, DR, TAPS = 512, 16, 64, 4
MD = DI // P
KD = D // P
DT_MIN, DT_MAX = 0.001, 0.1
EPS = 1e-5
E, K = 8, 2
H = 1024
MH = H // P
CAP = int(round(K * T * 1.05 / E))
TS = 256
NTILES = (K * T + E * (TS - 1)) // TS
SLOTS = NTILES * TS
MAXT = (T + TS - 1) // TS
HEADS, HD = 16, 16
TQ, SQ = 8, 512
UNITS = 2 * NS


class Signal:

    def __init__(self, sem, per):
        self.sem, self.per = sem, per

    def at(self, r, k=None):
        return r * self.per + (self.per if k is None else k)


class Room:

    def __init__(self, nc, ctx, tag, keep):
        self.nc, self.ctx, self.tag, self.taken = nc, ctx, tag, keep["taken"]

    def sb(self, name, shape, dt=F32):
        return self.ctx.enter_context(self.nc.sbuf_tensor(f"{self.tag}_{name}", shape, dt))

    def ps(self, name, shape):
        return self.ctx.enter_context(self.nc.psum_tensor(f"{self.tag}_{name}", shape, F32))

    def sig(self, name, per=1):
        sem = self.nc.alloc_semaphore(name=f"{self.tag}_{name}")
        self.taken.append(sem)
        return Signal(sem, per)


def moments(nc, dve, r, mom, stats, n, sig):
    even, odd = stats[:, 0:n, 1], stats[:, 0:n, 4]
    nc.vector.tensor_tensor(mom[:, 0, 0:n], even, odd, ALU.add).then_inc(sig.sem, 1)
    nc.vector.tensor_tensor(mom[:, 1, 0:n], even, odd, ALU.subtract).then_inc(sig.sem, 1)
    nc.vector.tensor_tensor(mom[:, 2, 0:n], stats[:, 0:n, 2], stats[:, 0:n, 5], ALU.add).then_inc(sig.sem, 1)
    dve.wait_ge(sig.sem, r + 3)
    nc.vector.tensor_scalar(mom[:, 0, 0:n], mom[:, 0, 0:n], 0.5, None, ALU.mult).then_inc(sig.sem, 1)
    nc.vector.tensor_tensor(mom[:, 1, 0:n], mom[:, 1, 0:n], mom[:, 1, 0:n], ALU.mult).then_inc(sig.sem, 1)
    dve.wait_ge(sig.sem, r + 5)
    nc.vector.scalar_tensor_tensor(mom[:, 2, 0:n], mom[:, 1, 0:n], D / 4.0, mom[:, 2, 0:n], ALU.mult, ALU.add).then_inc(sig.sem, 1)


def setup(nc, io, keep):
    with ExitStack() as ctx:
        r = Room(nc, ctx, "set", keep)
        cT = r.sb("cT", [P, 2, KD, B])
        sT = r.sb("sT", [P, 2, KD, B])
        wmod = r.sb("wmod", [P, 2, KD, 6 * D])
        row = r.sb("row", [B, 2, 6 * D])
        sgn = r.sb("sgn", [B, 2, 2, D])
        rowp = r.ps("rowp", [B, 3, 512])
        colp = r.ps("colp", [P, 2 * KD, B])
        c_in, w_in, consts = r.sig("c_in", 32), r.sig("w_in", 32), r.sig("consts", 48)
        silu_c, row_mm, row_cp, col_mm, col_cp = r.sig("silu_c"), r.sig("row_mm"), r.sig("row_cp"), r.sig("col_mm"), r.sig("col_cp")
        step, row_ok, row_out = r.sig("step"), r.sig("row_ok"), r.sig("row_out")
        ones_ok = r.sig("ones_ok")
        block = ctx.enter_context(nc.Block())

        @block.sync
        def _(sp):
            for ly in range(2):
                sp.dma_start(cT[:, ly], io["cT"][ly]).then_inc(c_in.sem, 16)
                sp.dma_start(wmod[:, ly], io["wmod"][ly].rearrange("(k p) n -> p k n", p=P)).then_inc(w_in.sem, 16)
            sp.dma_start(keep["ident"][:, :], io["ident"]).then_inc(consts.sem, 16)
            sp.dma_start(keep["below"][:, :], io["below"]).then_inc(consts.sem, 16)
            sp.dma_start(keep["iota"][:, :], io["iota"]).then_inc(consts.sem, 16)
            sp.wait_ge(row_ok.sem, 2)
            for ly in range(2):
                sp.dma_start(io["modrow"][ly], row[:, ly, 2 * D:]).then_inc(row_out.sem, 16)
            sp.wait_ge(row_out.sem, 32)
            sp.wait_ge(consts.sem, 48)

        @block.gpsimd
        def _(pool):
            pool.memset(keep["ones"][:, :], 1.0).then_inc(ones_ok.sem, 1)
            pool.wait_ge(ones_ok.sem, 1)

        @block.scalar
        def _(act):
            act.wait_ge(c_in.sem, 32)
            nc.scalar.activation(sT[:, :, :, :], cT[:, :, :, :], ACT.Silu).then_inc(silu_c.sem, 1)

        @block.tensor
        def _(pe):
            pe.wait_ge(silu_c.sem, 1)
            pe.wait_ge(w_in.sem, 32)
            for ly in range(2):
                if ly:
                    pe.wait_ge(row_cp.sem, ly)
                for n in range(3):
                    for k in range(KD):
                        mm = nc.tensor.matmul(rowp[:, n, :], sT[:, ly, k, :], wmod[:, ly, k, n * 512:(n + 1) * 512],
                                              start=(k == 0), stop=(k == KD - 1))
                mm.then_inc(row_mm.sem, 1)
                if ly:
                    pe.wait_ge(col_cp.sem, ly)
                for c in range(2 * KD):
                    for k in range(KD):
                        mm = nc.tensor.matmul(colp[:, c, :], wmod[:, ly, k, c * P:(c + 1) * P], sT[:, ly, k, :],
                                              start=(k == 0), stop=(k == KD - 1))
                mm.then_inc(col_mm.sem, 1)

        @block.vector
        def _(dve):
            n = 0
            for ly in range(2):
                dve.wait_ge(row_mm.sem, ly + 1)
                nc.vector.tensor_copy(row[:, ly, :].rearrange("b (n c) -> b n c", n=3), rowp[:, :, :]).then_inc(row_cp.sem, 1)
                dve.wait_ge(row_cp.sem, ly + 1)
                m = row[:, ly, :].rearrange("b (m d) -> b m d", m=6)
                gate = m[:, 2:6:3, :]
                nc.vector.tensor_scalar(sgn[:, ly], gate, 0.0, 2.0, ALU.is_ge, ALU.mult).then_inc(step.sem, 1)
                n += 1
                dve.wait_ge(step.sem, n)
                nc.vector.tensor_scalar(sgn[:, ly], sgn[:, ly], 1.0, None, ALU.subtract).then_inc(step.sem, 1)
                n += 1
                dve.wait_ge(step.sem, n)
                nc.vector.tensor_tensor(gate, gate, sgn[:, ly], ALU.mult).then_inc(step.sem, 1)
                n += 1
                dve.wait_ge(step.sem, n)
                nc.vector.scalar_tensor_tensor(gate, gate, 0.25, sgn[:, ly], ALU.max, ALU.mult).then_inc(step.sem, 1)
                n += 1
                dve.wait_ge(step.sem, n)
                nc.vector.tensor_scalar(m[:, 4, :], m[:, 4, :], 1.0, None, ALU.add).then_inc(row_ok.sem, 1)
                dve.wait_ge(col_mm.sem, ly + 1)
                nc.vector.tensor_copy(keep["modT"][:, ly, 0:KD, :], colp[:, 0:KD, :]).then_inc(step.sem, 1)
                n += 1
                nc.vector.tensor_scalar(keep["modT"][:, ly, KD:, :], colp[:, KD:, :], 1.0, None, ALU.add).then_inc(col_cp.sem, 1)


def mamba(nc, io, keep):
    with ExitStack() as ctx:
        r = Room(nc, ctx, "mam", keep)
        ident = keep["ident"]
        w_in = r.sb("w_in", [P, KD, 2 * DI])
        w_conv = r.sb("w_conv", [P, TAPS, 2, DI])
        w_x = r.sb("w_x", [P, MD, DR + 2 * NS])
        w_dt = r.sb("w_dt", [DR, DI])
        w_out = r.sb("w_out", [P, MD, D])
        w_gate = r.sb("w_gate", [P, KD, E])
        vecs = r.sb("vecs", [P, 3, MD])
        a_neg = r.sb("a_neg", [P, MD, NS])
        eps = r.sb("eps", [P, 1])
        x = r.sb("x", [P, JT, D])
        st = r.sb("st", [P, JT, 6])
        mom = r.sb("mom", [P, 3, JT])
        rstd = r.sb("rstd", [P, JT])
        hT = r.sb("hT", [P, KD, L])
        xs = r.sb("xs", [P, MD, TAPS - 1 + L])
        raw = r.sb("raw", [P, 2 * MD, L])
        su = [r.sb(f"su{i}", [P, 2 * MD, L]) for i in range(2)]
        dbcT = r.sb("dbcT", [DR + 2 * NS, L])
        dtT, bcT = dbcT[0:DR], dbcT[DR:]
        delta = [r.sb(f"delta{i}", [P, MD, L]) for i in range(2)]
        du = [r.sb(f"du{i}", [P, MD, L]) for i in range(2)]
        bc = [r.sb(f"bc{i}", [P, 2, 2, L]) for i in range(2)]
        dA = [r.sb(f"dA{i}", [P, 2, L]) for i in range(4)]
        w = [r.sb(f"w{i}", [P, 2, L]) for i in range(4)]
        xres = r.sb("xres", [P, JT, D])
        rep = r.sb("rep", [P, 4, D])
        x1 = r.sb("x1", [P, JT, D])
        h2 = r.sb("h2", [P, JT, D])
        st2 = r.sb("st2", [P, JT, 6])
        mom2 = r.sb("mom2", [P, 3, JT])
        rstd2 = r.sb("rstd2", [P, JT])
        hT2 = r.sb("hT2", [P, KD, L])
        yacc = r.ps("yacc", [P, MD, L])
        fb = [r.ps(f"fb{i}", [P, L]) for i in range(2)]
        tb = [r.ps(f"tb{i}", [P, L]) for i in range(2)]

        small_in, w_in_in, conv_in, rest_in, ready = r.sig("small_in", 32), r.sig("w_in_in", 16), r.sig("conv_in", 16), r.sig("rest_in", 64), r.sig("ready")
        x_in, ln_st, ln_mv, ln_rs, xn_ok = r.sig("x_in", 16), r.sig("ln_st", 4), r.sig("ln_mv", 6), r.sig("ln_rs", 2), r.sig("xn_ok", 4)
        mm = {"turn": r.sig("turn_mm", KD), "in": r.sig("in_mm", 2 * MD), "conv": r.sig("conv_mm", MD),
              "xb": r.sig("xb_mm"), "dt": r.sig("dt_mm", MD)}
        ev = {"turn": r.sig("turn_ev", KD), "in": r.sig("in_ev", 2 * MD), "conv": r.sig("conv_ev", MD),
              "xb": r.sig("xb_ev"), "dt": r.sig("dt_ev", MD)}
        silued, sp_exp, sp_ln, clipped, du_ok = r.sig("silued", 2), r.sig("sp_exp"), r.sig("sp_ln"), r.sig("clipped"), r.sig("du_ok")
        bc_out, bc_in = r.sig("bc_out", 16), [r.sig(f"bc_in{i}", 64) for i in range(2)]
        folded = [q for q in range(UNITS) if q % 8 in (0,)]
        SUMS = UNITS - len(folded)
        da_ok, bu_ok, h_ok, acc_ok = (r.sig(n, per) for n, per in (("da_ok", UNITS), ("bu_ok", UNITS), ("h_ok", UNITS), ("acc_ok", SUMS)))
        by_vector = [q for q in range(UNITS) if q % 8 in (3,7)]
        hcv_ok, hcp_ok = r.sig("hcv_ok", len(by_vector)), r.sig("hcp_ok", SUMS - len(by_vector))
        fold_ok = r.sig("fold_ok", 2 * len(folded))
        yd_ok, z_ok = r.sig("yd_ok", MD), r.sig("z_ok")
        res_in, rep_in = r.sig("res_in", 16), r.sig("rep_in", 16)
        t_mm, o_ok, x1_ok = r.sig("t_mm", 5), r.sig("o_ok", 2), r.sig("x1_ok")
        st2_ok, mv2_ok, rs2_ok, xn2_ok, sc2_ok, h2_ok = r.sig("st2_ok", 4), r.sig("mv2_ok", 6), r.sig("rs2_ok", 2), r.sig("xn2_ok", 4), r.sig("sc2_ok"), r.sig("h2_ok")
        hT2_ok, lg_ok = r.sig("hT2_ok", 2), r.sig("lg_ok")
        x1_out, h2_out = r.sig("x1_out", 16), r.sig("h2_out", 16)
        block = ctx.enter_context(nc.Block())
        x_dram = io["x"].rearrange("b (j p) d -> b p j d", p=P)
        x1_dram = io["x1"].rearrange("(b j p) d -> b p j d", b=B, p=P)
        h_dram = io["h0"].rearrange("(b j p) d -> b p j d", b=B, p=P)

        PHASES, SCAN = 4, 2
        front_mm = [(10, "turn", 0), (10, "turn", 1), (12, "in", 0), (14, "in", 1), (17, "in", 2), (19, "in", 3),
                    (20, "conv", 0), (22, "in", 4), (25, "conv", 1), (26, "in", 5), (30, "conv", 2), (31, "in", 6),
                    (34, "conv", 3), (35, "in", 7), (44, "xb", 0),
                    (48, "dt", 0), (48, "dt", 1), (50, "dt", 2), (50, "dt", 3)]
        ring = sorted(front_mm, key=lambda job: job[0] % UNITS)
        bank = {(kind, i): fb[n % 2] for n, (_, kind, i) in enumerate(ring)}

        def one(ap, b):
            return ap[b] if isinstance(b, int) else ap[bass.ds(b, 1)].rearrange("o p j d -> (o p) j d")

        def periods(eng, events, unit=None):
            def period(batch, par):
                for q in range(UNITS):
                    for place, step in events:
                        k = place // UNITS
                        if place % UNITS == q and batch(k) is not None:
                            step(batch(k), (par + k) % 2)
                    if unit is not None and batch(SCAN) is not None:
                        unit(batch(SCAN), q, par)

            def fixed(p):
                return lambda k: p - k if 0 <= p - k < B else None

            for p in range(PHASES):
                period(fixed(p), p % 2)
            with eng.Fori(PHASES // 2, B // 2) as i:
                for half in range(2):
                    period(lambda k, half=half: i * 2 + (half - k), half)
            for p in range(B, B + PHASES - 1):
                period(fixed(p), p % 2)

        def before(b, n=1):
            return not isinstance(b, int) or b >= n

        def sums(q):
            return q + 1 - len([f for f in folded if f <= q])

        def pool_units(q):
            return sums(q) - len([n for n in by_vector if n <= q])

        @block.sync
        def _(sp):
            sp.dma_start(x[:, :, :], one(x_dram, 0)).then_inc(x_in.sem, 16)
            for sig, loads in ((small_in, ((a_neg[:, :, :], io["A_log"].rearrange("(m p) n -> p m n", p=P)), (vecs[:, :, :], io["vecs"]))),
                               (w_in_in, ((w_in[:, :, :], io["W_in"].rearrange("(k p) n -> p k n", p=P)),)),
                               (conv_in, ((w_conv[:, :, :, :].rearrange("p t k n -> p (t k) n"), io["conv_k"].rearrange("t (k p) n -> p (t k) n", p=P)),)),
                               (rest_in, ((w_x[:, :, :], io["W_x"].rearrange("(k p) n -> p k n", p=P)), (w_dt[:, :], io["W_dt"]),
                                          (w_out[:, :, :], io["W_out"].rearrange("(k p) n -> p k n", p=P)), (w_gate[:, :, :], io["gate0"])))):
                for dst, src in loads:
                    sp.dma_start(dst, src).then_inc(sig.sem, 16)

            def load_x(b, par):
                if not before(b):
                    return
                sp.wait_ge(mm["turn"].sem, mm["turn"].at(b - 1))
                sp.dma_start(x[:, :, :], one(x_dram, b)).then_inc(x_in.sem, 16)

            def store_bc(b, par):
                if before(b, 2):
                    sp.wait_ge(bc_in[0].sem, bc_in[0].at(b - 2) * (NS // 4))
                    sp.wait_ge(bc_in[1].sem, bc_in[1].at(b - 2) * (NS // 4))
                sp.wait_ge(ev["xb"].sem, ev["xb"].at(b))
                sp.dma_start(io["bc"][par], bcT[:, :]).then_inc(bc_out.sem, 16)

            def load_tail(b, par):
                if before(b):
                    sp.wait_ge(x1_ok.sem, x1_ok.at(b - 1))
                    sp.wait_ge(h2_ok.sem, h2_ok.at(b - 1))
                sp.dma_start(xres[:, :, :], one(x_dram, b)).then_inc(res_in.sem, 16)
                src = io["modrow"][0, bass.ds(b, 1)] if not isinstance(b, int) else io["modrow"][0, b:b + 1]
                sp.dma_start(rep[:, :, :], src.rearrange("o (m d) -> o m d", m=4).to_broadcast([P, 4, D])).then_inc(rep_in.sem, 16)

            def store_x1(b, par):
                sp.wait_ge(x1_ok.sem, x1_ok.at(b))
                sp.dma_start(one(x1_dram, b), x1[:, :, :]).then_inc(x1_out.sem, 16)

            def store_h2(b, par):
                sp.wait_ge(h2_ok.sem, h2_ok.at(b))
                sp.dma_start(one(h_dram, b), h2[:, :, :]).then_inc(h2_out.sem, 16)

            def unit(b, q, par):
                if q % 4:
                    return
                c = q // 4
                if c >= 2 or before(b):
                    sp.wait_ge(acc_ok.sem, acc_ok.at(b, sums(4 * c - 5)) if c >= 2 else acc_ok.at(b - 1, sums(UNITS - 5 + 4 * c)))
                if c == 0:
                    sp.wait_ge(bc_out.sem, bc_out.at(b))
                src = io["bc"][par].rearrange("(g n) t -> n g t", g=2)[2 * c:2 * c + 2]
                for n in range(2):
                    for g in range(2):
                        sp.dma_start(bc[c % 2][:, n, g], src[n, g:g + 1, :].to_broadcast([P, L])).then_inc(bc_in[c % 2].sem, 16)

            periods(sp, [(0, load_x), (54, store_bc), (98, load_tail), (113, store_x1), (125, store_h2)], unit)
            sp.wait_ge(x1_out.sem, 16 * B)
            sp.wait_ge(h2_out.sem, 16 * B)

        @block.scalar
        def _(act):
            act.wait_ge(small_in.sem, small_in.at(0))
            nc.scalar.activation(a_neg[:, :, :], a_neg[:, :, :], ACT.Exp).then_inc(ready.sem, 1)
            act.wait_ge(ready.sem, 5)

            def unit(b, q, par):
                n, m0 = q // 2, 2 * (q % 2)
                if q == 0:
                    act.wait_ge(clipped.sem, clipped.at(b))
                if q >= 4 or before(b):
                    act.wait_ge(h_ok.sem, h_ok.at(b, q - 3) if q >= 4 else h_ok.at(b - 1, UNITS + q - 3))
                for m in range(2):
                    ins = nc.scalar.activation(dA[q % 4][:, m, 1:], delta[par][:, m0 + m, 1:], ACT.Exp,
                                               scale=a_neg[:, m0 + m, n:n + 1])
                ins.then_inc(da_ok.sem, 1)

            def evac(kind, i, out, func, b, rows=P, **kw):
                act.wait_ge(mm[kind].sem, mm[kind].at(b, i + 1))
                nc.scalar.activation(out, bank[kind, i][0:rows, :], func, **kw).then_inc(ev[kind].sem, 1)

            def rstd_x(b, par):
                act.wait_ge(ln_mv.sem, ln_mv.at(b))
                nc.scalar.activation(rstd[:, :], mom[:, 2, :], ACT.Ln, bias=eps[:, 0:1], scale=1.0 / D).then_inc(ln_rs.sem, 1)
                act.wait_ge(ln_rs.sem, ln_rs.at(b, 1))
                nc.scalar.activation(rstd[:, :], rstd[:, :], ACT.Exp, scale=-0.5).then_inc(ln_rs.sem, 1)

            def turned(b, par):
                if before(b):
                    act.wait_ge(mm["in"].sem, mm["in"].at(b - 1))
                for dh in range(KD):
                    at = slice(b, b + 1) if isinstance(b, int) else bass.ds(b, 1)
                    evac("turn", dh, hT[:, dh, :], ACT.Identity, b,
                         scale=keep["modT"][:, 0, KD + dh, at], bias=keep["modT"][:, 0, dh, at])

            def in_out(m):
                def step(b, par):
                    if m == 0 and before(b):
                        act.wait_ge(mm["conv"].sem, mm["conv"].at(b - 1))
                    evac("in", m, xs[:, m, TAPS - 1:] if m < MD else raw[:, m - MD, :], ACT.Copy, b)
                return step

            def conv_out(m):
                def step(b, par):
                    evac("conv", m, raw[:, MD + m, :], ACT.Identity, b, bias=vecs[:, 0, m:m + 1])
                return step

            def silu(b, par):
                if before(b, 2):
                    act.wait_ge(t_mm.sem, t_mm.at(b - 2, 2))
                act.wait_ge(ev["conv"].sem, ev["conv"].at(b))
                act.wait_ge(ev["in"].sem, ev["in"].at(b))
                for g in (1, 0):
                    nc.scalar.activation(su[par][:, MD * g:MD * g + MD, :], raw[:, MD * g:MD * g + MD, :], ACT.Silu).then_inc(silued.sem, 1)

            def dbc_rows(b, par):
                if before(b):
                    act.wait_ge(mm["dt"].sem, mm["dt"].at(b - 1))
                    act.wait_ge(bc_out.sem, bc_out.at(b - 1))
                evac("xb", 0, dbcT[:, :], ACT.Copy, b, rows=DR + 2 * NS)

            def softplus(b, par):
                act.wait_ge(ev["dt"].sem, ev["dt"].at(b))
                nc.scalar.activation(delta[par][:, :, :], delta[par][:, :, :], ACT.Exp).then_inc(sp_exp.sem, 1)
                act.wait_ge(sp_exp.sem, sp_exp.at(b))
                nc.scalar.activation(delta[par][:, :, :], delta[par][:, :, :], ACT.Ln, bias=1.0).then_inc(sp_ln.sem, 1)

            def rstd_x1(b, par):
                act.wait_ge(mv2_ok.sem, mv2_ok.at(b))
                nc.scalar.activation(rstd2[:, :], mom2[:, 2, :], ACT.Ln, bias=eps[:, 0:1], scale=1.0 / D).then_inc(rs2_ok.sem, 1)
                act.wait_ge(rs2_ok.sem, rs2_ok.at(b, 1))
                nc.scalar.activation(rstd2[:, :], rstd2[:, :], ACT.Exp, scale=-0.5).then_inc(rs2_ok.sem, 1)

            def turned2(b, par):
                for dh in range(KD):
                    act.wait_ge(t_mm.sem, t_mm.at(b, 3 + dh))
                    nc.scalar.activation(hT2[:, dh, :], tb[dh % 2][:, :], ACT.Copy).then_inc(hT2_ok.sem, 1)

            periods(act, [(7, rstd_x), (15, turned)]
                    + [(place + 5, in_out(i)) for place, kind, i in front_mm if kind == "in"]
                    + [(place + 8, conv_out(i)) for place, kind, i in front_mm if kind == "conv"]
                    + [(45, silu), (50, dbc_rows), (56, softplus), (114, rstd_x1), (125, turned2)], unit)

        @block.vector
        def _(dve):
            for i in range(4):
                nc.vector.memset(dA[i][:, :, 0:1], 0.0)
            nc.vector.memset(xs[:, :, 0:TAPS - 1], 0.0).then_inc(ready.sem, 1)
            nc.vector.memset(eps[:, :], EPS).then_inc(ready.sem, 1)
            nc.vector.memset(rstd[:, :], 0.0).then_inc(ready.sem, 1)
            dve.wait_ge(ready.sem, 4)
            nc.vector.tensor_scalar(a_neg[:, :, :], a_neg[:, :, :], -1.0, None, ALU.mult).then_inc(ready.sem, 1)

            def unit(b, q, par):
                n, m0 = q // 2, 2 * (q % 2)
                if q == 0:
                    dve.wait_ge(du_ok.sem, du_ok.at(b))
                if q % 4 == 0:
                    dve.wait_ge(bc_in[(q // 4) % 2].sem, b * (64 * NS // 4) + 64 * (q // 8 + 1))
                if q >= 4 or before(b):
                    old, at = (b, q - 4) if q >= 4 else (b - 1, q - 4 + UNITS)
                    if at in folded:
                        dve.wait_ge(hcp_ok.sem, hcp_ok.at(old, pool_units(at + 2)))
                    else:
                        dve.wait_ge(acc_ok.sem, acc_ok.at(old, sums(at)))
                bn = bc[(q // 4) % 2][:, n % 2, 0:1, :].to_broadcast([P, 2, L])
                nc.vector.tensor_tensor(w[q % 4][:, :, :], du[par][:, m0:m0 + 2, :], bn, ALU.mult).then_inc(bu_ok.sem, 1)
                dve.wait_ge(bu_ok.sem, bu_ok.at(b, q + 1))
                dve.wait_ge(da_ok.sem, da_ok.at(b, q + 1))
                wf = w[q % 4][:, :, :].rearrange("p m t -> p (m t)")
                nc.vector.tensor_tensor_scan(wf, dA[q % 4][:, :, :].rearrange("p m t -> p (m t)"), wf, 0.0,
                                             ALU.mult, ALU.add).then_inc(h_ok.sem, 1)
                if q in by_vector:
                    dve.wait_ge(h_ok.sem, h_ok.at(b, q + 1))
                    cn = bc[(q // 4) % 2][:, n % 2, 1:2, :].to_broadcast([P, 2, L])
                    nc.vector.tensor_tensor(w[q % 4][:, :, :], w[q % 4][:, :, :], cn, ALU.mult).then_inc(hcv_ok.sem, 1)

            def add_du(half):
                def step(b, par):
                    dve.wait_ge(acc_ok.sem, acc_ok.at(b, SUMS - 1 + half))
                    for m in (2 * half, 2 * half + 1):
                        nc.vector.scalar_tensor_tensor(su[par][:, MD + m, :], su[par][:, MD + m, :], vecs[:, 2, m:m + 1],
                                                       yacc[:, m, :], ALU.mult, ALU.add).then_inc(yd_ok.sem, 1)
                return step

            def gated(b, par):
                dve.wait_ge(yd_ok.sem, yd_ok.at(b))
                nc.vector.tensor_tensor(su[par][:, MD:, :], su[par][:, MD:, :], su[par][:, 0:MD, :], ALU.mult).then_inc(z_ok.sem, 1)

            def norm(b, src, stats, mean, s_ok, m_ok):
                for j in range(JT):
                    nc.vector.bn_stats(stats[:, j, :], src[:, j, :]).then_inc(s_ok.sem, 1)
                dve.wait_ge(s_ok.sem, s_ok.at(b))
                moments(nc, dve, m_ok.at(b, 0), mean, stats, JT, m_ok)

            def norm_x(b, par):
                dve.wait_ge(x_in.sem, x_in.at(b))
                norm(b, x, st, mom, ln_st, ln_mv)

            def scaled_x(b, par):
                dve.wait_ge(ln_rs.sem, ln_rs.at(b))
                for j in range(JT):
                    nc.vector.tensor_scalar(x[:, j, :], x[:, j, :], mom[:, 0, j:j + 1], rstd[:, j:j + 1],
                                            ALU.subtract, ALU.mult).then_inc(xn_ok.sem, 1)

            def dt_out(half):
                def step(b, par):
                    for m in (2 * half, 2 * half + 1):
                        dve.wait_ge(mm["dt"].sem, mm["dt"].at(b, m + 1))
                        nc.vector.tensor_scalar(delta[par][:, m, :], bank["dt", m][:, :], vecs[:, 1, m:m + 1], 20.0,
                                                ALU.add, ALU.min).then_inc(ev["dt"].sem, 1)
                return step

            def clip(b, par):
                dve.wait_ge(sp_ln.sem, sp_ln.at(b))
                nc.vector.tensor_scalar(delta[par][:, :, :], delta[par][:, :, :], DT_MIN, DT_MAX,
                                        ALU.max, ALU.min).then_inc(clipped.sem, 1)

            def times_u(b, par):
                dve.wait_ge(clipped.sem, clipped.at(b))
                nc.vector.tensor_tensor(du[par][:, :, :], delta[par][:, :, :], su[par][:, MD:, :], ALU.mult).then_inc(du_ok.sem, 1)

            def residual(g):
                def step(b, par):
                    if g == 0:
                        dve.wait_ge(rep_in.sem, rep_in.at(b))
                        dve.wait_ge(res_in.sem, res_in.at(b))
                        if before(b):
                            dve.wait_ge(x1_out.sem, x1_out.at(b - 1))
                    dve.wait_ge(t_mm.sem, t_mm.at(b, g + 1))
                    nc.vector.tensor_tensor(x1[:, 2 * g:2 * g + 2, :], tb[g][:, :].rearrange("p (j d) -> p j d", j=2),
                                            rep[:, 0:1, :].to_broadcast([P, 2, D]), ALU.mult).then_inc(o_ok.sem, 1)
                    if g == 1:
                        dve.wait_ge(o_ok.sem, o_ok.at(b))
                        nc.vector.tensor_tensor(x1[:, :, :], x1[:, :, :], xres[:, :, :], ALU.add).then_inc(x1_ok.sem, 1)
                return step

            def norm_x1(b, par):
                dve.wait_ge(x1_ok.sem, x1_ok.at(b))
                norm(b, x1, st2, mom2, st2_ok, mv2_ok)

            def scaled_x1(b, par):
                dve.wait_ge(rs2_ok.sem, rs2_ok.at(b))
                if before(b):
                    dve.wait_ge(h2_out.sem, h2_out.at(b - 1))
                for j in range(JT):
                    nc.vector.tensor_scalar(h2[:, j, :], x1[:, j, :], mom2[:, 0, j:j + 1], rstd2[:, j:j + 1],
                                            ALU.subtract, ALU.mult).then_inc(xn2_ok.sem, 1)

            def logits(b, par):
                dve.wait_ge(t_mm.sem, t_mm.at(b))
                dst = keep["logits"][:, b * JT:(b + 1) * JT, :] if isinstance(b, int) else keep["logits"][:, bass.ds(b * JT, JT), :]
                nc.vector.tensor_scalar(dst, tb[0][:, 0:JT * E].rearrange("p (j e) -> p j e", j=JT), 1.0, None,
                                        ALU.mult).then_inc(lg_ok.sem, 1)

            periods(dve, [(4, norm_x), (9, scaled_x), (52, dt_out(0)), (54, dt_out(1)), (58, clip), (59, times_u),
                          (98, add_du(0)), (99, add_du(1)), (99, gated), (107, residual(0)), (109, residual(1)),
                          (111, norm_x1), (116, scaled_x1), (127, logits)], unit)

        @block.gpsimd
        def _(pool):
            def unit(b, q, par):
                if q in by_vector:
                    return
                n = q // 2
                if q % 4 == 0 or (q % 4 == 1 and q - 1 in by_vector):
                    pool.wait_ge(bc_in[(q // 4) % 2].sem, b * (64 * NS // 4) + 64 * (q // 8 + 1))
                pool.wait_ge(h_ok.sem, h_ok.at(b, q + 1))
                cn = bc[(q // 4) % 2][:, n % 2, 1:2, :].to_broadcast([P, 2, L])
                nc.gpsimd.tensor_tensor(w[q % 4][:, :, :], w[q % 4][:, :, :], cn, ALU.mult).then_inc(
                    fold_ok.sem if q in folded or q - 2 in folded else hcp_ok.sem, 1)
                if q - 2 in folded:
                    pool.wait_ge(fold_ok.sem, fold_ok.at(b, 2 * (folded.index(q - 2) + 1)))
                    nc.gpsimd.tensor_tensor(w[q % 4][:, :, :], w[q % 4][:, :, :], w[(q - 2) % 4][:, :, :], ALU.add).then_inc(hcp_ok.sem, 1)

            def scale_h2(b, par):
                pool.wait_ge(xn2_ok.sem, xn2_ok.at(b))
                nc.gpsimd.tensor_tensor(h2[:, :, :], h2[:, :, :], rep[:, 2:3, :].to_broadcast([P, JT, D]), ALU.mult).then_inc(sc2_ok.sem, 1)

            def shift_h2(b, par):
                pool.wait_ge(sc2_ok.sem, sc2_ok.at(b))
                nc.gpsimd.tensor_tensor(h2[:, :, :], h2[:, :, :], rep[:, 1:2, :].to_broadcast([P, JT, D]), ALU.add).then_inc(h2_ok.sem, 1)

            periods(pool, [(115, scale_h2), (117, shift_h2)], unit)

        @block.tensor
        def _(pe):
            pe.wait_ge(ready.sem, 5)

            def unit(b, q, par):
                if q in folded:
                    return
                m0 = 2 * (q % 2)
                fresh = q == min(n for n in range(UNITS) if n % 2 == q % 2 and n not in folded)
                if fresh and before(b):
                    pe.wait_ge(yd_ok.sem, yd_ok.at(b - 1, m0 + 2))
                if q in by_vector:
                    pe.wait_ge(hcv_ok.sem, hcv_ok.at(b, by_vector.index(q) + 1))
                else:
                    pe.wait_ge(hcp_ok.sem, hcp_ok.at(b, pool_units(q)))
                for m in range(2):
                    ins = nc.tensor.matmul(yacc[:, m0 + m, :], ident[:, :], w[q % 4][:, m, :],
                                           start=fresh, stop=(q >= UNITS - 2))
                ins.then_inc(acc_ok.sem, 1)

            def free(b, kind, i):
                mine = bank[kind, i]
                n = [job[1:] for job in ring].index((kind, i))
                p = b + ring[n][0] // UNITS
                while not isinstance(p, int) or p >= 0:
                    n -= 1
                    if n < 0:
                        n, p = n + len(ring), p - 1
                    place, kind, i = ring[n]
                    older = p - place // UNITS
                    if bank[kind, i] is not mine:
                        continue
                    if not isinstance(p, int) or 0 <= older < B:
                        pe.wait_ge(ev[kind].sem, ev[kind].at(older, i + 1))
                        return

            def turn(b, par):
                pe.wait_ge(xn_ok.sem, xn_ok.at(b))
                for dh in range(KD):
                    free(b, "turn", dh)
                    for j in range(JT):
                        ins = nc.tensor.transpose(bank["turn", dh][:, j * P:(j + 1) * P], x[:, j, dh * P:(dh + 1) * P], ident[:, :])
                    ins.then_inc(mm["turn"].sem, 1)

            def product(kind, i, pairs, part=0, parts=1, rows=P, need=None):
                def step(b, par):
                    if part == 0:
                        if not before(b) and i == 0 and kind in ("in", "conv", "xb"):
                            weights = {"in": w_in_in, "conv": conv_in, "xb": rest_in}[kind]
                            pe.wait_ge(weights.sem, weights.at(0))
                        if need is not None:
                            need(b)
                        free(b, kind, i)
                    todo = pairs(par)
                    size = len(todo) // parts
                    for n in range(part * size, (part + 1) * size):
                        ins = nc.tensor.matmul(bank[kind, i][0:rows, :], todo[n][0], todo[n][1], start=(n == 0), stop=(n == len(todo) - 1))
                    if part == parts - 1:
                        ins.then_inc(mm[kind].sem, 1)
                return step

            events = [(10, turn)]
            for place, kind, i in front_mm:
                if kind == "in":
                    events.append((place, product("in", i, lambda par, m=i: [(w_in[:, k, m * P:(m + 1) * P], hT[:, k, :]) for k in range(KD)],
                                                  need=lambda b: pe.wait_ge(ev["turn"].sem, ev["turn"].at(b)))))
                if kind == "conv":
                    at = [place + s for s in ((0, 1, 2, 3) if i < MD - 1 else (0, 1, 3, 5))]
                    for tap in range(TAPS):
                        events.append((at[tap], product("conv", i, lambda par, m=i: [(w_conv[:, t, k, m * P:(m + 1) * P], xs[:, 2 * (m // 2) + k, t:t + L])
                                                                                    for t in range(TAPS) for k in range(2)], tap, TAPS,
                                                        need=lambda b, m=i: pe.wait_ge(ev["in"].sem, ev["in"].at(b, 2 * (m // 2) + 2)))))
                if kind == "xb":
                    events.append((place, product("xb", i, lambda par: [(w_x[:, k, :], su[par][:, MD + k, :]) for k in range(MD)], rows=DR + 2 * NS,
                                                  need=lambda b: pe.wait_ge(silued.sem, silued.at(b, 1)))))
                if kind == "dt":
                    events.append((place, product("dt", i, lambda par, m=i: [(w_dt[:, m * P:(m + 1) * P], dtT[:, :])],
                                                  need=lambda b: pe.wait_ge(ev["xb"].sem, ev["xb"].at(b, 1)))))

            def out(j):
                def step(b, par):
                    g = j // 2
                    if j == 0:
                        pe.wait_ge(z_ok.sem, z_ok.at(b))
                    if j == 0 and before(b):
                        pe.wait_ge(lg_ok.sem, lg_ok.at(b - 1))
                    if j == 2 and before(b):
                        pe.wait_ge(hT2_ok.sem, hT2_ok.at(b - 1))
                    for k in range(MD):
                        ins = nc.tensor.matmul(tb[g][:, (j % 2) * D:(j % 2 + 1) * D], su[par][:, MD + k, j * P:(j + 1) * P],
                                               w_out[:, k, :], start=(k == 0), stop=(k == MD - 1))
                    if j % 2:
                        ins.then_inc(t_mm.sem, 1)
                return step

            def turn2(b, par):
                pe.wait_ge(h2_ok.sem, h2_ok.at(b))
                for dh in range(KD):
                    pe.wait_ge(o_ok.sem, o_ok.at(b, dh + 1))
                    for j in range(JT):
                        ins = nc.tensor.transpose(tb[dh][:, j * P:(j + 1) * P], h2[:, j, dh * P:(dh + 1) * P], ident[:, :])
                    ins.then_inc(t_mm.sem, 1)

            def logits(b, par):
                pe.wait_ge(hT2_ok.sem, hT2_ok.at(b))
                for j in range(JT):
                    for dh in range(KD):
                        ins = nc.tensor.matmul(tb[0][:, j * E:(j + 1) * E], hT2[:, dh, j * P:(j + 1) * P], w_gate[:, dh, :],
                                               start=(dh == 0), stop=(dh == KD - 1))
                ins.then_inc(t_mm.sem, 1)

            periods(pe, events + [(100, out(0)), (102, out(1)), (104, out(2)), (105, out(3)), (120, turn2), (123, logits)], unit)


def route(nc, io, keep, ly):
    with ExitStack() as ctx:
        r = Room(nc, ctx, f"rt{ly}", keep)
        lg, iota = keep["logits"], keep["iota"]
        lg2 = r.sb("lg2", [P, NT, E])
        top = [r.sb(f"top{k}", [P, NT]) for k in range(K)]
        sc = r.sb("sc", [P, NT, E])
        best = r.sb("best", [P, NT])
        hot = r.sb("hot", [P, E, K, NT])
        ex = r.sb("ex", [P, NT, E])
        d2 = r.sb("d2", [P, NT])
        ssum = r.sb("ssum", [P, NT])
        seg = r.sb("seg", [P, E, K * NT])
        tot = r.sb("tot", [P, E, K * NT])
        inc = r.sb("inc", [P, E, K * NT])
        rank = r.sb("rank", [P, E, K * NT])
        cnt = r.sb("cnt", [P, E])
        cmp = r.sb("cmp", [P, E, MAXT])
        nt = r.sb("nt", [P, E])
        end = r.sb("end", [P, E])
        base = r.sb("base", [P, E])
        own = r.sb("own", [P, NTILES, E])
        ownf = r.sb("ownf", [P, NTILES])
        rk = r.sb("rk", [P, K * NT])
        slot = r.sb("slot", [P, K * NT])
        inside = r.sb("inside", [P, K * NT])
        put = r.sb("put", [P, K * NT])
        part_i = r.sb("part_i", [P, 3, K * NT], I32)
        lane, tile = r.sb("lane", [P, K * NT]), r.sb("tile", [P, K * NT])
        lane_hot = r.sb("lane_hot", [P, K * NT, P], F32R)
        tile_id = r.sb("tile_id", [P, K * NT, SLOTS // P], F32R)
        pre_p, tot_p, source_p = r.ps("pre_p", [P, E * K * NT]), r.ps("tot_p", [P, E * K * NT]), r.ps("source_p", [P, SLOTS // P])
        step, hot_ok, counted, diff_ok, exp_ok, one_hot, source_mm = (r.sig(n) for n in ("step", "hot_ok", "counted", "diff_ok", "exp_ok", "one_hot", "source_mm"))
        tile_ok, ids_ok = r.sig("tile_ok"), r.sig("ids_ok")
        by_pool = [c for c in range(K * NT) if c % 2]
        block = ctx.enter_context(nc.Block())

        @block.gpsimd
        def _(pool):
            pool.wait_ge(tile_ok.sem, 1)
            for c in by_pool:
                nc.gpsimd.tensor_scalar(tile_id[:, c, :], iota[:, P:P + SLOTS // P], tile[:, c:c + 1], iota[:, 64 + c:65 + c],
                                        ALU.is_equal, ALU.mult).then_inc(ids_ok.sem, 1)

        @block.tensor
        def _(pe):
            pe.wait_ge(hot_ok.sem, K)
            hf = hot[:, :, :, :].rearrange("p e k j -> p (e k j)")
            nc.tensor.matmul(pre_p[:, :], keep["below"][:, :], hf, start=True, stop=True)
            nc.tensor.matmul(tot_p[:, :], keep["ones"][:, :], hf, start=True, stop=True).then_inc(counted.sem, 1)
            for c in range(K * NT):
                pe.wait_ge(one_hot.sem, c + 1)
                if c in by_pool:
                    pe.wait_ge(ids_ok.sem, by_pool.index(c) + 1)
                mm = nc.tensor.matmul(source_p[:, :], lane_hot[:, c, :], tile_id[:, c, :], start=(c == 0), stop=(c == K * NT - 1))
            mm.then_inc(source_mm.sem, 1)

        @block.scalar
        def _(act):
            act.wait_ge(diff_ok.sem, 2)
            nc.scalar.activation(ex[:, :, :], ex[:, :, :], ACT.Exp).then_inc(exp_ok.sem, 1)
            nc.scalar.activation(d2[:, :], d2[:, :], ACT.Exp).then_inc(exp_ok.sem, 1)

        @block.vector
        def _(dve):
            done = [0]

            def link(ins):
                done[0] += 1
                ins.then_inc(step.sem, 1)
                dve.wait_ge(step.sem, done[0])

            V = nc.vector

            def wide(ap, n=E):
                return ap.unsqueeze(2).to_broadcast([P, ap.shape[1], n])

            falling = iota[:, 0:E].unsqueeze(1).to_broadcast([P, NT, E])
            for k in range(K):
                cur = lg if k == 0 else lg2
                link(V.tensor_reduce(top[k][:, :], cur[:, :, :], AX.X, ALU.max))
                link(V.tensor_tensor(sc[:, :, :], cur[:, :, :], wide(top[k][:, :]), ALU.is_equal))
                link(V.tensor_tensor(sc[:, :, :], sc[:, :, :], falling, ALU.mult))
                link(V.tensor_reduce(best[:, :], sc[:, :, :], AX.X, ALU.max))
                link(V.tensor_tensor(sc[:, :, :], sc[:, :, :], wide(best[:, :]), ALU.is_equal))
                V.tensor_copy(hot[:, :, k, :], sc[:, :, :].rearrange("p j e -> p e j")).then_inc(hot_ok.sem, 1)
                if k == 0:
                    link(V.scalar_tensor_tensor(lg2[:, :, :], sc[:, :, :], -3e38, lg[:, :, :], ALU.mult, ALU.add))
            V.tensor_tensor(ex[:, :, :], lg[:, :, :], wide(top[0][:, :]), ALU.subtract).then_inc(diff_ok.sem, 1)
            V.tensor_tensor(d2[:, :], top[1][:, :], top[0][:, :], ALU.subtract).then_inc(diff_ok.sem, 1)
            link(V.memset(seg[:, :, :], 1.0))
            link(V.memset(seg[:, :, 0:1], 0.0))
            dve.wait_ge(exp_ok.sem, 2)
            link(V.tensor_reduce(ssum[:, :], ex[:, :, :], AX.X, ALU.add))
            w0, w1 = keep["wts"][:, 0:NT], keep["wts"][:, NT:]
            link(V.reciprocal(w0, ssum[:, :]))
            link(V.tensor_tensor(w1, d2[:, :], w0, ALU.mult))
            if ly == 1:
                link(V.tensor_tensor(ssum[:, :], w0, w1, ALU.add))
                link(V.reciprocal(ssum[:, :], ssum[:, :]))
                link(V.tensor_tensor(w0, w0, ssum[:, :], ALU.mult))
                link(V.tensor_tensor(w1, w1, ssum[:, :], ALU.mult))
            dve.wait_ge(counted.sem, 1)
            flat = "p e c -> p (e c)"
            link(V.tensor_copy(tot[:, :, :].rearrange(flat), tot_p[:, :]))
            link(V.tensor_tensor_scan(inc[:, :, :].rearrange(flat), seg[:, :, :].rearrange(flat),
                                      tot[:, :, :].rearrange(flat), 0.0, ALU.mult, ALU.add))
            link(V.tensor_tensor(tot[:, :, :], inc[:, :, :], tot[:, :, :], ALU.subtract))
            link(V.tensor_tensor(rank[:, :, :].rearrange(flat), pre_p[:, :], tot[:, :, :].rearrange(flat), ALU.add))
            cap = float(CAP if ly == 0 else T)
            link(V.tensor_scalar(cnt[:, :], inc[:, :, K * NT - 1], cap, None, ALU.min))
            link(V.tensor_tensor(cmp[:, :, :], wide(cnt[:, :], MAXT), iota[:, E:E + MAXT].unsqueeze(1).to_broadcast([P, E, MAXT]), ALU.is_gt))
            link(V.tensor_reduce(nt[:, :], cmp[:, :, :], AX.X, ALU.add))
            link(V.memset(base[:, :], 1.0))
            link(V.tensor_tensor_scan(end[:, :], base[:, :], nt[:, :], 0.0, ALU.mult, ALU.add))
            link(V.tensor_tensor(base[:, :], end[:, :], nt[:, :], ALU.subtract))
            link(V.tensor_scalar(base[:, :], base[:, :], float(TS), None, ALU.mult))
            tiles = iota[:, 24:24 + NTILES].unsqueeze(2).to_broadcast([P, NTILES, E])
            link(V.tensor_tensor(own[:, :, :], end[:, :].unsqueeze(1).to_broadcast([P, NTILES, E]), tiles, ALU.is_le))
            link(V.tensor_reduce(ownf[:, :], own[:, :, :], AX.X, ALU.add))
            link(V.tensor_scalar(keep["owner"][:, :], ownf[:, :], float(E - 1), None, ALU.min))
            hotc = hot[:, :, :, :].rearrange("p e k j -> p e (k j)")
            link(V.tensor_tensor(tot[:, :, :], rank[:, :, :], hotc, ALU.mult))
            link(V.tensor_reduce(rk[:, :], tot[:, :, :].rearrange("p e c -> p c e"), AX.X, ALU.add))
            link(V.tensor_tensor(tot[:, :, :], hotc, wide(base[:, :], K * NT), ALU.mult))
            link(V.tensor_reduce(slot[:, :], tot[:, :, :].rearrange("p e c -> p c e"), AX.X, ALU.add))
            link(V.tensor_tensor(slot[:, :], slot[:, :], rk[:, :], ALU.add))
            link(V.tensor_scalar(inside[:, :], rk[:, :], cap, None, ALU.is_lt))
            link(V.tensor_tensor(slot[:, :], slot[:, :], inside[:, :], ALU.mult))
            link(V.tensor_tensor(keep["wts"][:, :], keep["wts"][:, :], inside[:, :], ALU.mult))
            link(V.tensor_copy(keep["get"][:, :], slot[:, :]))
            link(V.tensor_scalar(inside[:, :], inside[:, :], -float(SLOTS), float(SLOTS), ALU.mult, ALU.add))
            link(V.tensor_tensor(put[:, :], inside[:, :], slot[:, :], ALU.add))
            link(V.tensor_copy(part_i[:, 0, :], put[:, :]))
            link(V.tensor_scalar(part_i[:, 1, :], part_i[:, 0, :], P - 1, None, ALU.bitwise_and))
            link(V.tensor_scalar(part_i[:, 2, :], part_i[:, 0, :], P.bit_length() - 1, None, ALU.logical_shift_right))
            V.tensor_copy(tile[:, :], part_i[:, 2, :]).then_inc(tile_ok.sem, 1)
            link(V.tensor_copy(lane[:, :], part_i[:, 1, :]))
            for c in range(K * NT):
                if c not in by_pool:
                    V.tensor_scalar(tile_id[:, c, :], iota[:, P:P + SLOTS // P], tile[:, c:c + 1], iota[:, 64 + c:65 + c], ALU.is_equal, ALU.mult)
                V.tensor_scalar(lane_hot[:, c, :], iota[:, P:2 * P], lane[:, c:c + 1], None, ALU.is_equal).then_inc(one_hot.sem, 1)
            dve.wait_ge(source_mm.sem, 1)
            link(V.tensor_copy(keep["source"][:, :], source_p[:, :]))


def experts(nc, io, keep, ly):
    with ExitStack() as ctx:
        r = Room(nc, ctx, f"ex{ly}", keep)
        ident = keep["ident"]
        SB = TS // P
        HI, LO = 0, 1
        w1 = [r.sb(f"w1_{i}", [P, KD, H]) for i in range(2)]
        w2 = [r.sb(f"w2_{i}", [P, MH, D]) for i in range(2)]
        w1s = [r.sb(f"w1s_{i}", [P, 2, KD, H], F32R) for i in range(2)]
        w2s = [r.sb(f"w2s_{i}", [P, 2, MH, D], F32R) for i in range(2)]
        b1 = [r.sb(f"b1_{i}", [P, MH]) for i in range(2)]
        b2 = [r.sb(f"b2_{i}", [P, D]) for i in range(2)]
        xin = [r.sb(f"xin{i}", [P, SB, D]) for i in range(2)]
        xTs = [r.sb(f"xTs{i}", [P, 2, KD, TS], F32R) for i in range(2)]
        hid = [r.sb(f"hid{i}", [P, MH, TS]) for i in range(2)]
        hids = [r.sb(f"hids{i}", [P, 2, MH, TS], F32R) for i in range(2)]
        y = [r.sb(f"y{i}", [P, SB, D]) for i in range(2)]
        tp = [r.ps(f"tp{i}", [P, KD, TS]) for i in range(2)]
        hp = [r.ps(f"hp{i}", [P, 2, TS]) for i in range(4)]
        yp = [r.ps(f"yp{i}", [P, SB, D]) for i in range(2)]
        w1_in, w2_in = [r.sig(f"w1_in{i}", 32) for i in range(2)], [r.sig(f"w2_in{i}", 16) for i in range(2)]
        b2_in = [r.sig(f"b2_in{i}", 16) for i in range(2)]
        x_in = [r.sig(f"x_in{i}", 16 * SB) for i in range(2)]
        w1_hi, w1_lo, w2_hi, w2_lo = r.sig("w1_hi"), r.sig("w1_lo"), r.sig("w2_hi"), r.sig("w2_lo")
        turned, x_hi, x_lo = r.sig("turned"), r.sig("x_hi"), r.sig("x_lo")
        h_mm, h_ok, h_hi, h_lo = (r.sig(n, MH // 2) for n in ("h_mm", "h_ok", "h_hi", "h_lo"))
        y_mm, y_ok = r.sig("y_mm"), [r.sig(f"y_ok{i}") for i in range(2)]
        y_out = [r.sig(f"y_out{i}", 16) for i in range(2)]
        block = ctx.enter_context(nc.Block())
        W1, W2, B1, B2 = (io[f"{n}_{ly}"] for n in ("w1", "w2", "b1", "b2"))
        ybuf = io[f"ybuf{ly}"].rearrange("(t s p) d -> t p s d", s=SB, p=P)

        def one(ap, t):
            return ap[t] if isinstance(t, int) else ap[bass.ds(t, 1)].rearrange("o p s d -> (o p) s d")

        def tiles(eng, body):
            for t in range(3):
                body(t, t % 2, t // 2)
            with eng.Fori(1, (NTILES - 2) // 2) as i:
                body(i * 2 + 1, 1, i)
                body(i * 2 + 2, 0, i + 1)
            for t in range(1 + 2 * ((NTILES - 2) // 2), NTILES):
                body(t, t % 2, t // 2)

        def first(t):
            return isinstance(t, int) and t == 0

        def old(t):
            return not isinstance(t, int) or t >= 2

        def final(t):
            return isinstance(t, int) and t == NTILES - 1

        @block.sync
        def _(sp):
            def body(t, par, rd):
                idx = keep["owner"][0:1, t:t + 1] if isinstance(t, int) else keep["owner"][0:1, bass.ds(t, 1)]
                e = sp.value_load(idx, min_val=0, max_val=E - 1)
                if old(t):
                    sp.wait_ge(w1_lo.sem, w1_lo.at(t - 2))
                sp.dma_start(w1[par][:, :, :], W1[bass.ds(e, 1)].rearrange("o (k p) h -> (o p) k h", p=P)).then_inc(w1_in[par].sem, 16)
                if old(t):
                    sp.wait_ge(h_ok.sem, h_ok.at(t - 2))
                sp.dma_start(b1[par][:, :], B1[bass.ds(e, 1)].rearrange("o p m -> (o p) m")).then_inc(w1_in[par].sem, 16)
                if old(t):
                    sp.wait_ge(w2_lo.sem, w2_lo.at(t - 2))
                sp.dma_start(w2[par][:, :, :], W2[bass.ds(e, 1)].rearrange("o (m p) d -> (o p) m d", p=P)).then_inc(w2_in[par].sem, 16)
                if not first(t):
                    load_b2(t - 1, 1 - par, rd - 1 + par)

            def load_b2(t, par, rd):
                idx = keep["owner"][0:1, t:t + 1] if isinstance(t, int) else keep["owner"][0:1, bass.ds(t, 1)]
                e = sp.value_load(idx, min_val=0, max_val=E - 1)
                if old(t):
                    sp.wait_ge(y_ok[par].sem, rd)
                sp.dma_start(b2[par][:, :], B2[bass.ds(e, 1), :].to_broadcast([P, D])).then_inc(b2_in[par].sem, 16)

            tiles(sp, body)
            load_b2(NTILES - 1, (NTILES - 1) % 2, (NTILES - 1) // 2)

        @block.gpsimd
        def _(pool):
            def rows(t):
                if old(t):
                    pool.wait_ge(turned.sem, turned.at(t - 2))
                for s in range(SB):
                    c = t * SB + s
                    pool.indirect_dma_start(xin[t % 2][:, s, :], None, io[f"h{ly}"],
                                            bass.IndirectOffsetOnAxis(ap=keep["source"][:, c:c + 1], axis=0)).then_inc(x_in[t % 2].sem, 16)

            for t in range(NTILES):
                rows(t)

        @block.scalar
        def _(act):
            def hi_w1(t, par, rd):
                if old(t):
                    act.wait_ge(h_mm.sem, h_mm.at(t - 2))
                act.wait_ge(w1_in[par].sem, w1_in[par].at(rd))
                nc.scalar.activation(w1s[par][:, HI], w1[par][:, :, :], ACT.Copy).then_inc(w1_hi.sem, 1)

            def hi_w2(t, par, rd):
                act.wait_ge(w2_in[par].sem, w2_in[par].at(rd))
                nc.scalar.activation(w2s[par][:, HI], w2[par][:, :, :], ACT.Copy).then_inc(w2_hi.sem, 1)

            def hi_x(t, par):
                if old(t):
                    act.wait_ge(h_mm.sem, h_mm.at(t - 2))
                act.wait_ge(turned.sem, turned.at(t))
                nc.scalar.activation(xTs[par][:, HI], tp[par][:, :, :], ACT.Copy).then_inc(x_hi.sem, 1)

            def store(t, par, rd):
                act.wait_ge(y_ok[par].sem, y_ok[par].at(rd))
                act.dma_start(one(ybuf, t), y[par][:, :, :]).then_inc(y_out[par].sem, 16)

            def body(t, par, rd):
                if first(t):
                    hi_w1(0, 0, 0)
                    hi_x(0, 0)
                if old(t):
                    act.wait_ge(h_lo.sem, h_lo.at(t - 2))
                for i in range(MH // 2):
                    act.wait_ge(h_mm.sem, h_mm.at(t, i + 1))
                    for m in range(2):
                        ins = nc.scalar.activation(hid[par][:, 2 * i + m, :], hp[i][:, m, :], ACT.Gelu,
                                                   bias=b1[par][:, 2 * i + m:2 * i + m + 1])
                    ins.then_inc(h_ok.sem, 1)
                    if i == 0 and old(t):
                        act.wait_ge(y_mm.sem, y_mm.at(t - 2))
                    act.wait_ge(h_ok.sem, h_ok.at(t, i + 1))
                    nc.scalar.activation(hids[par][:, HI, 2 * i:2 * i + 2, :], hid[par][:, 2 * i:2 * i + 2, :], ACT.Copy).then_inc(h_hi.sem, 1)
                    if i == 0 and not final(t):
                        hi_w1(t + 1, 1 - par, rd + par)
                if not final(t):
                    hi_x(t + 1, 1 - par)
                if old(t):
                    store(t - 2, par, rd - 1)
                hi_w2(t, par, rd)

            tiles(act, body)
            for t in (NTILES - 2, NTILES - 1):
                store(t, t % 2, t // 2)
            act.wait_ge(y_out[0].sem, 16 * ((NTILES + 1) // 2))
            act.wait_ge(y_out[1].sem, 16 * (NTILES // 2))

        @block.vector
        def _(dve):
            V = nc.vector

            def lo_w1(t, par):
                dve.wait_ge(w1_hi.sem, w1_hi.at(t))
                V.tensor_tensor(w1s[par][:, LO], w1[par][:, :, :], w1s[par][:, HI].bitcast(F32), ALU.subtract).then_inc(w1_lo.sem, 1)

            def lo_w2(t, par):
                dve.wait_ge(w2_hi.sem, w2_hi.at(t))
                V.tensor_tensor(w2s[par][:, LO], w2[par][:, :, :], w2s[par][:, HI].bitcast(F32), ALU.subtract).then_inc(w2_lo.sem, 1)

            def lo_x(t, par):
                dve.wait_ge(x_hi.sem, x_hi.at(t))
                V.tensor_tensor(xTs[par][:, LO], tp[par][:, :, :], xTs[par][:, HI].bitcast(F32), ALU.subtract).then_inc(x_lo.sem, 1)

            def out(t, par, rd):
                dve.wait_ge(b2_in[par].sem, b2_in[par].at(rd))
                if old(t):
                    dve.wait_ge(y_out[par].sem, y_out[par].per * rd)
                dve.wait_ge(y_mm.sem, y_mm.at(t))
                V.tensor_tensor(y[par][:, :, :], yp[par][:, :, :], b2[par][:, :].unsqueeze(1).to_broadcast([P, SB, D]),
                                ALU.add).then_inc(y_ok[par].sem, 1)

            def body(t, par, rd):
                if first(t):
                    lo_w1(0, 0)
                    lo_x(0, 0)
                for i in range(MH // 2):
                    dve.wait_ge(h_hi.sem, h_hi.at(t, i + 1))
                    V.tensor_tensor(hids[par][:, LO, 2 * i:2 * i + 2, :], hid[par][:, 2 * i:2 * i + 2, :],
                                    hids[par][:, HI, 2 * i:2 * i + 2, :].bitcast(F32), ALU.subtract).then_inc(h_lo.sem, 1)
                    if i == 0 and not final(t):
                        lo_w1(t + 1, 1 - par)
                if not final(t):
                    lo_x(t + 1, 1 - par)
                lo_w2(t, par)
                if not first(t):
                    out(t - 1, 1 - par, rd - 1 + par)

            tiles(dve, body)
            out(NTILES - 1, (NTILES - 1) % 2, (NTILES - 1) // 2)

        @block.tensor
        def _(pe):
            def product(out, terms):
                n = 0
                for a, b in terms:
                    for i, j in ((HI, HI), (HI, LO), (LO, HI)):
                        mm = nc.tensor.matmul(out, a(i), b(j), start=(n == 0), stop=(n == 3 * len(terms) - 1))
                        n += 1
                return mm

            def turn(t, par, rd):
                pe.wait_ge(x_in[par].sem, x_in[par].at(rd))
                if old(t):
                    pe.wait_ge(x_lo.sem, x_lo.at(t - 2))
                for s in range(SB):
                    for k in range(KD):
                        mm = nc.tensor.transpose(tp[par][:, k, s * P:(s + 1) * P], xin[par][:, s, k * P:(k + 1) * P], ident[:, :])
                mm.then_inc(turned.sem, 1)

            def up(t, par, rd):
                pe.wait_ge(w1_lo.sem, w1_lo.at(t))
                pe.wait_ge(x_lo.sem, x_lo.at(t))
                for i in range(MH // 2):
                    if not first(t):
                        pe.wait_ge(h_ok.sem, h_ok.at(t - 1, i + 1))
                    for m in (2 * i, 2 * i + 1):
                        mm = product(hp[i][:, m % 2, :], [(lambda s, k=k: w1s[par][:, s, k, m * P:(m + 1) * P],
                                                           lambda s, k=k: xTs[par][:, s, k, :]) for k in range(KD)])
                    mm.then_inc(h_mm.sem, 1)

            def down(t, par, rd):
                pe.wait_ge(w2_lo.sem, w2_lo.at(t))
                if old(t):
                    pe.wait_ge(y_ok[par].sem, rd)
                pe.wait_ge(h_lo.sem, h_lo.at(t))
                for s in range(SB):
                    mm = product(yp[par][:, s, :], [(lambda i, m=m: hids[par][:, i, m, s * P:(s + 1) * P],
                                                     lambda i, m=m: w2s[par][:, i, m, :]) for m in range(MH)])
                mm.then_inc(y_mm.sem, 1)

            def body(t, par, rd):
                if first(t):
                    turn(0, 0, 0)
                up(t, par, rd)
                if not final(t):
                    turn(t + 1, 1 - par, rd + par)
                if not first(t):
                    down(t - 1, 1 - par, rd - 1 + par)

            tiles(pe, body)
            down(NTILES - 1, (NTILES - 1) % 2, (NTILES - 1) // 2)


def gather(nc, io, keep, ly, pool, dst, got, free, order):
    for n, j in enumerate(order):
        for k in range(K):
            buf = n % len(dst[k])
            if n >= len(dst[k]):
                pool.wait_ge(free.sem, n - len(dst[k]) + 1)
            c = k * NT + j
            pool.indirect_dma_start(dst[k][buf][:, :], None, io[f"ybuf{ly}"],
                                    bass.IndirectOffsetOnAxis(ap=keep["get"][:, c:c + 1], axis=0)).then_inc(got[buf].sem, 16)


def mixer(nc, io, keep):
    with ExitStack() as ctx:
        r = Room(nc, ctx, "mix", keep)
        ident = keep["ident"]
        NST = SQ // P
        W3 = 3 * D
        w_qkv = r.sb("w_qkv", [P, KD, W3])
        w_o = r.sb("w_o", [P, KD, D])
        w_gate = r.sb("w_gate", [P, KD, E])
        b_qkv = r.sb("b_qkv", [P, W3])
        b_o = r.sb("b_o", [P, D])
        gb0 = r.sb("gb0", [P, TQ, D])
        rep = r.sb("rep", [P, TQ, 3, D])
        eps = r.sb("eps", [P, 1])
        yk = [[r.sb(f"y{k}_{i}", [P, D]) for i in range(4)] for k in range(K)]
        xa = r.sb("xa", [P, TQ, D])
        xi = r.sb("xi", [P, TQ, D])
        st = {part: r.sb(f"st_{part}", [P, TQ, 6]) for part in ("entry", "out")}
        mom = {part: r.sb(f"mom_{part}", [P, 3, TQ]) for part in ("entry", "out")}
        rstd = {part: r.sb(f"rstd_{part}", [P, TQ]) for part in ("entry", "out")}
        shift = {part: r.sb(f"shift_{part}", [P, TQ]) for part in ("entry", "out")}
        xn = r.sb("xn", [P, TQ, D])
        hT = r.sb("hT", [P, KD, TQ, P])
        qk = r.sb("qk", [P, TQ, 2 * D])
        v_next = r.sb("v_next", [P, TQ, D])
        v = r.sb("v", [P, TQ, D])
        squares = r.sb("squares", [P, TQ, 2 * D])
        mean = r.sb("mean", [P, 2, D])
        rs = r.sb("rs", [P, 2, D])
        corr = r.sb("corr", [P, HEADS, HD, HD])
        rz = r.sb("rz", [P, HEADS, HD])
        prod = [r.sb(f"prod{i}", [P, TQ * D]) for i in range(4)]
        att = r.sb("att", [P, TQ, D])
        bank = r.ps("bank", [P, 8, 512])
        NPC, NPA = 2 * TQ, HD
        NPR = NPC + NPA
        gb0_in, qkv_in, out_in, ready = r.sig("gb0_in", 16 * B), r.sig("qkv_in", 32), r.sig("out_in", 16 * (3 + B)), r.sig("ready")
        xa_in, x2_out, xi_in, x3_out, h_out = (r.sig(n, 16) for n in ("xa_in", "x2_out", "xi_in", "x3_out", "h_out"))
        got, used = [r.sig(f"got{i}", 16 * K) for i in range(4)], r.sig("used", TQ)
        yw, ysum, x2_ok = r.sig("yw", TQ), r.sig("ysum"), r.sig("x2_ok")
        stats = {part: r.sig(f"stats_{part}", TQ) for part in ("entry", "out")}
        means = {part: r.sig(f"means_{part}", 6) for part in ("entry", "out")}
        rstds = {part: r.sig(f"rstds_{part}", 2) for part in ("entry", "out")}
        shifts = {part: r.sig(f"shifts_{part}") for part in ("entry", "out")}
        norms = {part: r.sig(f"norms_{part}", TQ) for part in ("entry", "out")}
        turned = {src: r.sig(f"turned_{src}", 4) for src in ("entry", "att", "out")}
        hT_ok = {src: r.sig(f"hT_{src}") for src in ("entry", "att", "out")}
        qkv_mm, qkv_ok = r.sig("qkv_mm", TQ), r.sig("qkv_ok", TQ)
        msum, centred, sq, sqs, unit, unit_ok, v_ok = r.sig("msum"), r.sig("centred"), r.sig("sq"), r.sig("sqs"), r.sig("unit", 2), r.sig("unit_ok"), r.sig("v_ok")
        prod_ok, acc_ok = r.sig("prod_ok", NPR), r.sig("acc_ok", NPR)
        clip_ok, exp_ok, zs_ok, rz_ok, att_ok = r.sig("clip_ok", 2), r.sig("exp_ok", 2), r.sig("zs_ok"), r.sig("rz_ok"), r.sig("att_ok")
        o_mm, o_b, o_g, x3_ok, sc_ok, h_ok, lg_mm, lg_ok = (r.sig(n) for n in ("o_mm", "o_b", "o_g", "x3_ok", "sc_ok", "h_ok", "lg_mm", "lg_ok"))
        block = ctx.enter_context(nc.Block())

        def seqs(name, s):
            ap = io[name].rearrange("(t s p) d -> s p t d", t=TQ, p=P)
            return ap[s] if isinstance(s, int) else ap[bass.ds(s, 1)].rearrange("o p t d -> (o p) t d")

        def rounds(eng, body):
            body(None, 0, None)
            body(0, 1, None)
            with eng.Fori(1, NST - 1) as s:
                body(s, s + 1, s - 1)
            body(NST - 1, None, NST - 2)
            body(None, None, NST - 1)

        def later(s):
            return not isinstance(s, int) or s > 0

        @block.sync
        def _(sp):
            mod = io["modrow"][1]
            for b in range(B):
                sp.dma_start(gb0[:, b, :], io["modrow"][0][b:b + 1, 3 * D:].to_broadcast([P, D])).then_inc(gb0_in.sem, 16)

            def body(s, nxt, prv):
                if nxt is not None:
                    if later(nxt):
                        sp.wait_ge(x2_out.sem, x2_out.at(nxt - 1))
                        sp.wait_ge(norms["entry"].sem, norms["entry"].at(nxt - 1))
                    sp.dma_start(xa[:, :, :], seqs("x1", nxt)).then_inc(xa_in.sem, 16)
                if s is None and prv is None:
                    for dst, src in ((w_qkv[:, :, :], io["WqkvT"]), (b_qkv[:, :], io["bqkv"].to_broadcast([P, W3]))):
                        sp.dma_start(dst, src).then_inc(qkv_in.sem, 16)
                if prv is not None:
                    sp.wait_ge(x3_ok.sem, x3_ok.at(prv))
                    sp.dma_start(seqs("x3", prv), xi[:, :, :]).then_inc(x3_out.sem, 16)
                    sp.wait_ge(h_ok.sem, h_ok.at(prv))
                    sp.dma_start(seqs("h1", prv), att[:, :, :]).then_inc(h_out.sem, 16)
                if s is not None:
                    if later(s):
                        sp.wait_ge(x3_out.sem, x3_out.at(s - 1))
                        sp.wait_ge(norms["out"].sem, norms["out"].at(s - 1))
                    sp.wait_ge(x2_out.sem, x2_out.at(s))
                    sp.dma_start(xi[:, :, :], seqs("x2", s)).then_inc(xi_in.sem, 16)
                if nxt is not None:
                    sp.wait_ge(x2_ok.sem, x2_ok.at(nxt))
                    sp.dma_start(seqs("x2", nxt), xa[:, :, :]).then_inc(x2_out.sem, 16)
                if s is None and prv is None:
                    for dst, src in ((w_o[:, :, :], io["WoutT"]), (w_gate[:, :, :], io["gate1"]), (b_o[:, :], io["bout"].to_broadcast([P, D]))):
                        sp.dma_start(dst, src).then_inc(out_in.sem, 16)
                    for b in range(B):
                        sp.dma_start(rep[:, b, :, :].rearrange("p m d -> p (m d)"), mod[b:b + 1, 0:3 * D].to_broadcast([P, 3 * D])).then_inc(out_in.sem, 16)

            rounds(sp, body)
            sp.wait_ge(x3_out.sem, 16 * NST)
            sp.wait_ge(h_out.sem, 16 * NST)

        @block.gpsimd
        def _(pool):
            gather(nc, io, keep, 0, pool, yk, got, used, [t * NST + s for s in range(NST) for t in range(TQ)])

        @block.scalar
        def _(act):
            act.wait_ge(ready.sem, 1)

            def root(s, part):
                act.wait_ge(means[part].sem, means[part].at(s))
                nc.scalar.activation(rstd[part][:, :], mom[part][:, 2, :], ACT.Ln, bias=eps[:, 0:1], scale=1.0 / D).then_inc(rstds[part].sem, 1)
                act.wait_ge(rstds[part].sem, rstds[part].at(s, 1))
                nc.scalar.activation(rstd[part][:, :], rstd[part][:, :], ACT.Exp, scale=-0.5).then_inc(rstds[part].sem, 1)

            def normed(s, part, x, out):
                act.wait_ge(shifts[part].sem, shifts[part].at(s))
                for t in range(TQ):
                    nc.scalar.activation(out[:, t, :], x[:, t, :], ACT.Identity, bias=shift[part][:, t:t + 1],
                                         scale=rstd[part][:, t:t + 1]).then_inc(norms[part].sem, 1)

            def weigh(s, steps):
                if steps[0] == 0 and later(s):
                    act.wait_ge(turned["entry"].sem, turned["entry"].at(s - 1))
                for t in steps:
                    act.wait_ge(got[t % 4].sem, got[t % 4].per * (s * 2 + t // 4 + 1))
                    c = s + t * NST
                    wt = keep["wts"][:, c:c + 1] if isinstance(c, int) else keep["wts"][:, bass.ds(c, 1)]
                    nc.scalar.activation(xn[:, t, :], yk[0][t % 4][:, :], ACT.Copy, scale=wt).then_inc(yw.sem, 1)

            def copy_hT(s, src):
                b0 = 4 if src == "entry" else 0
                for g in range(4):
                    act.wait_ge(turned[src].sem, turned[src].at(s, g + 1))
                    if src == "entry":
                        for dh in range(KD):
                            for t in (2 * g, 2 * g + 1):
                                ins = nc.scalar.activation(hT[:, dh, t, :], bank[:, b0 + g, (2 * dh + t % 2) * P:(2 * dh + t % 2 + 1) * P],
                                                           ACT.Identity, scale=keep["modT"][:, 1, KD + dh, t:t + 1],
                                                           bias=keep["modT"][:, 1, dh, t:t + 1])
                    else:
                        ins = nc.scalar.activation(hT[:, :, 2 * g:2 * g + 2, :], bank[:, b0 + g, :].rearrange("p (d t c) -> p d t c", d=KD, t=2), ACT.Copy)
                ins.then_inc(hT_ok[src].sem, 1)

            def exp(s, hf):
                act.wait_ge(clip_ok.sem, clip_ok.at(s, hf + 1))
                c = corr[:, 8 * hf:8 * hf + 8, :, :].rearrange("p h i j -> p (h i j)")
                nc.scalar.activation(c, c, ACT.Exp).then_inc(exp_ok.sem, 1)

            def body(s, nxt, prv):
                if nxt is not None:
                    weigh(nxt, range(0, TQ // 2))
                if prv is not None:
                    root(prv, "out")
                    normed(prv, "out", xi, att)
                if nxt is not None:
                    weigh(nxt, range(TQ // 2, TQ))
                if s is not None:
                    exp(s, 0)
                if prv is not None:
                    copy_hT(prv, "out")
                if nxt is not None:
                    root(nxt, "entry")
                if s is not None:
                    exp(s, 1)
                if nxt is not None:
                    normed(nxt, "entry", xa, xn)
                    copy_hT(nxt, "entry")
                    act.wait_ge(centred.sem, centred.at(nxt))
                    nc.scalar.activation(squares[:, :, :], qk[:, :, :], ACT.Square).then_inc(sq.sem, 1)
                    act.wait_ge(sqs.sem, sqs.at(nxt))
                    nc.scalar.activation(rs[:, :, :], rs[:, :, :], ACT.Ln).then_inc(unit.sem, 1)
                    act.wait_ge(unit.sem, unit.at(nxt, 1))
                    nc.scalar.activation(rs[:, :, :], rs[:, :, :], ACT.Exp, scale=-0.5).then_inc(unit.sem, 1)
                    if s is not None:
                        act.wait_ge(prod_ok.sem, prod_ok.at(s))
                    act.wait_ge(qkv_ok.sem, qkv_ok.at(nxt))
                    nc.scalar.activation(v[:, :, :], v_next[:, :, :], ACT.Copy).then_inc(v_ok.sem, 1)
                if s is not None:
                    copy_hT(s, "att")

            rounds(act, body)

        @block.vector
        def _(dve):
            V = nc.vector
            V.memset(eps[:, :], EPS).then_inc(ready.sem, 1)

            def column(c):
                return keep["wts"][:, c:c + 1] if isinstance(c, int) else keep["wts"][:, bass.ds(c, 1)]

            def variance(s, part, x):
                for t in range(TQ):
                    V.bn_stats(st[part][:, t, :], x[:, t, :]).then_inc(stats[part].sem, 1)
                dve.wait_ge(stats[part].sem, stats[part].at(s))
                moments(nc, dve, means[part].at(s, 0), mom[part], st[part], TQ, means[part])

            def offsets(s, part):
                dve.wait_ge(rstds[part].sem, rstds[part].at(s))
                V.scalar_tensor_tensor(shift[part][:, :], mom[part][:, 0, :], -1.0, rstd[part][:, :], ALU.mult, ALU.mult).then_inc(shifts[part].sem, 1)

            def combine(s, t):
                dve.wait_ge(yw.sem, yw.at(s, t + 1))
                V.scalar_tensor_tensor(xn[:, t, :], yk[1][t % 4][:, :], column(s + (NT + t * NST)), xn[:, t, :], ALU.mult, ALU.add).then_inc(used.sem, 1)

            def gate_rows(s):
                if not later(s):
                    dve.wait_ge(gb0_in.sem, gb0_in.at(0))
                dve.wait_ge(used.sem, used.at(s))
                V.tensor_tensor(xn[:, :, :], xn[:, :, :], gb0[:, :, :], ALU.mult).then_inc(ysum.sem, 1)

            def add_rows(s):
                dve.wait_ge(ysum.sem, ysum.at(s))
                dve.wait_ge(xa_in.sem, xa_in.at(s))
                V.tensor_tensor(xa[:, :, :], xa[:, :, :], xn[:, :, :], ALU.add).then_inc(x2_ok.sem, 1)

            def entry_variance(s):
                dve.wait_ge(x2_ok.sem, x2_ok.at(s))
                variance(s, "entry", xa)

            def qkv_rows(s, t):
                dve.wait_ge(qkv_mm.sem, qkv_mm.at(s, t + 1))
                both = bank[:, 4 + 2 * (t % 2):6 + 2 * (t % 2), :].rearrange("p b c -> p (b c)")
                if t == 0 and not later(s):
                    dve.wait_ge(qkv_in.sem, qkv_in.at(0))
                if t == 0 and later(s):
                    dve.wait_ge(v_ok.sem, v_ok.at(s - 1))
                V.tensor_tensor(qk[:, t, :], both[:, 0:2 * D], b_qkv[:, 0:2 * D], ALU.add)
                V.tensor_tensor(v_next[:, t, :], both[:, 2 * D:W3], b_qkv[:, 2 * D:], ALU.add).then_inc(qkv_ok.sem, 1)

            def centre(s):
                dve.wait_ge(qkv_ok.sem, qkv_ok.at(s))
                flat = mean[:, :, :].rearrange("p a d -> p (a d)")
                V.tensor_reduce(flat, qk[:, :, :].rearrange("p t c -> p c t"), AX.X, ALU.add).then_inc(msum.sem, 1)
                dve.wait_ge(msum.sem, msum.at(s))
                V.scalar_tensor_tensor(qk[:, :, :], flat.unsqueeze(1).to_broadcast([P, TQ, 2 * D]), -1.0 / TQ, qk[:, :, :],
                                       ALU.mult, ALU.add).then_inc(centred.sem, 1)

            def lengths(s):
                dve.wait_ge(sq.sem, sq.at(s))
                V.tensor_reduce(rs[:, :, :].rearrange("p a d -> p (a d)"), squares[:, :, :].rearrange("p t c -> p c t"), AX.X, ALU.add).then_inc(sqs.sem, 1)

            def scale_qk(s):
                dve.wait_ge(unit.sem, unit.at(s))
                V.tensor_tensor(qk[:, :, :], qk[:, :, :], rs[:, :, :].rearrange("p a d -> p (a d)").unsqueeze(1).to_broadcast([P, TQ, 2 * D]),
                                ALU.mult).then_inc(unit_ok.sem, 1)

            def pair(s, n):
                if n == 0:
                    dve.wait_ge(unit_ok.sem, unit_ok.at(s))
                if n == NPC:
                    dve.wait_ge(exp_ok.sem, exp_ok.at(s))
                    dve.wait_ge(v_ok.sem, v_ok.at(s))
                if n >= 4:
                    dve.wait_ge(acc_ok.sem, acc_ok.at(s, n - 3))
                if n < NPC:
                    hf, t = n // TQ, n % TQ
                    q_ = qk[:, t, 128 * hf:128 * hf + 128].rearrange("p (h i) -> p h i", i=HD).unsqueeze(3).to_broadcast([P, 8, HD, HD])
                    k_ = qk[:, t, D + 128 * hf:D + 128 * hf + 128].rearrange("p (h j) -> p h j", j=HD).unsqueeze(2).to_broadcast([P, 8, HD, HD])
                    V.tensor_tensor(prod[n % 4][:, :].rearrange("p (h i j) -> p h i j", h=8, i=HD), q_, k_, ALU.mult).then_inc(prod_ok.sem, 1)
                else:
                    d = n - NPC
                    v_ = v[:, :, :].rearrange("p t (h d) -> p t h d", d=HD)[:, :, :, d:d + 1].to_broadcast([P, TQ, HEADS, HD])
                    c_ = corr[:, :, d, :].unsqueeze(1).to_broadcast([P, TQ, HEADS, HD])
                    V.tensor_tensor(prod[n % 4][:, :].rearrange("p (t h e) -> p t h e", t=TQ, h=HEADS), v_, c_, ALU.mult).then_inc(prod_ok.sem, 1)

            def clip(s, hf):
                dve.wait_ge(acc_ok.sem, acc_ok.at(s, TQ * (hf + 1)))
                V.tensor_scalar(corr[:, 8 * hf:8 * hf + 8, :, :].rearrange("p h i j -> p (h i j)"),
                                bank[:, 4 * hf:4 * hf + 4, :].rearrange("p b c -> p (b c)"), 0.0, 1.0, ALU.max, ALU.min).then_inc(clip_ok.sem, 1)

            def softmax_sums(s):
                V.tensor_reduce(rz[:, :, :], corr[:, :, :, :].rearrange("p h i j -> p h j i"), AX.X, ALU.add).then_inc(zs_ok.sem, 1)

            def softmax_inverse(s):
                dve.wait_ge(zs_ok.sem, zs_ok.at(s))
                V.reciprocal(rz[:, :, :], rz[:, :, :]).then_inc(rz_ok.sem, 1)

            def attention(s):
                dve.wait_ge(acc_ok.sem, acc_ok.at(s))
                dve.wait_ge(rz_ok.sem, rz_ok.at(s))
                if later(s):
                    dve.wait_ge(h_out.sem, h_out.at(s - 1))
                V.tensor_tensor(att[:, :, :], bank[:, 0:4, :].rearrange("p b (t c) -> p (b t) c", t=2),
                                rz[:, :, :].rearrange("p h e -> p (h e)").unsqueeze(1).to_broadcast([P, TQ, D]), ALU.mult).then_inc(att_ok.sem, 1)

            def out_bias(s):
                if not later(s):
                    dve.wait_ge(out_in.sem, out_in.at(0))
                dve.wait_ge(o_mm.sem, o_mm.at(s))
                V.tensor_tensor(att[:, :, :], bank[:, 4:8, :].rearrange("p b (t c) -> p (b t) c", t=2),
                                b_o[:, :].unsqueeze(1).to_broadcast([P, TQ, D]), ALU.add).then_inc(o_b.sem, 1)

            def out_gate(s):
                dve.wait_ge(o_b.sem, o_b.at(s))
                V.tensor_tensor(att[:, :, :], att[:, :, :], rep[:, :, 0, :], ALU.mult).then_inc(o_g.sem, 1)

            def out_add(s):
                dve.wait_ge(o_g.sem, o_g.at(s))
                dve.wait_ge(xi_in.sem, xi_in.at(s))
                V.tensor_tensor(xi[:, :, :], xi[:, :, :], att[:, :, :], ALU.add).then_inc(x3_ok.sem, 1)

            def out_variance(s):
                dve.wait_ge(x3_ok.sem, x3_ok.at(s))
                variance(s, "out", xi)

            def out_scale(s):
                dve.wait_ge(norms["out"].sem, norms["out"].at(s))
                V.tensor_tensor(att[:, :, :], att[:, :, :], rep[:, :, 2, :], ALU.mult).then_inc(sc_ok.sem, 1)

            def out_shift(s):
                dve.wait_ge(sc_ok.sem, sc_ok.at(s))
                V.tensor_tensor(att[:, :, :], att[:, :, :], rep[:, :, 1, :], ALU.add).then_inc(h_ok.sem, 1)

            def logits(s):
                dve.wait_ge(lg_mm.sem, lg_mm.at(s))
                dst = keep["logits"][:, :, :].rearrange("p (t s) e -> p s t e", s=NST)
                dst = dst[:, s] if isinstance(s, int) else dst[:, bass.ds(s, 1)].rearrange("p o t e -> p (o t) e")
                V.tensor_scalar(dst, bank[:, 0, 0:TQ * E].rearrange("p (t e) -> p t e", t=TQ), 1.0, None, ALU.mult).then_inc(lg_ok.sem, 1)

            def body(s, nxt, prv):
                outs = [(3, out_bias), (4, out_gate), (5, out_add), (6, out_variance), (7, lambda b: offsets(b, "out")),
                        (10, out_scale), (11, out_shift), (15, logits)]
                entry = [(1 + t if t < TQ // 2 else 4 + t, lambda b, t=t: combine(b, t)) for t in range(TQ)]
                entry += [(12, gate_rows), (13, add_rows), (14, entry_variance), (15, lambda b: offsets(b, "entry"))]
                entry += [(21 + t // 2, lambda b, t=t: qkv_rows(b, t)) for t in range(TQ)] + [(26, centre), (29, lengths), (31, scale_qk)]
                own = [(12, lambda b: clip(b, 0)), (15, lambda b: clip(b, 1)), (17, softmax_sums), (18, softmax_inverse), (NPR + 1, attention)]
                for n in range(NPR + 4):
                    if s is not None and n < NPR:
                        pair(s, n)
                    for tile, steps in ((s, own), (prv, outs), (nxt, entry)):
                        for place, step in steps:
                            if place == n and tile is not None:
                                step(tile)

            rounds(dve, body)

        @block.tensor
        def _(pe):
            def turn(src, rows, b0):
                for g in range(4):
                    for dh in range(KD):
                        for t in (2 * g, 2 * g + 1):
                            mm = nc.tensor.transpose(bank[:, b0 + g, (2 * dh + t % 2) * P:(2 * dh + t % 2 + 1) * P], rows[:, t, dh * P:(dh + 1) * P], ident[:, :])
                    mm.then_inc(turned[src].sem, 1)

            def turn_entry(s, now):
                pe.wait_ge(norms["entry"].sem, norms["entry"].at(s))
                if now is not None:
                    pe.wait_ge(clip_ok.sem, clip_ok.at(now))
                turn("entry", xn, 4)

            def qkv(s, t):
                if t == 0:
                    if not later(s):
                        pe.wait_ge(qkv_in.sem, qkv_in.at(0))
                    pe.wait_ge(hT_ok["entry"].sem, hT_ok["entry"].at(s))
                else:
                    if t >= 2:
                        pe.wait_ge(qkv_ok.sem, qkv_ok.at(s, t - 1))
                for c0, c1, bk in ((0, 512, 4 + 2 * (t % 2)), (512, W3, 5 + 2 * (t % 2))):
                    for k in range(KD):
                        mm = nc.tensor.matmul(bank[:, bk, 0:c1 - c0], hT[:, k, t, :], w_qkv[:, k, c0:c1], start=(k == 0), stop=(k == KD - 1))
                mm.then_inc(qkv_mm.sem, 1)

            def add(s, n):
                if n == 0 and later(s):
                    pe.wait_ge(hT_ok["att"].sem, hT_ok["att"].at(s - 1))
                if n == TQ:
                    pe.wait_ge(qkv_ok.sem, qkv_ok.at(s))
                    if later(s):
                        pe.wait_ge(o_b.sem, o_b.at(s - 1))
                if n == NPC:
                    pe.wait_ge(clip_ok.sem, clip_ok.at(s, 1))
                    if later(s):
                        pe.wait_ge(lg_ok.sem, lg_ok.at(s - 1))
                pe.wait_ge(prod_ok.sem, prod_ok.at(s, n + 1))
                b0 = 4 if TQ <= n < NPC else 0
                a, z = (n % TQ == 0, n % TQ == TQ - 1) if n < NPC else (n == NPC, n == NPR - 1)
                for i in range(4):
                    mm = nc.tensor.matmul(bank[:, b0 + i, :], ident[:, :], prod[n % 4][:, 512 * i:512 * (i + 1)], start=a, stop=z)
                mm.then_inc(acc_ok.sem, 1)

            def turn_out(s, now):
                pe.wait_ge(h_ok.sem, h_ok.at(s))
                if now is not None:
                    pe.wait_ge(clip_ok.sem, clip_ok.at(now, 1))
                turn("out", att, 0)

            def logits(s):
                pe.wait_ge(hT_ok["out"].sem, hT_ok["out"].at(s))
                for t in range(TQ):
                    for k in range(KD):
                        mm = nc.tensor.matmul(bank[:, 0, t * E:(t + 1) * E], hT[:, k, t, :], w_gate[:, k, :], start=(k == 0), stop=(k == KD - 1))
                mm.then_inc(lg_mm.sem, 1)

            def output(s, nxt):
                if not later(s):
                    pe.wait_ge(out_in.sem, out_in.at(0))
                pe.wait_ge(att_ok.sem, att_ok.at(s))
                turn("att", att, 0)
                pe.wait_ge(hT_ok["att"].sem, hT_ok["att"].at(s))
                if nxt is not None:
                    pe.wait_ge(qkv_ok.sem, qkv_ok.at(nxt))
                else:
                    pe.wait_ge(clip_ok.sem, clip_ok.at(s))
                for t in range(TQ):
                    for k in range(KD):
                        mm = nc.tensor.matmul(bank[:, 4 + t // 2, (t % 2) * D:(t % 2 + 1) * D], hT[:, k, t, :], w_o[:, k, :], start=(k == 0), stop=(k == KD - 1))
                mm.then_inc(o_mm.sem, 1)

            def body(s, nxt, prv):
                for n in range(NPR):
                    if n == 13 and prv is not None:
                        turn_out(prv, s)
                    if n == 15 and prv is not None:
                        logits(prv)
                    if n == 18 and nxt is not None:
                        turn_entry(nxt, s)
                    if 19 <= n < 19 + TQ // 2 and nxt is not None:
                        qkv(nxt, 2 * (n - 19))
                        qkv(nxt, 2 * (n - 19) + 1)
                    if s is not None:
                        add(s, n)
                if s is not None:
                    output(s, nxt)

            rounds(pe, body)


def last(nc, io, keep):
    with ExitStack() as ctx:
        r = Room(nc, ctx, "last", keep)
        gb = [r.sb(f"gb{i}", [P, D]) for i in range(2)]
        yk = [[r.sb(f"y{k}_{i}", [P, D]) for i in range(8)] for k in range(K)]
        x = [r.sb(f"x{i}", [P, JT, D]) for i in range(2)]
        acc = [r.sb(f"acc{i}", [P, JT, D]) for i in range(2)]
        x_in, out = [r.sig(f"x_in{i}", 32) for i in range(2)], [r.sig(f"out{i}", 16) for i in range(2)]
        got, used = [r.sig(f"got{i}", 16 * K) for i in range(8)], r.sig("used", JT)
        yw, gated, sum_ok = r.sig("yw", JT), r.sig("gated"), r.sig("sum_ok")
        block = ctx.enter_context(nc.Block())

        def one(ap, b):
            return ap[b] if isinstance(b, int) else ap[bass.ds(b, 1)].rearrange("o p j d -> (o p) j d")

        def pairs(eng, body):
            body(0, False)
            with eng.Fori(1, B // 2) as i:
                body(i, True)

        @block.sync
        def _(sp):
            src = io["x3"].rearrange("(b j p) d -> b p j d", b=B, p=P)
            dst = io["out"].rearrange("b (j p) d -> b p j d", p=P)
            def body(i, later):
                for h in range(2):
                    if later:
                        sp.wait_ge(out[h].sem, i * 16)
                    sp.dma_start(x[h][:, :, :], one(src, i * 2 + h)).then_inc(x_in[h].sem, 16)
                    b = i * 2 + h
                    src_gb = io["modrow"][1][b:b + 1, 3 * D:] if isinstance(b, int) else io["modrow"][1][bass.ds(b, 1), 3 * D:]
                    sp.dma_start(gb[h][:, :], src_gb.to_broadcast([P, D])).then_inc(x_in[h].sem, 16)
                for h in range(2):
                    sp.wait_ge(sum_ok.sem, sum_ok.at(i * 2 + h))
                    sp.dma_start(one(dst, i * 2 + h), x[h][:, :, :]).then_inc(out[h].sem, 16)

            pairs(sp, body)
            for h in range(2):
                sp.wait_ge(out[h].sem, 16 * (B // 2))

        @block.gpsimd
        def _(pool):
            gather(nc, io, keep, 1, pool, yk, got, used, range(NT))

        @block.vector
        def _(dve):
            V = nc.vector
            def body(i, later):
                for h in range(2):
                    b = i * 2 + h
                    for j in range(JT):
                        n = h * JT + j
                        dve.wait_ge(got[n].sem, got[n].at(i))
                        cs = [b * JT + (k * NT + j) for k in range(K)]
                        wt = [keep["wts"][:, c:c + 1] if isinstance(c, int) else keep["wts"][:, bass.ds(c, 1)] for c in cs]
                        V.tensor_scalar(acc[h][:, j, :], yk[0][n][:, :], wt[0], None, ALU.mult).then_inc(yw.sem, 1)
                        dve.wait_ge(yw.sem, yw.at(b, j + 1))
                        V.scalar_tensor_tensor(acc[h][:, j, :], yk[1][n][:, :], wt[1], acc[h][:, j, :], ALU.mult, ALU.add).then_inc(used.sem, 1)
                    dve.wait_ge(used.sem, used.at(b))
                    dve.wait_ge(x_in[h].sem, x_in[h].at(i))
                    V.tensor_tensor(acc[h][:, :, :], acc[h][:, :, :], gb[h][:, :].unsqueeze(1).to_broadcast([P, JT, D]), ALU.mult).then_inc(gated.sem, 1)
                    dve.wait_ge(gated.sem, gated.at(b))
                    V.tensor_tensor(x[h][:, :, :], x[h][:, :, :], acc[h][:, :, :], ALU.add).then_inc(sum_ok.sem, 1)

            pairs(dve, body)


def program(nc, io, until=99):
    scratch = {"modrow": [2, B, 4 * D], "bc": [2, 2 * NS, L], "x1": [T, D], "x2": [T, D], "h0": [T, D], "x3": [T, D], "h1": [T, D],
               "ybuf0": [SLOTS, D], "ybuf1": [SLOTS, D]}
    for name, shape in scratch.items():
        io[name] = nc.dram_tensor(f"s_{name}", shape, F32, kind="Internal").ap()
    with ExitStack() as ctx:
        def sb(name, shape, dt=F32):
            return ctx.enter_context(nc.sbuf_tensor(f"keep_{name}", shape, dt))

        keep = {"ident": sb("ident", [P, P]), "below": sb("below", [P, P]), "ones": sb("ones", [P, P]), "iota": sb("iota", [P, 2 * P]),
                "modT": sb("modT", [P, 2, 2 * KD, B]), "logits": sb("logits", [P, NT, E]), "wts": sb("wts", [P, K * NT]),
                "source": sb("source", [P, SLOTS // P], I32), "get": sb("get", [P, K * NT], I32), "owner": sb("owner", [P, NTILES], I32), "taken": []}
        stages = [lambda: setup(nc, io, keep), lambda: mamba(nc, io, keep), lambda: route(nc, io, keep, 0),
                  lambda: experts(nc, io, keep, 0), lambda: mixer(nc, io, keep), lambda: route(nc, io, keep, 1),
                  lambda: experts(nc, io, keep, 1), lambda: last(nc, io, keep)]
        for stage in stages[:until]:
            stage()
            nc.clear_and_free_semaphores(keep["taken"])
            keep["taken"].clear()
            nc.all_engine_barrier()


def kernel(**a):
    import numpy as np
    from concourse import bacc
    from concourse.bass_utils import run_bass_kernel_spmd

    def cols(v):
        return np.ascontiguousarray(v.reshape(-1, P).T)

    def rows(w):
        return np.ascontiguousarray(w.reshape(-1, P, w.shape[1]).transpose(1, 0, 2))

    a = {n: np.asarray(v) for n, v in a.items()}
    iota = np.zeros((P, 2 * P), np.float32)
    iota[:, 0:E] = E - np.arange(E)
    iota[:, E:E + MAXT] = TS * np.arange(MAXT)
    iota[:, 24:24 + NTILES] = np.arange(NTILES)
    iota[:, 64:64 + K * NT] = P * (np.arange(K * NT)[None, :] % NT) + np.arange(P)[:, None]
    iota[:, P:] = np.arange(P)
    arrays = {
        "x": a["L0_attn_x"], "W_in": a["L0_attn_W_in"], "conv_k": a["L0_attn_conv_k"], "W_x": a["L0_attn_W_x"],
        "W_dt": a["L0_attn_W_dt"], "A_log": a["L0_attn_A_log"], "W_out": a["L0_attn_W_out"],
        "vecs": np.stack([cols(a["L0_attn_conv_b"]), cols(a["L0_attn_b_dt"]), cols(a["L0_attn_D"])], axis=1),
        "gate0": rows(a["L0_ffn_Wg"].T), "gate1": rows(a["L1_ffn_router_w"]),
        "WqkvT": rows(a["L1_attn_Wqkv"].T), "WoutT": rows(a["L1_attn_Wout"].T),
        "bqkv": a["L1_attn_bqkv"].reshape(1, -1), "bout": a["L1_attn_bout"].reshape(1, -1),
        "cT": np.stack([rows(a["L0_c"].T), rows(a["L1_c"].T)]), "wmod": np.stack([a["L0_wmod"], a["L1_wmod"]]),
        "w1_0": a["L0_ffn_W1"], "w2_0": a["L0_ffn_W2"], "b2_0": a["L0_ffn_b2"],
        "w1_1": a["L1_ffn_w1"], "w2_1": a["L1_ffn_w2"], "b2_1": a["L1_ffn_b2"],
        "b1_0": a["L0_ffn_b1"].reshape(E, MH, P).transpose(0, 2, 1), "b1_1": a["L1_ffn_b1"].reshape(E, MH, P).transpose(0, 2, 1),
        "ident": np.eye(P, dtype=np.float32), "below": np.triu(np.ones((P, P), np.float32), 1), "iota": iota,
    }
    arrays = {n: np.ascontiguousarray(v) for n, v in arrays.items()}
    nc = bacc.Bacc("TRN2", target_bir_lowering=False, num_devices=1)
    io = {n: nc.dram_tensor(f"in_{n}", v.shape, mybir.dt.from_np(v.dtype), kind="ExternalInput").ap() for n, v in arrays.items()}
    io["out"] = nc.dram_tensor("out", (B, L, D), F32, kind="ExternalOutput").ap()
    program(nc, io, kernel.until)
    r = run_bass_kernel_spmd(nc, [{f"in_{n}": v for n, v in arrays.items()}], core_ids=[0])
    return r.results[0]["out"]


kernel.until = 99
```
